# Optimizing a Trainium2 kernel written in Bass

```python
import numpy as np
import jax
import jax.numpy as jnp

def _softmax(x, axis=-1):
    return jax.nn.softmax(x, axis=axis)

def _gelu(x):
    return jax.nn.gelu(x, approximate=True)

def _silu(x):
    return jax.nn.silu(x)

def _sigmoid(x):
    return jax.nn.sigmoid(x)

def _layernorm(x, axis=-1, eps=1e-05):
    m = jnp.mean(x, axis=axis, keepdims=True)
    v = jnp.var(x, axis=axis, keepdims=True)
    return (x - m) / jnp.sqrt(v + eps)

def _scatter_add(tgt, idx, src, axis=0):
    return tgt.at[idx].add(src)

def _segment_sum(src, seg, n):
    return jax.ops.segment_sum(src, seg, n)
kernel_name = 'mk_prb_d2_jaxref_r8_400f1a'

def setup_inputs(seed: int=0):
    np.random.seed(seed)
    _w = jnp.asarray

    def _L0_attn_setup():
        import jax, jax.numpy as jnp
        import numpy as np
        from jax import lax
        HID = 128
        NH = 16
        NKV = 4
        HD = 64
        SPLIT = 64
        KS = 3

        def _dynamic_conv(x, w_kgen, b_kgen, w_conv, b_conv):
            context = x.mean(axis=1)
            dyn = context @ w_kgen.T + b_kgen
            gate = jax.nn.sigmoid(dyn).mean(axis=1)
            x_t = x.transpose(0, 2, 1)
            y = lax.conv_general_dilated(x_t, w_conv, window_strides=(1,), padding=[(KS // 2, KS // 2)], feature_group_count=HID, dimension_numbers=('NCH', 'OIH', 'NCH'))
            y = (y + b_conv[None, :, None]) * gate[:, None, None]
            return y.transpose(0, 2, 1)

        def _fixed_split_attention(x, w_q, w_k, w_v, w_o):
            B, S, _ = x.shape
            q = (x @ w_q.T).reshape(B, S, NH, HD).transpose(0, 2, 1, 3)
            k = (x @ w_k.T).reshape(B, S, NKV, HD).transpose(0, 2, 1, 3)
            v = (x @ w_v.T).reshape(B, S, NKV, HD).transpose(0, 2, 1, 3)
            n_rep = NH // NKV
            k = jnp.repeat(k, n_rep, axis=1)
            v = jnp.repeat(v, n_rep, axis=1)
            C = S // SPLIT
            kc = k.reshape(B, NH, C, SPLIT, HD)
            vc = v.reshape(B, NH, C, SPLIT, HD)
            scale = HD ** (-0.5)
            scores = jnp.einsum('bhqd,bhckd->bhcqk', q, kc) * scale
            w = jax.nn.softmax(scores.astype(jnp.float32), axis=-1).astype(q.dtype)
            chunk_out = jnp.einsum('bhcqk,bhckd->bhcqd', w, vc)
            sum_w = w.sum(axis=-1, keepdims=True)
            combined = (chunk_out * sum_w).sum(axis=2)
            total = sum_w.sum(axis=2)
            out = combined / (total + 1e-09)
            out = out.transpose(0, 2, 1, 3).reshape(B, S, NH * HD)
            return out @ w_o.T
        key = jax.random.key(seed)
        ks = jax.random.split(key, 9)
        s = 0.02
        return {'hidden_states': jax.random.normal(ks[0], (2, 256, HID), jnp.float32), 'w_q': jax.random.normal(ks[1], (NH * HD, HID), jnp.float32) * s, 'w_k': jax.random.normal(ks[2], (NKV * HD, HID), jnp.float32) * s, 'w_v': jax.random.normal(ks[3], (NKV * HD, HID), jnp.float32) * s, 'w_o': jax.random.normal(ks[4], (HID, NH * HD), jnp.float32) * s, 'w_kgen': jax.random.normal(ks[5], (KS, HID), jnp.float32) * s, 'b_kgen': jnp.zeros((KS,), jnp.float32), 'w_conv': jax.random.normal(ks[6], (HID, 1, KS), jnp.float32) * s, 'b_conv': jnp.zeros((HID,), jnp.float32)}
    _L0_attn_in = _L0_attn_setup()

    def _L0_ffn_setup():
        import jax, jax.numpy as jnp
        import numpy as np
        B, N, D, H, E = (4, 128, 128, 16, 8)
        DK = D // H
        HID = 4 * D
        EPS = 1e-05

        def _layernorm(x, w, b):
            m = jnp.mean(x, axis=-1, keepdims=True)
            v = jnp.mean(jnp.square(x - m), axis=-1, keepdims=True)
            return (x - m) * jax.lax.rsqrt(v + EPS) * w + b

        def _msa(x, w_qkv, w_proj):
            b, n, d = x.shape
            qkv = (x @ w_qkv).reshape(b, n, 3, H, DK)
            q = qkv[:, :, 0].transpose(0, 2, 1, 3)
            k = qkv[:, :, 1].transpose(0, 2, 1, 3)
            v = qkv[:, :, 2].transpose(0, 2, 1, 3)
            attn = jnp.einsum('bhnd,bhmd->bhnm', q, k) * (1.0 / np.sqrt(DK))
            attn = jax.nn.softmax(attn, axis=-1)
            y = jnp.einsum('bhnm,bhmd->bhnd', attn, v)
            y = y.transpose(0, 2, 1, 3).reshape(b, n, d)
            return y @ w_proj

        def _moe_mlp(x, gate_w, gate_b, w1, w2):
            b, n, d = x.shape
            xf = x.reshape(b * n, d)
            logits = xf @ gate_w + gate_b
            one_hot = jax.nn.one_hot(jnp.argmax(logits, axis=-1), E, dtype=xf.dtype)
            h = jax.nn.gelu(jnp.einsum('td,edh->teh', xf, w1), approximate=True)
            y = jnp.einsum('teh,ehd->ted', h, w2)
            out = jnp.einsum('te,ted->td', one_hot, y)
            return out.reshape(b, n, d)
        key = jax.random.key(seed)
        ks = jax.random.split(key, 8)
        s = 0.02
        return {'x': jax.random.normal(ks[0], (B, N, D), jnp.float32), 'ln1_w': jnp.ones((D,), jnp.float32), 'ln1_b': jnp.zeros((D,), jnp.float32), 'w_qkv': jax.random.normal(ks[1], (D, 3 * D), jnp.float32) * s, 'w_proj': jax.random.normal(ks[2], (D, D), jnp.float32) * s, 'ln2_w': jnp.ones((D,), jnp.float32), 'ln2_b': jnp.zeros((D,), jnp.float32), 'gate_w': jax.random.normal(ks[3], (D, E), jnp.float32) * s, 'gate_b': jnp.zeros((E,), jnp.float32), 'w1': jax.random.normal(ks[4], (E, D, HID), jnp.float32) * s, 'w2': jax.random.normal(ks[5], (E, HID, D), jnp.float32) * s}
    _L0_ffn_in = _L0_ffn_setup()

    def _L1_attn_setup():
        import jax, jax.numpy as jnp
        import numpy as np
        B, S, D = (4, 256, 128)
        key = jax.random.key(seed)
        kx, kq, kk, kv = jax.random.split(key, 4)
        bound = float(np.sqrt(6.0 / (D + D)))
        return {'x': jax.random.normal(kx, (B, S, D), dtype=jnp.float32), 'WQ': jax.random.uniform(kq, (D, D), jnp.float32, -bound, bound), 'WK': jax.random.uniform(kk, (D, D), jnp.float32, -bound, bound), 'WV': jax.random.uniform(kv, (D, D), jnp.float32, -bound, bound)}
    _L1_attn_in = _L1_attn_setup()

    def _L1_ffn_setup():
        import jax, jax.numpy as jnp
        import numpy as np
        import math
        BETA = 0.9
        THRESHOLD = 1.0
        NUM_STEPS = 5
        ALPHA = 2.0

        @jax.custom_vjp
        def spike_fn(u):
            return (u > 0).astype(u.dtype)

        def _spike_fwd(u):
            return (spike_fn(u), u)

        def _spike_bwd(u, g):
            s = jnp.pi / 2.0 * ALPHA * u
            return (g * (ALPHA / 2.0) / (1.0 + s * s),)
        spike_fn.defvjp(_spike_fwd, _spike_bwd)
        key = jax.random.key(seed)
        k1, k2, k3 = jax.random.split(key, 3)
        n_embd = 128
        x = jax.random.normal(k1, (4, 256, n_embd), dtype=jnp.float32)
        W_fc = jax.random.normal(k2, (4 * n_embd, n_embd), dtype=jnp.float32) / math.sqrt(n_embd)
        W_proj = jax.random.normal(k3, (n_embd, 4 * n_embd), dtype=jnp.float32) / math.sqrt(4 * n_embd)
        return {'x': x, 'W_fc': W_fc, 'W_proj': W_proj}
    _L1_ffn_in = _L1_ffn_setup()
    _d = {'L0_attn_hidden_states': _L0_attn_in['hidden_states'], 'L0_attn_w_q': _L0_attn_in['w_q'], 'L0_attn_w_k': _L0_attn_in['w_k'], 'L0_attn_w_v': _L0_attn_in['w_v'], 'L0_attn_w_o': _L0_attn_in['w_o'], 'L0_attn_w_kgen': _L0_attn_in['w_kgen'], 'L0_attn_b_kgen': _L0_attn_in['b_kgen'], 'L0_attn_w_conv': _L0_attn_in['w_conv'], 'L0_attn_b_conv': _L0_attn_in['b_conv'], 'L0_ffn_ln1_w': _L0_ffn_in['ln1_w'], 'L0_ffn_ln1_b': _L0_ffn_in['ln1_b'], 'L0_ffn_w_qkv': _L0_ffn_in['w_qkv'], 'L0_ffn_w_proj': _L0_ffn_in['w_proj'], 'L0_ffn_ln2_w': _L0_ffn_in['ln2_w'], 'L0_ffn_ln2_b': _L0_ffn_in['ln2_b'], 'L0_ffn_gate_w': _L0_ffn_in['gate_w'], 'L0_ffn_gate_b': _L0_ffn_in['gate_b'], 'L0_ffn_w1': _L0_ffn_in['w1'], 'L0_ffn_w2': _L0_ffn_in['w2'], 'L1_attn_WQ': _L1_attn_in['WQ'], 'L1_attn_WK': _L1_attn_in['WK'], 'L1_attn_WV': _L1_attn_in['WV'], 'L1_ffn_W_fc': _L1_ffn_in['W_fc'], 'L1_ffn_W_proj': _L1_ffn_in['W_proj']}
    _x0 = _d['L0_attn_hidden_states']
    _d['L0_attn_hidden_states'] = jax.random.normal(jax.random.fold_in(jax.random.key(seed), 1), (4, 512, 128), dtype=_x0.dtype)
    del _x0
    return _d

def reference(L0_attn_hidden_states, L0_attn_w_q, L0_attn_w_k, L0_attn_w_v, L0_attn_w_o, L0_attn_w_kgen, L0_attn_b_kgen, L0_attn_w_conv, L0_attn_b_conv, L0_ffn_ln1_w, L0_ffn_ln1_b, L0_ffn_w_qkv, L0_ffn_w_proj, L0_ffn_ln2_w, L0_ffn_ln2_b, L0_ffn_gate_w, L0_ffn_gate_b, L0_ffn_w1, L0_ffn_w2, L1_attn_WQ, L1_attn_WK, L1_attn_WV, L1_ffn_W_fc, L1_ffn_W_proj):

    def _L0_attn_ref(hidden_states, w_q, w_k, w_v, w_o, w_kgen, b_kgen, w_conv, b_conv):
        import jax, jax.numpy as jnp
        import numpy as np
        from jax import lax
        HID = 128
        NH = 16
        NKV = 4
        HD = 64
        SPLIT = 64
        KS = 3

        def _dynamic_conv(x, w_kgen, b_kgen, w_conv, b_conv):
            context = x.mean(axis=1)
            dyn = context @ w_kgen.T + b_kgen
            gate = jax.nn.sigmoid(dyn).mean(axis=1)
            x_t = x.transpose(0, 2, 1)
            y = lax.conv_general_dilated(x_t, w_conv, window_strides=(1,), padding=[(KS // 2, KS // 2)], feature_group_count=HID, dimension_numbers=('NCH', 'OIH', 'NCH'))
            y = (y + b_conv[None, :, None]) * gate[:, None, None]
            return y.transpose(0, 2, 1)

        def _fixed_split_attention(x, w_q, w_k, w_v, w_o):
            B, S, _ = x.shape
            q = (x @ w_q.T).reshape(B, S, NH, HD).transpose(0, 2, 1, 3)
            k = (x @ w_k.T).reshape(B, S, NKV, HD).transpose(0, 2, 1, 3)
            v = (x @ w_v.T).reshape(B, S, NKV, HD).transpose(0, 2, 1, 3)
            n_rep = NH // NKV
            k = jnp.repeat(k, n_rep, axis=1)
            v = jnp.repeat(v, n_rep, axis=1)
            C = S // SPLIT
            kc = k.reshape(B, NH, C, SPLIT, HD)
            vc = v.reshape(B, NH, C, SPLIT, HD)
            scale = HD ** (-0.5)
            scores = jnp.einsum('bhqd,bhckd->bhcqk', q, kc) * scale
            w = jax.nn.softmax(scores.astype(jnp.float32), axis=-1).astype(q.dtype)
            chunk_out = jnp.einsum('bhcqk,bhckd->bhcqd', w, vc)
            sum_w = w.sum(axis=-1, keepdims=True)
            combined = (chunk_out * sum_w).sum(axis=2)
            total = sum_w.sum(axis=2)
            out = combined / (total + 1e-09)
            out = out.transpose(0, 2, 1, 3).reshape(B, S, NH * HD)
            return out @ w_o.T
        h = _dynamic_conv(hidden_states, w_kgen, b_kgen, w_conv, b_conv)
        return _fixed_split_attention(h, w_q, w_k, w_v, w_o)

    def _L0_ffn_ref(x, ln1_w, ln1_b, w_qkv, w_proj, ln2_w, ln2_b, gate_w, gate_b, w1, w2):
        import jax, jax.numpy as jnp
        import numpy as np
        B, N, D, H, E = (4, 128, 128, 16, 8)
        DK = D // H
        HID = 4 * D
        EPS = 1e-05

        def _layernorm(x, w, b):
            m = jnp.mean(x, axis=-1, keepdims=True)
            v = jnp.mean(jnp.square(x - m), axis=-1, keepdims=True)
            return (x - m) * jax.lax.rsqrt(v + EPS) * w + b

        def _msa(x, w_qkv, w_proj):
            b, n, d = x.shape
            qkv = (x @ w_qkv).reshape(b, n, 3, H, DK)
            q = qkv[:, :, 0].transpose(0, 2, 1, 3)
            k = qkv[:, :, 1].transpose(0, 2, 1, 3)
            v = qkv[:, :, 2].transpose(0, 2, 1, 3)
            attn = jnp.einsum('bhnd,bhmd->bhnm', q, k) * (1.0 / np.sqrt(DK))
            attn = jax.nn.softmax(attn, axis=-1)
            y = jnp.einsum('bhnm,bhmd->bhnd', attn, v)
            y = y.transpose(0, 2, 1, 3).reshape(b, n, d)
            return y @ w_proj

        def _moe_mlp(x, gate_w, gate_b, w1, w2):
            b, n, d = x.shape
            xf = x.reshape(b * n, d)
            logits = xf @ gate_w + gate_b
            one_hot = jax.nn.one_hot(jnp.argmax(logits, axis=-1), E, dtype=xf.dtype)
            h = jax.nn.gelu(jnp.einsum('td,edh->teh', xf, w1), approximate=True)
            y = jnp.einsum('teh,ehd->ted', h, w2)
            out = jnp.einsum('te,ted->td', one_hot, y)
            return out.reshape(b, n, d)
        x = x + _msa(_layernorm(x, ln1_w, ln1_b), w_qkv, w_proj)
        x = x + _moe_mlp(_layernorm(x, ln2_w, ln2_b), gate_w, gate_b, w1, w2)
        return x

    def _L1_attn_ref(x, WQ, WK, WV):
        import jax, jax.numpy as jnp
        import numpy as np
        B, S, D = (4, 256, 128)
        dk = WQ.shape[1]
        q = x @ WQ
        k = x @ WK
        v = x @ WV
        scores = jnp.einsum('bsd,btd->bst', q, k) / jnp.sqrt(jnp.asarray(dk, x.dtype))
        s = x.shape[1]
        causal = jnp.tril(jnp.ones((s, s), dtype=bool))
        scores = jnp.where(causal[None, :, :], scores, jnp.asarray(-jnp.inf, x.dtype))
        attention = jax.nn.softmax(scores, axis=-1)
        return jnp.einsum('bst,btd->bsd', attention, v)

    def _L1_ffn_ref(x, W_fc, W_proj):
        import jax, jax.numpy as jnp
        import numpy as np
        import math
        BETA = 0.9
        THRESHOLD = 1.0
        NUM_STEPS = 5
        ALPHA = 2.0

        @jax.custom_vjp
        def spike_fn(u):
            return (u > 0).astype(u.dtype)

        def _spike_fwd(u):
            return (spike_fn(u), u)

        def _spike_bwd(u, g):
            s = jnp.pi / 2.0 * ALPHA * u
            return (g * (ALPHA / 2.0) / (1.0 + s * s),)
        spike_fn.defvjp(_spike_fwd, _spike_bwd)
        h = jnp.square(jax.nn.relu(jnp.einsum('bsd,fd->bsf', x, W_fc)))
        y = jnp.einsum('bsf,df->bsd', h, W_proj)

        def step(mem, _):
            reset = jax.lax.stop_gradient(spike_fn(mem - THRESHOLD))
            mem_new = BETA * mem + y - reset * THRESHOLD
            spk = spike_fn(mem_new - THRESHOLD)
            return (mem_new, spk)
        mem0 = jnp.zeros_like(y)
        _, spks = jax.lax.scan(step, mem0, None, length=NUM_STEPS)
        return jnp.sum(spks, axis=0) / NUM_STEPS
    x = L0_attn_hidden_states
    xn = _layernorm(x, axis=-1)
    x = x + _L0_attn_ref(xn, L0_attn_w_q, L0_attn_w_k, L0_attn_w_v, L0_attn_w_o, L0_attn_w_kgen, L0_attn_b_kgen, L0_attn_w_conv, L0_attn_b_conv) + _L0_ffn_ref(xn, L0_ffn_ln1_w, L0_ffn_ln1_b, L0_ffn_w_qkv, L0_ffn_w_proj, L0_ffn_ln2_w, L0_ffn_ln2_b, L0_ffn_gate_w, L0_ffn_gate_b, L0_ffn_w1, L0_ffn_w2)
    xn = _layernorm(x, axis=-1)
    x = x + _L1_attn_ref(xn, L1_attn_WQ, L1_attn_WK, L1_attn_WV) + _L1_ffn_ref(xn, L1_ffn_W_fc, L1_ffn_W_proj)
    return x

_drawn_inputs = setup_inputs


def setup_inputs(seed=0):
    import zlib

    import numpy as np

    out = dict(_drawn_inputs(seed))
    spreads = {'L0_attn_b_kgen': (0.0, 0.8),
     'L0_attn_b_conv': (0.0, 0.8),
     'L0_ffn_ln1_w': (1.0, 0.6),
     'L0_ffn_ln1_b': (0.0, 0.8),
     'L0_ffn_ln2_w': (1.0, 0.6),
     'L0_ffn_ln2_b': (0.0, 2.0),
     'L0_ffn_gate_b': (0.0, 1.585)}
    factors = {'L0_attn_w_q': 32.944,
     'L0_attn_w_k': 35.503,
     'L0_attn_w_v': 8.0,
     'L0_attn_w_o': 8.0,
     'L0_attn_w_kgen': 60.805,
     'L0_attn_w_conv': 30.234,
     'L0_ffn_w_qkv': 8.0,
     'L0_ffn_w_proj': 8.0,
     'L0_ffn_gate_w': 4.88,
     'L0_ffn_w1': 3.954,
     'L0_ffn_w2': 3.862,
     'L1_attn_WQ': 6.179,
     'L1_attn_WK': 5.813}
    for name, (base, spread) in spreads.items():
        noise = np.random.default_rng([zlib.crc32(name.encode()), seed]).standard_normal(out[name].shape)
        drawn = base * np.exp(spread * noise) if base else spread * noise
        out[name] = jnp.asarray(drawn.astype(out[name].dtype))
    for name, factor in factors.items():
        out[name] = (out[name] * factor).astype(out[name].dtype)
    return out
```

```python
from contextlib import ExitStack

import numpy as np

import concourse.bass as bass
from concourse import mybir

F32 = mybir.dt.float32
F32R = mybir.dt.float32r
BF16 = mybir.dt.bfloat16
ALU = mybir.AluOpType
ACT = mybir.ActivationFunctionType
AX_X = mybir.AxisListType.X

P = 128
BATCH, SEQ, D = 4, 512, 128
NT = BATCH * SEQ // P
QT = SEQ // P
KT = SEQ // P
GROUPS = 4
HG = 4
HDA = 64
CH = 64
NCH = SEQ // CH
HDB = 8
ITERS = BATCH * GROUPS
EXPERTS, FF = 8, 512
FB = FF // P
EPS = 1e-5
SCALE_A = HDA ** -0.5
SCALE_B = float(1.0 / np.sqrt(HDB))
SCALE_C = float(1.0 / np.sqrt(D))

C_ID, C_NEG, C_SELB, C_BD, C_SELL, C_CAUSAL, C_COL = 0, 128, 256, 384, 512, 640, 768
C_N = 768 + 24


def constant_columns():
    c = np.zeros((P, C_N), np.float32)
    r = np.arange(P)
    c[:, C_ID:C_ID + P] = np.eye(P)
    c[:, C_NEG:C_NEG + P] = -np.eye(P)
    c[:, C_SELB:C_SELB + P] = r[:, None] == 32 * (r[None, :] // 32) + 8
    c[:, C_BD:C_BD + P] = (r[:, None] // 32 == r[None, :] // 32) & (r[:, None] % 32 < NCH)
    for kt in range(KT):
        m = np.arange(32)
        c[:, C_SELL + 32 * kt:C_SELL + 32 * kt + 32] = (m[None, :] % NCH) == (2 * kt + r[:, None] // CH)
    c[:, C_CAUSAL:C_CAUSAL + P] = np.where(r[None, :] > r[:, None], -1e30, 0.0)
    k = C_COL
    c[:, k] = -1.0 * (r >= 64)
    c[:, k + 1] = -1.0 * ((r % 32 >= 9) & (r % 32 < 17))
    c[:, k + 2] = -1.0 * ((r % 32 >= 17) & (r % 32 < 25))
    c[:, k + 3] = -1.0 * ((r % 32 >= 8) & (r % 32 < 16))
    for j in range(HG):
        c[:, k + 4 + j] = r // 32 == j
        c[:, k + 8 + j] = r == 32 * j
    c[:, k + 12:k + 12 + EXPERTS] = EXPERTS - np.arange(EXPERTS)
    return c


S1 = [("SA", 0, 0), ("SA", 0, 1), ("SA", 1, 0), ("PB", 0, 0), ("SA", 1, 1), ("PB", 0, 1),
      ("SA", 2, 0), ("PB", 1, 0), ("SA", 2, 1), ("PB", 1, 1), ("SA", 3, 0), ("PB", 2, 0),
      ("SA", 3, 1), ("PB", 2, 1), ("PB", 3, 0), ("PB", 3, 1)]
S2 = [("qA", 0), ("qA", 1), ("kA",)]
S3 = []
for _j in range(HG):
    for _h in range(2):
        S3 += [("BC", _j, _h), ("SB", _j, _h), ("PA", _j, _h)]
BODY = [("qkB",)] + S1 + S2 + S3 + [("y",)]
PROLOGUE = S2 + [u for u in S3 if u[0] == "PA"]
NEXT = set(PROLOGUE)
EPILOGUE = [u for u in BODY if u not in NEXT]
N_PRO, N_BODY = len(PROLOGUE), len(BODY)
SLOTS = 3
assert N_BODY % SLOTS == 0


class Ring:

    def __init__(self, section, it):
        self.order, first = {"prologue": (PROLOGUE, 0), "body": (BODY, N_PRO),
                             "epilogue": (EPILOGUE, N_PRO + N_BODY * (ITERS - 1))}[section]
        self.place = {u: first + n for n, u in enumerate(self.order)}
        self.it = it
        self.section = section

    def slot(self, use):
        return self.place[use] % SLOTS

    def before(self, use):
        n = self.order.index(use)
        return self.order[n - SLOTS] if n >= SLOTS else None

    def filled(self, use):
        n = self.place[use] + 1
        return self.it * N_BODY + n if self.section == "body" else n


def build(nc, x, w_q, w_k, w_v, w_o, w_kgen, b_kgen, w_conv, b_conv, ln1_w, ln1_b, w_qkv, w_proj,
          ln2_w, ln2_b, gate_w, gate_b, w1, w2, c_wq, c_wk, c_wv, w_fc, w_pj, consts, out):
    with ExitStack() as ctx:
        def sb(name, shape, dt=F32):
            return ctx.enter_context(nc.sbuf_tensor(name, shape, dt))

        def sem(name):
            return ctx.enter_context(nc.semaphore(name))

        cst = sb("cst", [P, C_N])
        ones_shift = sb("ones_shift", [P, HG * KT, P], BF16)
        spread = sb("spread", [P, HG * KT, P], F32R)
        neg_bf = sb("neg_bf", [P, P], BF16)
        acc1 = sb("acc1", [P, NT, D])
        acc2 = sb("acc2", [P, NT, D])
        hT = sb("hT", [P, BATCH * SEQ])
        uT = sb("uT", [P, BATCH * SEQ])
        wqT = sb("wqT", [P, GROUPS, HG, HDA])
        wkT = sb("wkT", [P, GROUPS, HDA])
        w2all = sb("w2all", [P, GROUPS, 2, P])
        wA = sb("wA", [P, HG + 1, 2, HDA])
        wB = sb("wB", [P, 2, P])
        woT = sb("woT", [P, 2 * GROUPS, D])
        wpP = sb("wpP", [P, GROUPS, D])
        v_all = sb("v_all", [P, NT, GROUPS, HDA])
        vb_all = sb("vb_all", [P, NT, GROUPS * HG, HDB])
        QA = sb("QA", [P, HG, SEQ], F32R)
        HA = sb("HA", [P, 2, SEQ], F32R)
        KAh = sb("KAh", [P, SEQ], F32R)
        KAl = sb("KAl", [P, SEQ], F32R)
        QB = sb("QB", [P, SEQ], F32R)
        KB = sb("KB", [P, SEQ], F32R)
        HB = sb("HB", [P, 2, SEQ], F32R)
        KBj = sb("KBj", [P, HG, SEQ], F32R)
        VA = sb("VA", [P, KT, HDA])
        VB = sb("VB", [P, KT, HG, 32])
        eA = sb("eA", [P, HG, KT, SEQ])
        eB = sb("eB", [P, 2, KT, SEQ])
        maxA = sb("maxA", [P, QT, P], BF16)
        maxB = sb("maxB", [P, QT, P], BF16)
        shiftA = sb("shiftA", [P, SEQ], BF16)
        cr = sb("cr", [P, SEQ])
        cw = sb("cw", [P, SEQ])
        ct = sb("ct", [P, SEQ])
        cf = sb("cf", [P, SEQ])
        cfh = sb("cfh", [P, SEQ], F32R)
        cfl = sb("cfl", [P, SEQ], F32R)
        oB = sb("oB", [P, SEQ])
        rB = sb("rB", [P, SEQ])
        oA = sb("oA", [P, 2, SEQ])
        small = sb("small", [P, 160])
        wfcT = sb("wfcT", [P, FF])
        wpjT = sb("wpjT", [P, FB, D])
        cols = sb("cols", [P, 16])
        kgb = sb("kgb", [P, 3])
        gb = sb("gb", [P, EXPERTS])
        gw = sb("gw", [P, EXPERTS])
        c_w = sb("c_w", [P, 3, D])
        ps = ctx.enter_context(nc.psum_tensor("ps", [P, 8, 512], F32))

        ident = cst[:, C_ID:C_ID + P]

        def col(n):
            return cst[:, C_COL + n:C_COL + n + 1]

        eAf = eA[:].rearrange("p a b c -> p (a b c)")
        eBf = eB[:].rearrange("p a b c -> p (a b c)")
        raw = eBf[:, 0:28 * P].rearrange("p (n d) -> p n d", d=D)
        qkv_raw = eBf[:, 28 * P:31 * P]
        kg_raw = eBf[0:3, 31 * P:32 * P]
        xc = eAf[:, 0:2048].rearrange("p (n d) -> p n d", d=D)
        sq = eAf[:, 2048:4096].rearrange("p (n d) -> p n d", d=D)
        xnT = eAf[:, 4096:6144].rearrange("p (b s) -> p b s", b=BATCH)
        wvT = eAf[:, 6144:6400]
        kgT = eAf[:, 6400:6403]
        ctxb = eAf[:, 6528:7040].rearrange("p (b m) -> p b m", b=BATCH)
        un = sq
        cacc = eAf[:, 0:2048].rearrange("p (b s) -> p b s", b=BATCH)

        s_cst = sem("constants_loaded")
        s_x = sem("x_loaded")
        s_w = sem("weights_loaded")
        s_qkv = sem("qkv_loaded")
        s_col = sem("columns_loaded")
        s_wpj = sem("wproj_loaded")
        s_chain = sem("vector_chain")
        s_pset = sem("gpsimd_constants")
        s_wt = sem("weights_transposed")
        s_wtc = sem("weights_copied")
        s_cen = sem("centred")
        s_sqd = sem("squared")
        s_var = sem("variance")
        s_std = sem("deviation")
        s_nrm = sem("normalised")
        s_xt = sem("xn_transposed")
        s_xtc = sem("xn_copied")
        s_ut = sem("ln1_transposed")
        s_utc = sem("ln1_copied")
        s_ctx = sem("context_ready")
        s_dyn = sem("gate_filled")
        s_z = sem("gate_argument")
        s_ez = sem("gate_exponential")
        s_h = sem("conv_ready")
        s_v = sem("values_filled")
        s_vc = sem("values_copied")
        s_zt = sem("ln2_transposed")
        s_ztc = sem("ln2_copied")
        s_zh = sem("ln2_high")
        s_zl = sem("ln2_low")
        s_gl = sem("gate_logits_filled")
        s_hot = sem("one_hot_ready")
        s_yt = sem("norm2_transposed")
        s_ytc = sem("norm2_copied")
        s_vv = sem("L1_values_filled")
        s_vvc = sem("L1_values_copied")

        ring_full = sem("score_tile_filled")
        s_wA = sem("wA_ready")
        s_wB = sem("wB_ready")
        s_VA = sem("VA_ready")
        s_VB = sem("VB_ready")
        s_HA = sem("HA_rounded")
        s_KAh = sem("KAh_ready")
        s_QA = sem("QA_ready")
        s_KAl = sem("KAl_ready")
        s_HB = sem("HB_rounded")
        s_KB = sem("KB_ready")
        s_QB = sem("QB_ready")
        s_KBj = sem("KBj_ready")
        s_maxA = sem("maxA_taken")
        s_maxB = sem("maxB_taken")
        s_mtA = sem("shiftA_filled")
        s_shA = sem("shiftA_ready")
        s_mtB = sem("shiftB_filled")
        s_QBs = sem("QB_shifted")
        s_eA = sem("eA_ready")
        s_eB = sem("eB_ready")
        s_L = sem("chunk_sums_filled")
        s_r = sem("chunk_reciprocal")
        s_sw = sem("chunk_weight_sum")
        s_tot = sem("total_filled")
        s_c1 = sem("factor_times_sum")
        s_te = sem("total_with_eps")
        s_rt = sem("total_reciprocal")
        s_cf = sem("factor_ready")
        s_cfh = sem("factor_high")
        s_cfl = sem("factor_low")
        s_wts = sem("eA_weighted")
        s_ota = sem("outA_filled")
        s_otb = sem("outB_filled")
        s_oA = sem("outA_copied")
        s_oB = sem("outB_copied")
        s_lb = sem("outB_sums_filled")
        s_rB = sem("outB_reciprocal")
        s_yB = sem("outB_scaled")
        s_acc = sem("outputs_added")

        s_m1 = [sem(f"expert_w1_loaded{u}") for u in range(2)]
        s_m2 = [sem(f"expert_w2_loaded{u}") for u in range(2)]
        s_mh = sem("expert_w1_high")
        s_ml = sem("expert_w1_low")
        s_hf = sem("expert_hidden_filled")
        s_hr = sem("expert_hidden_ready")
        s_yf = sem("expert_out_filled")
        s_ya = sem("expert_out_added")

        s_lq = sem("L1_qk_filled")
        s_lqc = sem("L1_qk_copied")
        s_ls = sem("L1_scores_filled")
        s_lm = sem("L1_scores_masked")
        s_lx = sem("L1_max_negated")
        s_le = sem("L1_exp_ready")
        s_lt = sem("L1_transposed")
        s_ltc = sem("L1_transposed_copied")
        s_lo = sem("L1_out_filled")
        s_loa = sem("L1_out_added")
        s_fh = sem("ffn_hidden_filled")
        s_fr = sem("ffn_relu_ready")
        s_fs = sem("ffn_square_ready")
        s_fy = sem("ffn_out_filled")
        s_ff = sem("ffn_bank_free")
        s_sp = sem("spike_step")
        s_fin = sem("batch_finished")
        s_out = sem("stored")

        block = ctx.enter_context(nc.Block())

        w1f = eAf[:, 0:1024].rearrange("p (u f) -> p u f", u=2)
        w2f = eAf[:, 1024:2048].rearrange("p (u n d) -> p u n d", u=2, n=FB)
        hid = eAf[:, 2048:6144].rearrange("p (u n t) -> p u n t", u=2, n=FB)
        zn = eBf[:, 0:2048].rearrange("p (n d) -> p n d", d=D)
        zT = eBf[:, 2048:4096]
        zsq = hT[:].rearrange("p (n d) -> p n d", d=D)
        zH = QA[:].rearrange("p a b -> p (a b)")
        zL = KBj[:].rearrange("p a b -> p (a b)")
        spr = spread[:].rearrange("p a b -> p (a b)")
        w1h = spr[:, 0:1024].rearrange("p (u f) -> p u f", u=2)
        w1l = spr[:, 1024:2048].rearrange("p (u f) -> p u f", u=2)
        hot = sb("hot", [P, EXPERTS, NT])
        lg = sb("lg", [P, NT, EXPERTS])
        lge = sb("lge", [P, NT, EXPERTS])
        yn = eAf[:, 0:2048].rearrange("p (n d) -> p n d", d=D)
        ynsq = eAf[:, 2048:4096].rearrange("p (n d) -> p n d", d=D)
        ynT = eAf[:, 4096:6144]
        vC = eAf[:, 6144:8192].rearrange("p (n d) -> p n d", d=D)
        qkC = eBf[:, 0:1024].rearrange("p (u t) -> p u t", u=2)
        pC = eBf[:, 1024:3072].rearrange("p (q t) -> p q t", q=QT)
        pT = hT[:, 0:1280].rearrange("p (n t) -> p n t", n=10)
        fr = uT[:].rearrange("p (n t) -> p n t", n=FB)
        lif = v_all[:].rearrange("p a b c -> p (a b c)")
        t3 = vb_all[:].rearrange("p a b c -> p (a b c)")


        MEAN, VAR, STD, RSTD, CTX, DYN, GATE = 16, 32, 48, 64, 80, 96, 128

        def per_tile(c):
            return small[:, c:c + NT].unsqueeze(2).broadcast_to([P, NT, D])

        def score_c(q):
            return ps[:, (5, 7, 0, 1)[q], 0:P * (q + 1)]

        x_v = x.rearrange("b (n p) d -> p (b n) d", p=P)
        out_v = out.rearrange("b (n p) d -> b p n d", p=P)
        N_COLS = 12
        N_PSET = 5 + 3 + 2 * 3 * GROUPS

        @block.sync
        def _(sp):
            for b in range(BATCH):
                sp.dma_start(acc1[:, b * QT:(b + 1) * QT, :], x_v[:, b * QT:(b + 1) * QT, :]).then_inc(s_x, 16)
            sp.dma_start(raw[:, 0:8, :], w_q.rearrange("(n p) d -> p n d", p=P)).then_inc(s_w, 16)
            sp.dma_start(raw[:, 8:10, :], w_k.rearrange("(n p) d -> p n d", p=P)).then_inc(s_w, 16)
            sp.dma_start(raw[:, 10:12, :], w_v.rearrange("(n p) d -> p n d", p=P)).then_inc(s_w, 16)
            sp.dma_start(raw[:, 12:20, :], w_o.rearrange("o (n d) -> o n d", d=P)).then_inc(s_w, 16)
            sp.dma_start(raw[:, 20:24, :], w_fc.rearrange("(n p) d -> p n d", p=P)).then_inc(s_w, 16)
            sp.dma_start(raw[:, 24:28, :], w_pj.rearrange("o (n d) -> o n d", d=P)).then_inc(s_w, 16)
            sp.dma_start(kg_raw, w_kgen).then_inc(s_w, 16)

            for u in range(2):
                if u == 0:
                    sp.wait_ge(s_acc, 2 * ITERS + 1)
                sp.dma_start(w1f[:, u, :], w1[u]).then_inc(s_m1[u], 16)
                sp.dma_start(w2f[:, u], w2[u].rearrange("(n p) d -> p n d", p=P)).then_inc(s_m2[u], 16)
            w1_p = w1.rearrange("(i u) d f -> i u d f", u=2)
            w2_p = w2.rearrange("(i u) (n p) d -> i u p n d", u=2, p=P)
            with sp.Fori(1, EXPERTS // 2) as i:
                for u in range(2):
                    sp.wait_ge(s_yf, i * 8 + (4 * u + 4))
                    sp.dma_start(w1f[:, u, :], w1_p[i, u]).then_inc(s_m1[u], 16)
                    sp.dma_start(w2f[:, u], w2_p[i, u]).then_inc(s_m2[u], 16)
            with sp.Fori(0, BATCH) as b:
                sp.wait_ge(s_fin, b + 2)
                sp.dma_start(out_v[b], acc1[:, bass.ds(b * QT, QT), :]).then_inc(s_out, 16)
            sp.wait_ge(s_out, 16 * BATCH)

        @block.gpsimd
        def _(pool):
            g = nc.gpsimd
            g.memset(wpP[:], 0.0).then_inc(s_pset, 1)
            g.memset(w2all[:], 0.0).then_inc(s_pset, 1)
            g.memset(VB[:], 1.0).then_inc(s_pset, 1)
            g.memset(maxA[:], 0.0).then_inc(s_pset, 1)
            g.memset(maxB[:], 0.0).then_inc(s_pset, 1)
            pool.wait_ge(s_pset, 5)
            wp_v = w_proj.rearrange("(g j i) d -> j i g d", j=HG, i=HDB)
            for j in range(HG):
                g.dma_start(wpP[32 * j:32 * j + HDB, :, :], wp_v[j]).then_inc(s_wpj, 16)
            pool.wait_ge(s_cst, 16)
            pick = ident.rearrange("p (j r) -> p j r", r=32)
            def keys(rows):
                return pick[:, :, rows:rows + NCH].unsqueeze(3).broadcast_to([P, HG, NCH, CH])
            g.tensor_copy(ones_shift[:].rearrange("p (j a) (b m) -> p j (a b) m", j=HG, b=2), keys(0)).then_inc(s_pset, 1)
            g.tensor_tensor(spread[:].rearrange("p (j a) (b m) -> p j (a b) m", j=HG, b=2), keys(0), keys(NCH),
                            ALU.add).then_inc(s_pset, 1)
            g.tensor_copy(neg_bf[:], cst[:, C_NEG:C_NEG + P]).then_inc(s_pset, 1)
            pool.wait_ge(s_qkv, 16)
            for k in range(2):
                src = qkv_raw[:, k * P:(k + 1) * P].rearrange("p (a e) -> p a e", e=HDB)
                for r in range(3):
                    dst = w2all[:, :, k, :].rearrange("p g (j m) -> p g j m", m=32)[:, :, :, 1 + HDB * r:1 + HDB * (r + 1)]
                    for q in range(GROUPS):
                        g.tensor_copy(dst[:, q], src[:, HG * q:HG * q + HG, :]).then_inc(s_pset, 1)

            def copy_wA(g_idx):
                q = wqT[:, bass.ds(g_idx, 1), :, :].rearrange("p g h e -> p (g h) e")
                k = wkT[:, bass.ds(g_idx, 1), :]
                for c in range(2):
                    g.tensor_copy(wA[:, 0:HG, c, :], q).then_inc(s_wA, 1)
                    g.tensor_copy(wA[:, HG:HG + 1, c, :], k).then_inc(s_wA, 1)

            def copy_wB(g_idx):
                g.tensor_copy(wB[:], w2all[:, bass.ds(g_idx, 1), :, :].rearrange("p g k c -> p (g k) c")).then_inc(s_wB, 1)

            def body(it, ring, nxt):
                g_idx = it % GROUPS
                b_idx = it // GROUPS
                pool.wait_ge(s_oB, it + 1)
                g.tensor_copy(VB[:, :, :, 0:HDB],
                              vb_all[:, bass.ds(b_idx * QT, QT), bass.ds(g_idx * HG, HG), :]).then_inc(s_VB, 1)
                pool.wait_ge(s_oA, it * 2 + 2)
                g.tensor_copy(VA[:], v_all[:, bass.ds(b_idx * QT, QT), bass.ds(g_idx, 1), :]
                              .rearrange("p t g e -> p t (g e)")).then_inc(s_VA, 1)
                pool.wait_ge(s_pset, N_PSET)
                pool.wait_ge(s_KB, it + 1)
                for j in range(HG):
                    g.tensor_scalar(KBj[:, j, :], KB[:].bitcast(F32), col(4 + j), col(8 + j), ALU.mult,
                                    ALU.add).then_inc(s_KBj, 1)
                if nxt:
                    pool.wait_ge(ring_full, ring.filled(("qkB",)))
                    copy_wA((it + 1) % GROUPS)
                    copy_wB((it + 1) % GROUPS)
                pool.wait_ge(s_sw, it + 1)
                g.tensor_tensor(cr[:], cr[:], cw[:], ALU.mult).then_inc(s_c1, 1)

            pool.wait_ge(s_wtc, 9)
            pool.wait_ge(s_pset, N_PSET)
            copy_wA(0)
            copy_wB(0)
            pool.wait_ge(s_vc, 12)
            with g.Fori(0, ITERS - 1) as it:
                body(it, Ring("body", it), True)
            body(ITERS - 1, Ring("epilogue", ITERS - 1), False)
            pool.wait_ge(s_wpj, 16 * HG)

        @block.scalar
        def _(act):
            s = nc.scalar
            act.dma_start(cst[:], consts).then_inc(s_cst, 16)
            act.dma_start(qkv_raw, w_qkv).then_inc(s_qkv, 16)
            act.dma_start(cols[:, 0:3], w_conv.rearrange("d a k -> d (a k)")).then_inc(s_col, 16)
            for n, a in enumerate((b_conv, ln1_w, ln1_b, ln2_w, ln2_b)):
                act.dma_start(cols[:, 3 + n:4 + n], a.rearrange("(d a) -> d a", a=1)).then_inc(s_col, 16)
            act.dma_start(kgb[:], b_kgen.partition_broadcast(P)).then_inc(s_col, 16)
            act.dma_start(gb[:], gate_b.partition_broadcast(P)).then_inc(s_col, 16)
            act.dma_start(gw[:], gate_w).then_inc(s_col, 16)
            for n, a in enumerate((c_wq, c_wk, c_wv)):
                act.dma_start(c_w[:, n, :], a).then_inc(s_col, 16)

            def deviation(n):
                src, dst = ((xc, sq), (xc, sq), (zn, zsq), (yn, ynsq))[n]
                act.wait_ge(s_cen, n + 1)
                s.activation(dst, src, ACT.Square).then_inc(s_sqd, 1)
                act.wait_ge(s_var, n + 1)
                s.activation(small[:, STD:STD + NT], small[:, VAR:VAR + NT], ACT.Sqrt).then_inc(s_std, 1)

            deviation(0)
            act.wait_ge(s_wt, 1)
            s.copy(wqT[:, 0:2], ps[:, 0, :].rearrange("p (g h e) -> p g h e", g=2, h=HG)).then_inc(s_wtc, 1)
            act.wait_ge(s_wt, 2)
            s.copy(wqT[:, 2:4], ps[:, 1, :].rearrange("p (g h e) -> p g h e", g=2, h=HG)).then_inc(s_wtc, 1)
            act.wait_ge(s_wt, 3)
            s.copy(wkT[:], ps[:, 2, 0:256].rearrange("p (g e) -> p g e", g=GROUPS)).then_inc(s_wtc, 1)
            s.copy(wvT, ps[:, 2, 256:512]).then_inc(s_wtc, 1)
            for n in range(2):
                act.wait_ge(s_wt, 4 + n)
                s.copy(woT[:, 4 * n:4 * n + 4, :], ps[:, 3 + n, :].rearrange("p (n d) -> p n d", n=4)).then_inc(s_wtc, 1)
            act.wait_ge(s_wt, 6)
            s.copy(wfcT[:], ps[:, 5, :]).then_inc(s_wtc, 1)
            act.wait_ge(s_wt, 7)
            s.copy(wpjT[:], ps[:, 6, :].rearrange("p (n d) -> p n d", n=4)).then_inc(s_wtc, 1)
            act.wait_ge(s_wt, 8)
            s.copy(kgT, ps[:, 7, 0:3]).then_inc(s_wtc, 1)
            for b in range(BATCH):
                act.wait_ge(s_xt, b + 1)
                s.copy(xnT[:, b, :], ps[:, b, :]).then_inc(s_xtc, 1)
            deviation(1)
            act.wait_ge(s_col, 16 * N_COLS)
            for b in range(BATCH):
                act.wait_ge(s_ut, b + 1)
                s.activation(uT[:, b * SEQ:(b + 1) * SEQ], ps[:, 4 + b, :], ACT.Identity, scale=cols[:, 4:5],
                             bias=cols[:, 5:6]).then_inc(s_utc, 1)
            act.wait_ge(s_z, 1)
            s.activation(small[:, DYN:DYN + 12], small[:, DYN:DYN + 12], ACT.Exp, scale=-1.0).then_inc(s_ez, 1)
            for n in range(8):
                act.wait_ge(s_v, n + 1)
                s.copy(v_all[:, 2 * n:2 * n + 2], ps[:, n, :].rearrange("p (t g e) -> p t g e", t=2, g=GROUPS)).then_inc(s_vc, 1)
            for n in range(4):
                act.wait_ge(s_v, 9 + n)
                s.copy(vb_all[:, 4 * n:4 * n + 4].rearrange("p t h e -> p (t h e)"), ps[:, n, :]).then_inc(s_vc, 1)

            def tile(ring, use):
                r = ring.slot(use)
                return ps[:, 2 * r:2 * r + 2, :]

            def round_next(m, ring):
                for p in range(2):
                    t = tile(ring, ("qA", p))
                    act.wait_ge(ring_full, ring.filled(("qA", p)))
                    act.wait_ge(s_QA, m * 2 + (p + 1))
                    s.copy(HA[:], t).then_inc(s_HA, 1)
                t = tile(ring, ("kA",))
                act.wait_ge(ring_full, ring.filled(("kA",)))
                s.copy(KAh[:], t[:, 0, :]).then_inc(s_KAh, 1)

            def shift_a(m):
                act.wait_ge(s_mtA, m + 1)
                s.copy(shiftA[:], ps[:, 7, :]).then_inc(s_shA, 1)

            def body(it, ring, nxt):
                act.wait_ge(ring_full, ring.filled(("qkB",)))
                t = tile(ring, ("qkB",))
                s.copy(HB[:], t).then_inc(s_HB, 1)
                for use in S1:
                    if use[0] == "SA":
                        _, j, h = use
                        t = tile(ring, use)
                        act.wait_ge(ring_full, ring.filled(use))
                        s.activation(eA[:, j, 2 * h:2 * h + 2, :], t, ACT.Exp, scale=SCALE_A).then_inc(s_eA, 1)
                if nxt:
                    round_next(it + 1, ring)
                act.wait_ge(s_cf, it + 1)
                s.copy(cfh[:], cf[:]).then_inc(s_cfh, 1)
                for use in S3:
                    if use[0] == "SB":
                        _, j, h = use
                        t = tile(ring, use)
                        act.wait_ge(ring_full, ring.filled(use))
                        s.activation(eB[:, j % 2, 2 * h:2 * h + 2, :], t, ACT.Exp, scale=SCALE_B).then_inc(s_eB, 1)
                        if (j, h) == (3, 0):
                            act.wait_ge(s_ota, it * 2 + 1)
                            s.copy(oA[:, 0, :], ps[:, 7, :]).then_inc(s_oA, 1)
                act.wait_ge(s_otb, it + 1)
                s.copy(oB[:], ps[:, 6, :]).then_inc(s_oB, 1)
                act.wait_ge(s_ota, it * 2 + 2)
                s.copy(oA[:, 1, :], ps[:, 7, :]).then_inc(s_oA, 1)
                if nxt:
                    shift_a(it + 1)

            s.sem_inc(s_eB, 1)
            s.sem_inc(s_oB, 1)
            s.sem_inc(s_oA, 1)
            s.sem_inc(s_oA, 1)
            round_next(0, Ring("prologue", 0))
            shift_a(0)
            with act.Fori(0, ITERS - 1) as it:
                body(it, Ring("body", it), True)
            body(ITERS - 1, Ring("epilogue", ITERS - 1), False)

            deviation(2)
            for b in range(BATCH):
                act.wait_ge(s_zt, b + 1)
                s.activation(zT[:, b * SEQ:(b + 1) * SEQ], ps[:, b, :], ACT.Identity, scale=cols[:, 6:7],
                             bias=cols[:, 7:8]).then_inc(s_ztc, 1)
            act.wait_ge(s_ztc, BATCH)
            s.copy(zH, zT).then_inc(s_zh, 1)
            s.sem_inc(s_hr, 1)
            s.sem_inc(s_hr, 1)
            with act.Fori(0, EXPERTS // 2) as i:
                for u in range(2):
                    act.wait_ge(s_m1[u], i * 16 + 16)
                    act.wait_ge(s_yf, i * 8 + (4 * u + 4))
                    s.copy(w1h[:, u, :], w1f[:, u, :]).then_inc(s_mh, 1)
                    for tb in range(BATCH):
                        t = 4 * u + tb
                        act.wait_ge(s_yf, i * 8 + (t + 7))
                        for h in range(2):
                            act.wait_ge(s_hf, i * 16 + (2 * t + h + 1))
                            s.activation(hid[:, t % 2, 2 * h:2 * h + 2, :], ps[:, 2 * h:2 * h + 2, :],
                                         ACT.Gelu_apprx_tanh).then_inc(s_hr, 1)

            deviation(3)
            for b in range(BATCH):
                act.wait_ge(s_yt, b + 1)
                s.copy(ynT[:, b * SEQ:(b + 1) * SEQ], ps[:, b, :]).then_inc(s_ytc, 1)
            for n in range(4):
                act.wait_ge(s_vv, n + 1)
                s.copy(vC[:, 4 * n:4 * n + 4, :], ps[:, 4 + n, :].rearrange("p (n d) -> p n d", n=4)).then_inc(s_vvc, 1)
            with act.Fori(0, BATCH) as b:
                act.wait_ge(s_lq, b + 1)
                s.copy(qkC, ps[:, 0:2, :]).then_inc(s_lqc, 1)
                for f in range(2):
                    act.wait_ge(s_fh, b * 2 + (f + 1))
                    s.activation(fr[:, 2 * f:2 * f + 2, :], ps[:, 2 + 2 * f:4 + 2 * f, :], ACT.Relu).then_inc(s_fr, 1)
                for q in range(QT):
                    act.wait_ge(s_lx, b * 4 + (q + 1))
                    s.activation(pC[:, q, 0:P * (q + 1)], score_c(q), ACT.Exp, scale=SCALE_C, bias=small[:, q:q + 1],
                                 accum_out=small[:, 4 + q:5 + q]).then_inc(s_le, 1)
                act.wait_ge(s_lt, b + 1)
                s.copy(pT[:, 0:8, :], ps[:, 2:4, :].rearrange("p b (n t) -> p (b n) t", n=4)).then_inc(s_ltc, 1)
                s.copy(pT[:, 8:10, :], ps[:, 4, 0:256].rearrange("p (n t) -> p n t", n=2)).then_inc(s_ltc, 1)

        @block.tensor
        def _(pe):
            t = nc.tensor
            pe.wait_ge(s_cst, 16)
            pe.wait_ge(s_w, 16 * 7)
            for bank in range(7):
                for n in range(4):
                    m = t.transpose(ps[:, bank, n * P:(n + 1) * P], raw[:, 4 * bank + n, :], ident)
                m.then_inc(s_wt, 1)
            t.transpose(ps[:, 7, 0:3], kg_raw, ident[0:3, 0:3]).then_inc(s_wt, 1)

            def transposed(src, bank, n):
                for q in range(4):
                    m = t.transpose(ps[:, bank, q * P:(q + 1) * P], src[:, 4 * n + q, :], ident)
                return m

            pe.wait_ge(s_nrm, 1)
            pe.wait_ge(s_wtc, 9)
            for n in range(4):
                transposed(acc2, n, n).then_inc(s_xt, 1)
            pe.wait_ge(s_nrm, 2)
            for n in range(4):
                transposed(un, 4 + n, n).then_inc(s_ut, 1)
            pe.wait_ge(s_xtc, BATCH)
            pe.wait_ge(s_ctx, 1)
            for b in range(BATCH):
                m = t.matmul(ps[:, 0, 3 * b:3 * b + 3], ctxb[:, b, :], kgT, start=True, stop=True)
            m.then_inc(s_dyn, 1)
            pe.wait_ge(s_h, BATCH)
            pe.wait_ge(s_utc, BATCH)
            for n in range(8):
                for q in range(2):
                    k = 2 * n + q
                    m = t.matmul(ps[:, n, 256 * q:256 * q + 256], hT[:, k * P:(k + 1) * P], wvT, start=True, stop=True)
                m.then_inc(s_v, 1)
            for n in range(4):
                pe.wait_ge(s_vc, n + 1)
                for q in range(4):
                    k = 4 * n + q
                    m = t.matmul(ps[:, n, P * q:P * q + P], uT[:, k * P:(k + 1) * P], qkv_raw[:, 256:384],
                                 start=True, stop=True)
                m.then_inc(s_v, 1)

            def consumed(use, it):
                kind = use[0]
                if kind in ("SA", "SB", "PA", "PB", "BC"):
                    sema = {"SA": s_eA, "SB": s_eB, "PA": s_maxA, "PB": s_maxB, "BC": s_wts}[kind]
                    m = it + 1 if kind == "PA" else it
                    return sema, m * 8 + (2 * use[1] + use[2] + 1 + (kind == "SB"))
                if kind == "qA":
                    return s_QA, (it + 1) * 2 + (use[1] + 2)
                return {"kA": (s_KAl, it + 2), "qkB": (s_QB, it + 1), "y": (s_acc, it * 2 + 3)}[kind]

            def open_tile(ring, use, it):
                last = ring.before(use)
                if last is not None:
                    pe.wait_ge(*consumed(last, it))
                elif ring.section == "prologue":
                    pe.wait_ge(s_vc, 12)
                else:
                    pe.wait_ge(s_maxA, it * 8 + 8)
                    pe.wait_ge(s_eB, it * 8 + 1)
                    pe.wait_ge(s_acc, it * 2 + 1)
                r = ring.slot(use)
                return ps[:, 2 * r:2 * r + 2, :]

            def project_a(m, ring, sec):
                pe.wait_ge(s_wA, m * 4 + 4)
                b_idx = m // GROUPS
                rhs = hT[:, bass.ds(b_idx * SEQ, SEQ)]
                for p in range(2):
                    tile = open_tile(ring, ("qA", p), sec)
                    for q in range(2):
                        mm = t.matmul(tile[:, q, :], wA[:, 2 * p + q].rearrange("p c e -> p (c e)"), rhs, start=True, stop=True)
                    mm.then_inc(ring_full, 1)
                tile = open_tile(ring, ("kA",), sec)
                t.matmul(tile[:, 0, :], wA[:, HG].rearrange("p c e -> p (c e)"), rhs, start=True, stop=True).then_inc(ring_full, 1)

            def max_scores_a(m, ring, sec, j, h):
                tile = open_tile(ring, ("PA", j, h), sec)
                if h == 0:
                    pe.wait_ge(s_QA, m * 2 + (j // 2 + 2))
                    if j == 0:
                        pe.wait_ge(s_KAh, m + 1)
                for q in range(2):
                    k = 2 * h + q
                    mm = t.matmul(tile[:, q, :], QA[:, j, k * P:(k + 1) * P], KAh[:], start=True, stop=True)
                mm.then_inc(ring_full, 1)

            def shift_rows(src, sema, count, out_sem):
                pe.wait_ge(sema, count)
                for q in range(QT):
                    mm = t.matmul(ps[:, 7, q * P:(q + 1) * P], src[:, q, :], neg_bf[:], start=True, stop=True)
                mm.then_inc(out_sem, 1)

            def body(it, ring, nxt):
                tile = open_tile(ring, ("qkB",), it)
                pe.wait_ge(s_wB, it + 1)
                rhs = uT[:, bass.ds((it // GROUPS) * SEQ, SEQ)]
                for k in range(2):
                    mm = t.matmul(tile[:, k, :], wB[:, k, :], rhs, start=True, stop=True)
                mm.then_inc(ring_full, 1)
                pe.wait_ge(s_shA, it + 1)
                pe.wait_ge(s_KAl, it + 1)

                def chunk_sums(j):
                    if j == 0:
                        pe.wait_ge(s_rB, it + 1)
                    pe.wait_ge(s_eA, it * 8 + (2 * j + 2))
                    for kt in range(KT):
                        mm = t.matmul(ps[32 * j:32 * j + 32, 6, :], cst[:, C_SELL + 32 * kt:C_SELL + 32 * kt + 32],
                                      eA[:, j, kt, :], start=(kt == 0), stop=(kt == KT - 1))
                    if j == HG - 1:
                        mm.then_inc(s_L, 1)

                for use in S1:
                    kind, j, h = use
                    tile = open_tile(ring, use, it)
                    if kind == "SA":
                        for q in range(2):
                            kt = 2 * h + q
                            t.matmul(tile[:, q, :], KAh[:, kt * P:(kt + 1) * P], QA[:, j, :], start=True, stop=False)
                            t.matmul(tile[:, q, :], KAl[:, kt * P:(kt + 1) * P], QA[:, j, :], start=False, stop=False)
                            mm = t.matmul(tile[:, q, :], ones_shift[:, KT * j + kt, :], shiftA[:], start=False, stop=True)
                        mm.then_inc(ring_full, 1)
                        if h == 1 and j > 0:
                            chunk_sums(j - 1)
                    else:
                        if (j, h) == (0, 0):
                            pe.wait_ge(s_QB, it + 1)
                        if h == 0:
                            pe.wait_ge(s_KBj, it * 4 + (j + 1))
                        for q in range(2):
                            k = 2 * h + q
                            mm = t.matmul(tile[:, q, :], QB[:, k * P:(k + 1) * P], KBj[:, j, :], start=True, stop=True)
                        mm.then_inc(ring_full, 1)
                chunk_sums(HG - 1)
                shift_rows(maxB, s_maxB, it * 8 + 8, s_mtB)
                if nxt:
                    project_a(it + 1, ring, it)
                pe.wait_ge(s_sw, it + 1)
                t.matmul(ps[:, 6, :], cst[:, C_BD:C_BD + P], cw[:], start=True, stop=True).then_inc(s_tot, 1)

                def values_b(j):
                    if j == 0:
                        pe.wait_ge(s_te, it + 1)
                        pe.wait_ge(s_VB, it + 1)
                    pe.wait_ge(s_eB, it * 8 + (2 * j + 3))
                    for kt in range(KT):
                        mm = t.matmul(ps[32 * j:32 * j + 32, 6, :], VB[:, kt, j, :], eB[:, j % 2, kt, :],
                                      start=(kt == 0), stop=(kt == KT - 1))
                    if j == HG - 1:
                        mm.then_inc(s_otb, 1)

                def values_a(j):
                    if j == 0:
                        pe.wait_ge(s_QBs, it + 1)
                        pe.wait_ge(s_VA, it + 1)
                    if j == 2:
                        pe.wait_ge(s_oA, it * 2 + 3)
                    pe.wait_ge(s_wts, it * 8 + (2 * j + 2))
                    for kt in range(KT):
                        mm = t.matmul(ps[64 * (j % 2):64 * (j % 2) + 64, 7, :], VA[:, kt, :], eA[:, j, kt, :],
                                      start=(kt == 0), stop=(kt == KT - 1))
                    if j % 2:
                        mm.then_inc(s_ota, 1)

                for use in S3:
                    kind, j, h = use
                    if kind == "PA":
                        if nxt:
                            max_scores_a(it + 1, ring, it, j, h)
                        if h == 1 and j > 0:
                            values_b(j - 1)
                            values_a(j - 1)
                        continue
                    tile = open_tile(ring, use, it)
                    if kind == "BC":
                        if (j, h) == (0, 0):
                            pe.wait_ge(s_cfl, it + 1)
                        for q in range(2):
                            mm = t.matmul(tile[:, q, :], spread[:, KT * j + 2 * h + q, :], cfl[:], start=True, stop=True)
                    else:
                        if (j, h) == (0, 0):
                            pe.wait_ge(s_QBs, it + 1)
                        for q in range(2):
                            kt = 2 * h + q
                            mm = t.matmul(tile[:, q, :], KBj[:, j, kt * P:(kt + 1) * P], QB[:], start=True, stop=True)
                    mm.then_inc(ring_full, 1)
                values_b(HG - 1)
                values_a(HG - 1)
                if nxt:
                    pe.wait_ge(s_oA, it * 2 + 4)
                    shift_rows(maxA, s_maxA, it * 8 + 16, s_mtA)
                pe.wait_ge(s_oB, it + 2)
                t.matmul(ps[:, 6, :], cst[:, C_SELB:C_SELB + P], oB[:], start=True, stop=True).then_inc(s_lb, 1)
                tile = open_tile(ring, ("y",), it)
                g_idx = it % GROUPS
                pe.wait_ge(s_oA, it * 2 + 4)
                for q in range(QT):
                    for p in range(2):
                        t.matmul(tile[:, 0, q * P:(q + 1) * P], oA[:, p, q * P:(q + 1) * P],
                                 woT[:, bass.ds(g_idx * 2 + p, 1), :].rearrange("p n d -> p (n d)"), start=(p == 0), stop=(p == 1))
                pe.wait_ge(s_yB, it + 1)
                for q in range(QT):
                    mm = t.matmul(tile[:, 1, q * P:(q + 1) * P], oB[:, q * P:(q + 1) * P],
                                  wpP[:, bass.ds(g_idx, 1), :].rearrange("p n d -> p (n d)"), start=True, stop=True)
                mm.then_inc(ring_full, 1)

            pe.wait_ge(s_pset, N_PSET)
            pro = Ring("prologue", 0)
            project_a(0, pro, 0)
            for use in PROLOGUE[3:]:
                max_scores_a(0, pro, -1, use[1], use[2])
            shift_rows(maxA, s_maxA, 8, s_mtA)
            pe.wait_ge(s_wpj, 16 * HG)
            with pe.Fori(0, ITERS - 1) as it:
                body(it, Ring("body", it), True)
            body(ITERS - 1, Ring("epilogue", ITERS - 1), False)

            pe.wait_ge(s_nrm, 3)
            for n in range(4):
                transposed(zn, n, n).then_inc(s_zt, 1)
            pe.wait_ge(s_ztc, BATCH)
            for n in range(NT):
                m = t.matmul(ps[:, 4, 8 * n:8 * n + 8], zT[:, n * P:(n + 1) * P], gw[:], start=True, stop=True)
            m.then_inc(s_gl, 1)
            pe.wait_ge(s_hot, 1)
            for _ in range(8):
                t.sem_inc(s_yf, 1)
            with pe.Fori(0, EXPERTS // 2) as i:
                def outputs(n):
                    u, tb = n // BATCH, n % BATCH
                    pe.wait_ge(s_ya, i * 32 + (4 * n + 4))
                    pe.wait_ge(s_hr, i * 16 + (2 * n + 4))
                    pe.wait_ge(s_m2[u], i * 16 + 16)
                    for q in range(QT):
                        for f in range(FB):
                            mm = t.matmul(ps[:, 4 + tb, q * P:(q + 1) * P], hid[:, n % 2, f, q * P:(q + 1) * P],
                                          w2f[:, u, f, :], start=(f == 0), stop=(f == FB - 1))
                    mm.then_inc(s_yf, 1)

                for n in range(8):
                    u, tb = n // BATCH, n % BATCH
                    if tb == 0:
                        pe.wait_ge(s_mh, i * 2 + (u + 1))
                        pe.wait_ge(s_ml, i * 2 + (u + 1))
                    for h in range(2):
                        pe.wait_ge(s_hr, i * 16 + (2 * n + h + 1))
                        for q in range(2):
                            f = 2 * h + q
                            for k, (w, z) in enumerate(((w1h, zH), (w1l, zH), (w1h, zL))):
                                mm = t.matmul(ps[:, f, :], w[:, u, f * P:(f + 1) * P], z[:, tb * SEQ:(tb + 1) * SEQ],
                                              start=(k == 0), stop=(k == 2))
                        mm.then_inc(s_hf, 1)
                    if n:
                        outputs(n - 1)
                outputs(7)

            pe.wait_ge(s_nrm, 4)
            for n in range(4):
                transposed(yn, n, n).then_inc(s_yt, 1)
            pe.wait_ge(s_ytc, BATCH)
            for n in range(4):
                for q in range(4):
                    k = 4 * n + q
                    m = t.matmul(ps[:, 4 + n, P * q:P * q + P], ynT[:, k * P:(k + 1) * P], c_w[:, 2, :], start=True, stop=True)
                m.then_inc(s_vv, 1)
            pe.wait_ge(s_vvc, 4)
            with pe.Fori(0, BATCH) as b:
                rhs = ynT[:, bass.ds(b * SEQ, SEQ)]
                pe.wait_ge(s_fin, b + 1)
                for k in range(2):
                    mm = t.matmul(ps[:, k, :], c_w[:, k, :], rhs, start=True, stop=True)
                mm.then_inc(s_lq, 1)
                for f in range(FB):
                    mm = t.matmul(ps[:, 2 + f, :], wfcT[:, f * P:(f + 1) * P], rhs, start=True, stop=True)
                    if f % 2:
                        mm.then_inc(s_fh, 1)
                pe.wait_ge(s_lqc, b + 1)
                pe.wait_ge(s_fr, b * 2 + 2)
                for q in range(QT):
                    t.matmul(score_c(q), qkC[:, 0, q * P:(q + 1) * P], qkC[:, 1, 0:P * (q + 1)], start=True,
                             stop=True).then_inc(s_ls, 1)
                pe.wait_ge(s_fs, b * 2 + 2)
                for q in range(QT):
                    for f in range(FB):
                        mm = t.matmul(ps[:, 6, q * P:(q + 1) * P], fr[:, f, q * P:(q + 1) * P], wpjT[:, f, :],
                                      start=(f == 0), stop=(f == FB - 1))
                mm.then_inc(s_fy, 1)
                n = 0
                for q in range(QT):
                    pe.wait_ge(s_le, b * 4 + (q + 1))
                    for k in range(q + 1):
                        mm = t.transpose(ps[:, 2 + n // 4, (n % 4) * P:(n % 4 + 1) * P], pC[:, q, k * P:(k + 1) * P], ident)
                        n += 1
                mm.then_inc(s_lt, 1)
                pe.wait_ge(s_ltc, b * 2 + 2)
                n = 0
                for q in range(QT):
                    for k in range(q + 1):
                        mm = t.matmul(ps[:, 5, q * P:(q + 1) * P], pT[:, n, :],
                                      vC[:, bass.ds(b * QT + k, 1), :].rearrange("p n d -> p (n d)"), start=(k == 0), stop=(k == q))
                        n += 1
                mm.then_inc(s_lo, 1)

        @block.vector
        def _(dve):
            v = nc.vector
            chain = [0]

            def link(ins):
                chain[0] += 1
                ins.then_inc(s_chain, 1)
                dve.wait_ge(s_chain, chain[0])

            def layer_norm(n, src, xc, sq, dst):
                link(v.tensor_reduce(small[:, 0:NT], src, AX_X, ALU.add))
                link(v.tensor_scalar(small[:, MEAN:MEAN + NT], small[:, 0:NT], 1.0 / D, None, ALU.mult))
                v.tensor_tensor(xc, src, per_tile(MEAN), ALU.subtract).then_inc(s_cen, 1)
                dve.wait_ge(s_sqd, n + 1)
                link(v.tensor_reduce(small[:, 0:NT], sq, AX_X, ALU.add))
                v.tensor_scalar(small[:, VAR:VAR + NT], small[:, 0:NT], 1.0 / D, EPS, ALU.mult, ALU.add).then_inc(s_var, 1)
                dve.wait_ge(s_std, n + 1)
                link(v.reciprocal(small[:, RSTD:RSTD + NT], small[:, STD:STD + NT]))
                dve.wait_ge(s_cen, n + 1)
                v.tensor_tensor(dst, xc, per_tile(RSTD), ALU.mult).then_inc(s_nrm, 1)
                dve.wait_ge(s_nrm, n + 1)

            dve.wait_ge(s_x, 16 * BATCH)
            layer_norm(0, acc1[:], xc, sq, acc2[:])
            layer_norm(1, acc2[:], xc, sq, un)
            dve.wait_ge(s_xtc, BATCH)
            link(v.tensor_reduce(small[:, CTX:CTX + BATCH], xnT, AX_X, ALU.add))
            v.tensor_scalar(ctxb, small[:, CTX:CTX + BATCH].unsqueeze(2).broadcast_to([P, BATCH, P]), 1.0 / SEQ, None,
                            ALU.mult).then_inc(s_ctx, 1)
            dve.wait_ge(s_col, 16 * N_COLS)
            link(v.tensor_scalar(cacc, xnT, cols[:, 1:2], None, ALU.mult))
            link(v.scalar_tensor_tensor(cacc[:, :, 1:SEQ], xnT[:, :, 0:SEQ - 1], cols[:, 0:1], cacc[:, :, 1:SEQ],
                                        ALU.mult, ALU.add))
            link(v.scalar_tensor_tensor(cacc[:, :, 0:SEQ - 1], xnT[:, :, 1:SEQ], cols[:, 2:3], cacc[:, :, 0:SEQ - 1],
                                        ALU.mult, ALU.add))
            dve.wait_ge(s_dyn, 1)
            dyn = small[:, DYN:DYN + 12].rearrange("p (b k) -> p b k", k=3)
            v.tensor_tensor(dyn, ps[:, 0, 0:12].rearrange("p (b k) -> p b k", k=3),
                            kgb[:].unsqueeze(1).broadcast_to([P, BATCH, 3]), ALU.add).then_inc(s_z, 1)
            dve.wait_ge(s_ez, 1)
            link(v.tensor_scalar(dyn, dyn, 1.0, None, ALU.add))
            link(v.reciprocal(dyn, dyn))
            link(v.tensor_reduce(small[:, GATE:GATE + BATCH], dyn, AX_X, ALU.add))
            link(v.tensor_scalar(small[:, GATE:GATE + BATCH], small[:, GATE:GATE + BATCH], 1.0 / 3.0, None, ALU.mult))
            for b in range(BATCH):
                v.tensor_scalar(hT[:, b * SEQ:(b + 1) * SEQ], cacc[:, b, :], cols[:, 3:4],
                                small[:, GATE + b:GATE + b + 1], ALU.add, ALU.mult).then_inc(s_h, 1)
            v.sem_inc(s_QA, 1)
            v.sem_inc(s_rB, 1)
            v.sem_inc(s_acc, 1)

            def tile(ring, use):
                r = ring.slot(use)
                return ps[:, 2 * r:2 * r + 2, :]

            def split_next(m, ring):
                for p in range(2):
                    dve.wait_ge(s_HA, m * 2 + (p + 1))
                    v.scalar_tensor_tensor(QA[:, 2 * p:2 * p + 2, :], HA[:].bitcast(F32), col(0), tile(ring, ("qA", p)),
                                           ALU.mult, ALU.add).then_inc(s_QA, 1)
                dve.wait_ge(s_KAh, m + 1)
                v.tensor_tensor(KAl[:], tile(ring, ("kA",))[:, 0, :], KAh[:].bitcast(F32), ALU.subtract).then_inc(s_KAl, 1)

            def max_a(m, ring, j, h):
                use = ("PA", j, h)
                dve.wait_ge(ring_full, ring.filled(use))
                v.tensor_reduce(maxA[:, 2 * h:2 * h + 2, 32 * j:32 * j + NCH],
                                tile(ring, use).rearrange("p q (c k) -> p q c k", c=NCH), AX_X, ALU.max).then_inc(s_maxA, 1)

            def body(it, ring, nxt):
                dve.wait_ge(s_HB, it + 1)
                t = tile(ring, ("qkB",))
                v.scalar_tensor_tensor(KB[:], HB[:, 1, :].bitcast(F32), col(2), t[:, 1, :], ALU.mult, ALU.add).then_inc(s_KB, 1)
                v.scalar_tensor_tensor(QB[:], HB[:, 0, :].bitcast(F32), col(1), t[:, 0, :], ALU.mult, ALU.add).then_inc(s_QB, 1)
                for use in S1:
                    if use[0] == "PB":
                        _, j, h = use
                        dve.wait_ge(ring_full, ring.filled(use))
                        v.tensor_reduce(maxB[:, 2 * h:2 * h + 2, 32 * j:32 * j + 1], tile(ring, use), AX_X,
                                        ALU.max).then_inc(s_maxB, 1)
                dve.wait_ge(s_L, it + 1)
                v.reciprocal(cr[:], ps[:, 6, :]).then_inc(s_r, 1)
                dve.wait_ge(s_r, it + 1)
                v.tensor_tensor(cw[:], ps[:, 6, :], cr[:], ALU.mult).then_inc(s_sw, 1)
                dve.wait_ge(s_mtB, it + 1)
                v.tensor_tensor(QB[:], QB[:].bitcast(F32), ps[:, 7, :], ALU.add).then_inc(s_QBs, 1)
                if nxt:
                    split_next(it + 1, ring)
                dve.wait_ge(s_tot, it + 1)
                v.tensor_scalar(ct[:], ps[:, 6, :], 1e-9, None, ALU.add).then_inc(s_te, 1)
                dve.wait_ge(s_te, it + 1)
                v.reciprocal(ct[:], ct[:]).then_inc(s_rt, 1)
                dve.wait_ge(s_rt, it + 1)
                dve.wait_ge(s_c1, it + 1)
                v.tensor_tensor(cf[:], cr[:], ct[:], ALU.mult).then_inc(s_cf, 1)
                dve.wait_ge(s_cfh, it + 1)
                v.scalar_tensor_tensor(cfl[:], cfh[:].bitcast(F32), col(3), cf[:], ALU.mult, ALU.add).then_inc(s_cfl, 1)
                for use in S3:
                    kind, j, h = use
                    if kind == "BC":
                        dve.wait_ge(ring_full, ring.filled(use))
                        e = eA[:, j, 2 * h:2 * h + 2, :]
                        v.tensor_tensor(e, e, tile(ring, use), ALU.mult).then_inc(s_wts, 1)
                    elif kind == "PA" and nxt:
                        max_a(it + 1, ring, j, h)
                dve.wait_ge(s_lb, it + 1)
                v.reciprocal(rB[:], ps[:, 6, :]).then_inc(s_rB, 1)
                dve.wait_ge(s_rB, it + 2)
                v.tensor_tensor(oB[:], oB[:], rB[:], ALU.mult).then_inc(s_yB, 1)
                dve.wait_ge(ring_full, ring.filled(("y",)))
                dve.wait_ge(s_acc, it * 2 + 1)
                for k, acc in enumerate((acc1, acc2)):
                    a = acc[:, bass.ds((it // GROUPS) * QT, QT), :]
                    y = tile(ring, ("y",))[:, k, :].rearrange("p (q d) -> p q d", q=QT)
                    v.tensor_tensor(a, a, y, ALU.add).then_inc(s_acc, 1)

            pro = Ring("prologue", 0)
            split_next(0, pro)
            for use in PROLOGUE[3:]:
                max_a(0, pro, use[1], use[2])
            with dve.Fori(0, ITERS - 1) as it:
                body(it, Ring("body", it), True)
            body(ITERS - 1, Ring("epilogue", ITERS - 1), False)

            dve.wait_ge(s_acc, 2 * ITERS + 1)
            layer_norm(2, acc2[:], zn, zsq, zn)
            v.tensor_tensor(acc1[:], acc1[:], acc2[:], ALU.add).then_inc(s_ya, 1)
            dve.wait_ge(s_zh, 1)
            v.tensor_tensor(zL, zT, zH.bitcast(F32), ALU.subtract).then_inc(s_zl, 1)
            dve.wait_ge(s_gl, 1)
            link(v.tensor_tensor(lg[:], ps[:, 4, 0:NT * EXPERTS].rearrange("p (n e) -> p n e", n=NT),
                                 gb[:].unsqueeze(1).broadcast_to([P, NT, EXPERTS]), ALU.add))
            link(v.tensor_reduce(small[:, 0:NT], lg[:], AX_X, ALU.max))
            per_expert = small[:, 0:NT].unsqueeze(2).broadcast_to([P, NT, EXPERTS])
            link(v.tensor_tensor(lge[:], lg[:], per_expert, ALU.is_equal))
            link(v.tensor_tensor(lge[:], lge[:], cst[:, C_COL + 12:C_COL + 12 + EXPERTS].unsqueeze(1)
                                 .broadcast_to([P, NT, EXPERTS]), ALU.mult))
            link(v.tensor_reduce(small[:, 0:NT], lge[:], AX_X, ALU.max))
            v.tensor_tensor(hot[:].rearrange("p e n -> p n e"), lge[:], per_expert, ALU.is_equal).then_inc(s_hot, 1)
            dve.wait_ge(s_hot, 1)
            for _ in range(15):
                v.sem_inc(s_ya, 1)
            with dve.Fori(0, EXPERTS // 2) as i:
                def low_parts(u):
                    dve.wait_ge(s_mh, i * 2 + (u + 1))
                    v.tensor_tensor(w1l[:, u, :], w1f[:, u, :], w1h[:, u, :].bitcast(F32), ALU.subtract).then_inc(s_ml, 1)

                low_parts(0)
                for n in range(2 * BATCH):
                    u, tb = n // BATCH, n % BATCH
                    if n == 2:
                        low_parts(1)
                    dve.wait_ge(s_yf, i * 8 + (n + 9))
                    dve.wait_ge(s_ya, i * 32 + (4 * n + 16))
                    for q in range(QT):
                        k = tb * QT + q
                        v.scalar_tensor_tensor(acc1[:, k, :], ps[:, 4 + tb, q * P:(q + 1) * P],
                                               hot[:, bass.ds(i * 2 + u, 1), k:k + 1].rearrange("p e n -> p (e n)"),
                                               acc1[:, k, :], ALU.mult, ALU.add).then_inc(s_ya, 1)

            dve.wait_ge(s_ya, 16 + 4 * BATCH * EXPERTS)
            layer_norm(3, acc1[:], yn, ynsq, yn)
            v.sem_inc(s_fin, 1)
            LX, LL = 0, 4
            mem, tmp, spk, cnt = (lif[:, 512 * n:512 * n + 512] for n in range(4))
            with dve.Fori(0, BATCH) as b:
                for f in range(2):
                    dve.wait_ge(s_fr, b * 2 + (f + 1))
                    h = fr[:, 2 * f:2 * f + 2, :]
                    v.tensor_tensor(h, h, h, ALU.mult).then_inc(s_fs, 1)
                for q in range(QT):
                    dve.wait_ge(s_ls, b * 4 + (q + 1))
                    sc = score_c(q)
                    dg = sc[:, q * P:(q + 1) * P]
                    v.tensor_tensor(dg, dg, cst[:, C_CAUSAL:C_CAUSAL + P], ALU.add).then_inc(s_lm, 1)
                    dve.wait_ge(s_lm, b * 8 + (2 * q + 1))
                    v.tensor_reduce(small[:, 8 + q:9 + q], sc, AX_X, ALU.max).then_inc(s_lm, 1)
                    dve.wait_ge(s_lm, b * 8 + (2 * q + 2))
                    v.tensor_scalar(small[:, LX + q:LX + q + 1], small[:, 8 + q:9 + q], -SCALE_C, None, ALU.mult).then_inc(s_lx, 1)
                dve.wait_ge(s_fy, b + 1)
                y = ps[:, 6, :]
                seq = [0]
                STEPS = 3 + 4 * 4

                def spike(ins):
                    seq[0] += 1
                    ins.then_inc(s_sp, 1)
                    dve.wait_ge(s_sp, b * STEPS + seq[0])

                spike(v.tensor_copy(mem, y))
                spike(v.tensor_scalar(spk, mem, 1.0, None, ALU.is_gt))
                spike(v.tensor_copy(cnt, spk))
                for _ in range(4):
                    spike(v.scalar_tensor_tensor(tmp, mem, 0.9, y, ALU.mult, ALU.add))
                    spike(v.tensor_tensor(mem, tmp, spk, ALU.subtract))
                    spike(v.tensor_scalar(spk, mem, 1.0, None, ALU.is_gt))
                    spike(v.tensor_tensor(cnt, cnt, spk, ALU.add))
                dve.wait_ge(s_le, b * 4 + 4)
                v.reciprocal(small[:, 12:16], small[:, LL:LL + 4]).then_inc(s_loa, 1)
                dve.wait_ge(s_loa, b * 6 + 1)
                a = acc1[:, bass.ds(b * QT, QT), :]
                v.scalar_tensor_tensor(a, cnt.rearrange("p (q d) -> p q d", q=QT), 0.2, a, ALU.mult, ALU.add).then_inc(s_loa, 1)
                dve.wait_ge(s_loa, b * 6 + 2)
                dve.wait_ge(s_lo, b + 1)
                for q in range(QT):
                    a = acc1[:, bass.ds(b * QT + q, 1), :].rearrange("p n d -> p (n d)")
                    ins = v.scalar_tensor_tensor(a, ps[:, 5, q * P:(q + 1) * P], small[:, 12 + q:13 + q], a, ALU.mult, ALU.add)
                    ins.then_inc(s_fin if q == QT - 1 else s_loa, 1)
                dve.wait_ge(s_loa, b * 6 + 5)
                v.tensor_copy(small[:, 140:141], small[:, 12:13]).then_inc(s_loa, 1)


_INS = ['L0_attn_hidden_states', 'L0_attn_w_q', 'L0_attn_w_k', 'L0_attn_w_v', 'L0_attn_w_o', 'L0_attn_w_kgen',
        'L0_attn_b_kgen', 'L0_attn_w_conv', 'L0_attn_b_conv', 'L0_ffn_ln1_w', 'L0_ffn_ln1_b', 'L0_ffn_w_qkv',
        'L0_ffn_w_proj', 'L0_ffn_ln2_w', 'L0_ffn_ln2_b', 'L0_ffn_gate_w', 'L0_ffn_gate_b', 'L0_ffn_w1', 'L0_ffn_w2',
        'L1_attn_WQ', 'L1_attn_WK', 'L1_attn_WV', 'L1_ffn_W_fc', 'L1_ffn_W_proj']
_OUTS = [((4, 512, 128), 'float32')]


def kernel(**inputs):
    import numpy as _np
    import concourse.bacc as _bacc
    from concourse import mybir as _mybir
    from concourse.bass_utils import run_bass_kernel_spmd as _run

    nc = _bacc.Bacc("TRN2", target_bir_lowering=False, num_devices=1)
    arrays, args = {}, []
    named = [(name, _np.ascontiguousarray(inputs[name])) for name in _INS] + [("constants", constant_columns())]
    for name, a in named:
        arrays[f"in_{name}_dram"] = a
        args.append(nc.dram_tensor(f"in_{name}_dram", a.shape, _mybir.dt.from_np(a.dtype), kind="ExternalInput").ap())
    for i, (shape, dtype) in enumerate(_OUTS):
        dt = _mybir.dt.from_np(_np.dtype(dtype))
        args.append(nc.dram_tensor(f"out_{i}_dram", shape, dt, kind="ExternalOutput").ap())
    build(nc, *args)
    r = _run(nc, [arrays], core_ids=[0])
    return r.results[0]["out_0_dram"]
```

```python
from contextlib import ExitStack

import numpy as np

import concourse.bass as bass
from concourse import mybir

F32 = mybir.dt.float32
F32R = mybir.dt.float32r
BF16 = mybir.dt.bfloat16
ALU = mybir.AluOpType
ACT = mybir.ActivationFunctionType
AX_X = mybir.AxisListType.X

P = 128
BATCH, SEQ, D = 4, 512, 128
NT = BATCH * SEQ // P
QT = SEQ // P
KT = SEQ // P
GROUPS = 4
HG = 4
HDA = 64
CH = 64
NCH = SEQ // CH
HDB = 8
ITERS = BATCH * GROUPS
EXPERTS, FF = 8, 512
FB = FF // P
EPS = 1e-5
SCALE_A = HDA ** -0.5
SCALE_B = float(1.0 / np.sqrt(HDB))
SCALE_C = float(1.0 / np.sqrt(D))

C_ID, C_NEG, C_SELB, C_BD, C_SELL, C_CAUSAL, C_COL = 0, 128, 256, 384, 512, 640, 768
C_N = 768 + 24


def constant_columns():
    c = np.zeros((P, C_N), np.float32)
    r = np.arange(P)
    c[:, C_ID:C_ID + P] = np.eye(P)
    c[:, C_NEG:C_NEG + P] = -np.eye(P)
    c[:, C_SELB:C_SELB + P] = r[:, None] == 32 * (r[None, :] // 32) + 8
    c[:, C_BD:C_BD + P] = (r[:, None] // 32 == r[None, :] // 32) & (r[:, None] % 32 < NCH)
    for kt in range(KT):
        m = np.arange(32)
        c[:, C_SELL + 32 * kt:C_SELL + 32 * kt + 32] = (m[None, :] % NCH) == (2 * kt + r[:, None] // CH)
    c[:, C_CAUSAL:C_CAUSAL + P] = np.where(r[None, :] > r[:, None], -1e30, 0.0)
    k = C_COL
    c[:, k] = -1.0 * (r >= 64)
    c[:, k + 1] = -1.0 * ((r % 32 >= 9) & (r % 32 < 17))
    c[:, k + 2] = -1.0 * ((r % 32 >= 17) & (r % 32 < 25))
    c[:, k + 3] = -1.0 * ((r % 32 >= 8) & (r % 32 < 16))
    for j in range(HG):
        c[:, k + 4 + j] = r // 32 == j
        c[:, k + 8 + j] = r == 32 * j
    c[:, k + 20] = 1e-9
    c[:, k + 12:k + 12 + EXPERTS] = EXPERTS - np.arange(EXPERTS)
    return c


STEPS = [
    ("SA", 0, 0), ("SA", 0, 1), ("SA", 1, 0), ("PB", 0, 0), ("SA", 1, 1), ("PB", 0, 1), ("SA", 2, 0), ("PB", 1, 0),
    ("SA", 2, 1), ("PB", 1, 1), ("SA", 3, 0), ("PB", 2, 0), ("SA", 3, 1), ("PB", 2, 1), ("PB", 3, 0), ("PB", 3, 1),
    ("qA", 0), ("L",), ("r",), ("cw",), ("mB",), ("qA", 1), ("TOT",), ("kA",), ("ct",),
    ("SB", 0, 0), ("SB", 1, 0), ("cf",), ("cfh",), ("SB", 2, 0), ("cfl",), ("SB", 3, 0), ("PA", 0, 0), ("PA", 0, 1),
    ("VB", 0), ("PA", 1, 0), ("SB", 0, 1), ("PA", 1, 1), ("SB", 1, 1), ("BC", 0, 0), ("SB", 2, 1), ("BC", 0, 1),
    ("SB", 3, 1), ("PA", 2, 0), ("VB", 1), ("BC", 1, 0), ("PA", 2, 1), ("BC", 1, 1), ("LB",), ("PA", 3, 0),
    ("PA", 3, 1), ("BC", 2, 0), ("VA", 0), ("BC", 2, 1), ("mA", 0), ("BC", 3, 0), ("BC", 3, 1), ("mA", 1), ("yB",),
    ("VA", 1), ("qkB",), ("yA",)]
FILLS = ("SA", "PB", "BC", "SB", "yA", "yB", "qA", "kA", "qkB", "PA", "mA")
NEXT = ("qA", "kA", "qkB", "PA", "mA")
PRO_STEPS = [u for u in STEPS if u[0] in NEXT]
EPI_STEPS = [u for u in STEPS if u[0] not in NEXT]
PROLOGUE, BODY, EPILOGUE = ([u for u in steps if u[0] in FILLS] for steps in (PRO_STEPS, STEPS, EPI_STEPS))
N_PRO, N_BODY = len(PROLOGUE), len(BODY)
SLOTS = 3
assert N_BODY % SLOTS == 0
assert BODY[-3:] == [("yB",), ("qkB",), ("yA",)] and PROLOGUE[-3:] == [("mA", 0), ("mA", 1), ("qkB",)]


class Ring:

    def __init__(self, section, it):
        self.order, first = {"prologue": (PROLOGUE, 0), "body": (BODY, N_PRO),
                             "epilogue": (EPILOGUE, N_PRO + N_BODY * (ITERS - 1))}[section]
        self.place = {u: first + n for n, u in enumerate(self.order)}
        self.it = it
        self.section = section

    def slot(self, use):
        return self.place[use] % SLOTS

    def before(self, use):
        n = self.order.index(use)
        return self.order[n - SLOTS] if n >= SLOTS else None

    def filled(self, use):
        n = self.place[use] + 1
        return self.it * N_BODY + n if self.section == "body" else n


def build(nc, x, w_q, w_k, w_v, w_o, w_kgen, b_kgen, w_conv, b_conv, ln1_w, ln1_b, w_qkv, w_proj,
          ln2_w, ln2_b, gate_w, gate_b, w1, w2, c_wq, c_wk, c_wv, w_fc, w_pj, consts, out):
    with ExitStack() as ctx:
        def sb(name, shape, dt=F32):
            return ctx.enter_context(nc.sbuf_tensor(name, shape, dt))

        def sem(name):
            return ctx.enter_context(nc.semaphore(name))

        cst = sb("cst", [P, C_N])
        spread = sb("spread", [P, HG * KT, P], F32R)
        neg_bf = sb("neg_bf", [P, P], BF16)
        acc1 = sb("acc1", [P, NT, D])
        acc2 = sb("acc2", [P, NT, D])
        hT = sb("hT", [P, BATCH * SEQ])
        uT = sb("uT", [P, BATCH * SEQ])
        wqT = sb("wqT", [P, GROUPS, HG, HDA])
        wkT = sb("wkT", [P, GROUPS, HDA])
        w2all = sb("w2all", [P, GROUPS, 2, P])
        wA = sb("wA", [P, HG + 1, 2, HDA])
        wB = sb("wB", [P, 2, P])
        woT = sb("woT", [P, 2 * GROUPS, D])
        wpP = sb("wpP", [P, GROUPS, D])
        v_all = sb("v_all", [P, NT, GROUPS, HDA])
        vb_all = sb("vb_all", [P, NT, GROUPS * HG, HDB])
        QA = sb("QA", [P, HG, SEQ], F32R)
        QS = sb("QS", [P, HG, SEQ], F32R)
        KAh = sb("KAh", [P, SEQ], F32R)
        KS = sb("KS", [P, SEQ], F32R)
        QB = sb("QB", [P, SEQ], F32R)
        KB = sb("KB", [P, SEQ], F32R)
        HB = sb("HB", [P, 2, SEQ], F32R)
        KBj = sb("KBj", [P, HG, SEQ], F32R)
        VA = sb("VA", [P, KT, HDA])
        VB = sb("VB", [P, KT, HG, 32])
        eA = sb("eA", [P, HG, KT, SEQ])
        eB = sb("eB", [P, HG, 2, SEQ])
        maxA = sb("maxA", [P, QT, HG, P], BF16)
        maxB = sb("maxB", [P, QT, P], BF16)
        cr = sb("cr", [P, SEQ])
        cw = sb("cw", [P, SEQ])
        ct = sb("ct", [P, SEQ])
        cf = sb("cf", [P, SEQ])
        cfh = sb("cfh", [P, SEQ], F32R)
        cfl = sb("cfl", [P, SEQ], F32R)
        oB = sb("oB", [P, SEQ])
        rB = sb("rB", [P, SEQ])
        oA = sb("oA", [P, 2, SEQ])
        small = sb("small", [P, 160])
        wfcT = sb("wfcT", [P, FF])
        wpjT = sb("wpjT", [P, FB, D])
        cols = sb("cols", [P, 16])
        kgb = sb("kgb", [P, 3])
        gb = sb("gb", [P, EXPERTS])
        gw = sb("gw", [P, EXPERTS])
        c_w = sb("c_w", [P, 3, D])
        ps = ctx.enter_context(nc.psum_tensor("ps", [P, 8, 512], F32))

        ident = cst[:, C_ID:C_ID + P]

        def col(n):
            return cst[:, C_COL + n:C_COL + n + 1]

        eAf = eA[:].rearrange("p a b c -> p (a b c)")
        eBf = eB[:].rearrange("p a b c -> p (a b c)")
        raw = eBf[:, 0:28 * P].rearrange("p (n d) -> p n d", d=D)
        qkv_raw = eBf[:, 28 * P:31 * P]
        kg_raw = eBf[0:3, 31 * P:32 * P]
        xc = eAf[:, 0:2048].rearrange("p (n d) -> p n d", d=D)
        sq = eAf[:, 2048:4096].rearrange("p (n d) -> p n d", d=D)
        xnT = eAf[:, 4096:6144].rearrange("p (b s) -> p b s", b=BATCH)
        wvT = eAf[:, 6144:6400]
        kgT = eAf[:, 6400:6403]
        ctxb = eAf[:, 6528:7040].rearrange("p (b m) -> p b m", b=BATCH)
        un = sq
        cacc = eAf[:, 0:2048].rearrange("p (b s) -> p b s", b=BATCH)

        s_cst = sem("constants_loaded")
        s_x = sem("x_loaded")
        s_w = sem("weights_loaded")
        s_qkv = sem("qkv_loaded")
        s_col = sem("columns_loaded")
        s_wpj = sem("wproj_loaded")
        s_chain = sem("vector_chain")
        s_pset = sem("gpsimd_constants")
        s_wt = sem("weights_transposed")
        s_wtc = sem("weights_copied")
        s_cen = sem("centred")
        s_sqd = sem("squared")
        s_var = sem("variance")
        s_std = sem("deviation")
        s_nrm = sem("normalised")
        s_xt = sem("xn_transposed")
        s_xtc = sem("xn_copied")
        s_ut = sem("ln1_transposed")
        s_utc = sem("ln1_copied")
        s_ctx = sem("context_ready")
        s_dyn = sem("gate_filled")
        s_z = sem("gate_argument")
        s_ez = sem("gate_exponential")
        s_h = sem("conv_ready")
        s_v = sem("values_filled")
        s_vc = sem("values_copied")
        s_zt = sem("ln2_transposed")
        s_ztc = sem("ln2_copied")
        s_zh = sem("ln2_high")
        s_zl = sem("ln2_low")
        s_gl = sem("gate_logits_filled")
        s_hot = sem("one_hot_ready")
        s_yt = sem("norm2_transposed")
        s_ytc = sem("norm2_copied")
        s_vv = sem("L1_values_filled")
        s_vvc = sem("L1_values_copied")

        ring_full = sem("score_tile_filled")
        s_wA = sem("wA_ready")
        s_wB = sem("wB_ready")
        s_VA = sem("VA_ready")
        s_VB = sem("VB_ready")
        s_QS = sem("QS_high_ready")
        s_KAh = sem("KAh_ready")
        s_QA = sem("QA_ready")
        s_KS = sem("KS_ready")
        s_HB = sem("HB_rounded")
        s_KB = sem("KB_ready")
        s_QB = sem("QB_ready")
        s_KBj = sem("KBj_ready")
        s_maxA = sem("maxA_taken")
        s_maxB = sem("maxB_taken")
        s_shA = sem("shiftA_ready")
        s_mtB = sem("shiftB_filled")
        s_QBs = sem("QB_shifted")
        s_eA = sem("eA_ready")
        s_eB = sem("eB_ready")
        s_L = sem("chunk_sums_filled")
        s_ln = sem("logarithm_ready")
        s_r = sem("chunk_reciprocal")
        s_sw = sem("chunk_weight_sum")
        s_tot = sem("total_filled")
        s_c1 = sem("factor_times_sum")
        s_rt = sem("total_reciprocal")
        s_cf = sem("factor_ready")
        s_cfh = sem("factor_high")
        s_cfl = sem("factor_low")
        s_wts = sem("eA_weighted")
        s_ota = sem("outA_filled")
        s_otb = sem("outB_filled")
        s_oA = sem("outA_copied")
        s_oB = sem("outB_copied")
        s_lb = sem("outB_sums_filled")
        s_rB = sem("outB_reciprocal")
        s_yB = sem("outB_scaled")
        s_acc = sem("outputs_added")

        s_m1 = [sem(f"expert_w1_loaded{u}") for u in range(2)]
        s_m2 = [sem(f"expert_w2_loaded{u}") for u in range(2)]
        s_mh = sem("expert_w1_high")
        s_ml = sem("expert_w1_low")
        s_hf = sem("expert_hidden_filled")
        s_hr = sem("expert_hidden_ready")
        s_yf = sem("expert_out_filled")
        s_ya = sem("expert_out_added")

        s_lq = sem("L1_qk_filled")
        s_lqc = sem("L1_qk_copied")
        s_ls = sem("L1_scores_filled")
        s_lm = sem("L1_scores_masked")
        s_lx = sem("L1_max_negated")
        s_le = sem("L1_exp_ready")
        s_lt = sem("L1_transposed")
        s_ltc = sem("L1_transposed_copied")
        s_lo = sem("L1_out_filled")
        s_loa = sem("L1_out_added")
        s_fh = sem("ffn_hidden_filled")
        s_fr = sem("ffn_relu_ready")
        s_fs = sem("ffn_square_ready")
        s_fy = sem("ffn_out_filled")
        s_ff = sem("ffn_bank_free")
        s_sp = sem("spike_step")
        s_fin = sem("batch_finished")
        s_out = sem("stored")

        block = ctx.enter_context(nc.Block())

        w1f = eAf[:, 0:1024].rearrange("p (u f) -> p u f", u=2)
        w2f = eAf[:, 1024:2048].rearrange("p (u n d) -> p u n d", u=2, n=FB)
        hid = eAf[:, 2048:6144].rearrange("p (u n t) -> p u n t", u=2, n=FB)
        zn = eBf[:, 0:2048].rearrange("p (n d) -> p n d", d=D)
        zT = eBf[:, 2048:4096]
        zsq = hT[:].rearrange("p (n d) -> p n d", d=D)
        zH = QA[:].rearrange("p a b -> p (a b)")
        zL = KBj[:].rearrange("p a b -> p (a b)")
        spr = spread[:].rearrange("p a b -> p (a b)")
        w1h = spr[:, 0:1024].rearrange("p (u f) -> p u f", u=2)
        w1l = spr[:, 1024:2048].rearrange("p (u f) -> p u f", u=2)
        hot = sb("hot", [P, EXPERTS, NT])
        lg = sb("lg", [P, NT, EXPERTS])
        lge = sb("lge", [P, NT, EXPERTS])
        yn = eAf[:, 0:2048].rearrange("p (n d) -> p n d", d=D)
        ynsq = eAf[:, 2048:4096].rearrange("p (n d) -> p n d", d=D)
        ynT = eAf[:, 4096:6144]
        vC = eAf[:, 6144:8192].rearrange("p (n d) -> p n d", d=D)
        qkC = eBf[:, 0:1024].rearrange("p (u t) -> p u t", u=2)
        pC = eBf[:, 1024:3072].rearrange("p (q t) -> p q t", q=QT)
        pT = hT[:, 0:1280].rearrange("p (n t) -> p n t", n=10)
        fr = uT[:].rearrange("p (n t) -> p n t", n=FB)
        lif = v_all[:].rearrange("p a b c -> p (a b c)")
        t3 = vb_all[:].rearrange("p a b c -> p (a b c)")


        MEAN, VAR, STD, RSTD, CTX, DYN, GATE = 16, 32, 48, 64, 80, 96, 128

        def per_tile(c):
            return small[:, c:c + NT].unsqueeze(2).broadcast_to([P, NT, D])

        def score_c(q):
            return ps[:, (5, 7, 0, 1)[q], 0:P * (q + 1)]

        x_v = x.rearrange("b (n p) d -> p (b n) d", p=P)
        out_v = out.rearrange("b (n p) d -> b p n d", p=P)
        N_COLS = 12
        N_PSET = 5 + 3 + 2 * 3 * GROUPS

        @block.sync
        def _(sp):
            for b in range(BATCH):
                sp.dma_start(acc1[:, b * QT:(b + 1) * QT, :], x_v[:, b * QT:(b + 1) * QT, :]).then_inc(s_x, 16)
            sp.dma_start(raw[:, 0:8, :], w_q.rearrange("(n p) d -> p n d", p=P)).then_inc(s_w, 16)
            sp.dma_start(raw[:, 8:10, :], w_k.rearrange("(n p) d -> p n d", p=P)).then_inc(s_w, 16)
            sp.dma_start(raw[:, 10:12, :], w_v.rearrange("(n p) d -> p n d", p=P)).then_inc(s_w, 16)
            sp.dma_start(raw[:, 12:20, :], w_o.rearrange("o (n d) -> o n d", d=P)).then_inc(s_w, 16)
            sp.dma_start(raw[:, 20:24, :], w_fc.rearrange("(n p) d -> p n d", p=P)).then_inc(s_w, 16)
            sp.dma_start(raw[:, 24:28, :], w_pj.rearrange("o (n d) -> o n d", d=P)).then_inc(s_w, 16)
            sp.dma_start(kg_raw, w_kgen).then_inc(s_w, 16)

            for u in range(2):
                if u == 0:
                    sp.wait_ge(s_acc, 2 * ITERS + 2)
                sp.dma_start(w1f[:, u, :], w1[u]).then_inc(s_m1[u], 16)
                sp.dma_start(w2f[:, u], w2[u].rearrange("(n p) d -> p n d", p=P)).then_inc(s_m2[u], 16)
            w1_p = w1.rearrange("(i u) d f -> i u d f", u=2)
            w2_p = w2.rearrange("(i u) (n p) d -> i u p n d", u=2, p=P)
            with sp.Fori(1, EXPERTS // 2) as i:
                for u in range(2):
                    sp.wait_ge(s_yf, i * 8 + (4 * u + 4))
                    sp.dma_start(w1f[:, u, :], w1_p[i, u]).then_inc(s_m1[u], 16)
                    sp.dma_start(w2f[:, u], w2_p[i, u]).then_inc(s_m2[u], 16)
            with sp.Fori(0, BATCH) as b:
                sp.wait_ge(s_fin, b + 2)
                sp.dma_start(out_v[b], acc1[:, bass.ds(b * QT, QT), :]).then_inc(s_out, 16)
            sp.wait_ge(s_out, 16 * BATCH)

        @block.gpsimd
        def _(pool):
            g = nc.gpsimd
            g.memset(wpP[:], 0.0).then_inc(s_pset, 1)
            g.memset(w2all[:], 0.0).then_inc(s_pset, 1)
            g.memset(VB[:], 1.0).then_inc(s_pset, 1)
            g.memset(maxA[:], 0.0).then_inc(s_pset, 1)
            g.memset(maxB[:], 0.0).then_inc(s_pset, 1)
            pool.wait_ge(s_pset, 5)
            wp_v = w_proj.rearrange("(g j i) d -> j i g d", j=HG, i=HDB)
            for j in range(HG):
                g.dma_start(wpP[32 * j:32 * j + HDB, :, :], wp_v[j]).then_inc(s_wpj, 16)
            pool.wait_ge(s_cst, 16)
            pick = ident.rearrange("p (j r) -> p j r", r=32)
            def keys(rows):
                return pick[:, :, rows:rows + NCH].unsqueeze(3).broadcast_to([P, HG, NCH, CH])
            g.tensor_copy(KS[64:96, :].rearrange("p (c m) -> p c m", m=CH),
                          ident[64:96, 64:64 + NCH].unsqueeze(2).broadcast_to([32, NCH, CH])).then_inc(s_pset, 1)
            pool.wait_ge(s_pset, 6)
            g.tensor_tensor(spread[:].rearrange("p (j a) (b m) -> p j (a b) m", j=HG, b=2), keys(0), keys(NCH),
                            ALU.add).then_inc(s_pset, 1)
            g.tensor_copy(neg_bf[:], cst[:, C_NEG:C_NEG + P]).then_inc(s_pset, 1)
            pool.wait_ge(s_qkv, 16)
            for k in range(2):
                src = qkv_raw[:, k * P:(k + 1) * P].rearrange("p (a e) -> p a e", e=HDB)
                for r in range(3):
                    dst = w2all[:, :, k, :].rearrange("p g (j m) -> p g j m", m=32)[:, :, :, 1 + HDB * r:1 + HDB * (r + 1)]
                    for q in range(GROUPS):
                        g.tensor_copy(dst[:, q], src[:, HG * q:HG * q + HG, :]).then_inc(s_pset, 1)

            def copy_wA(g_idx):
                q = wqT[:, bass.ds(g_idx, 1), :, :].rearrange("p g h e -> p (g h) e")
                k = wkT[:, bass.ds(g_idx, 1), :]
                for c in range(2):
                    g.tensor_copy(wA[:, 0:HG, c, :], q).then_inc(s_wA, 1)
                    g.tensor_copy(wA[:, HG:HG + 1, c, :], k).then_inc(s_wA, 1)

            def copy_wB(g_idx):
                g.tensor_copy(wB[:], w2all[:, bass.ds(g_idx, 1), :, :].rearrange("p g k c -> p (g k) c")).then_inc(s_wB, 1)

            def keys_b(count):
                pool.wait_ge(s_pset, N_PSET)
                pool.wait_ge(s_KB, count)
                for j in range(HG):
                    g.tensor_scalar(KBj[:, j, :], KB[:].bitcast(F32), col(4 + j), col(8 + j), ALU.mult,
                                    ALU.add).then_inc(s_KBj, 1)

            def body(it, nxt):
                g_idx = it % GROUPS
                b_idx = it // GROUPS
                pool.wait_ge(s_oB, it + 1)
                g.tensor_copy(VB[:, :, :, 0:HDB],
                              vb_all[:, bass.ds(b_idx * QT, QT), bass.ds(g_idx * HG, HG), :]).then_inc(s_VB, 1)
                pool.wait_ge(s_oA, it * 2 + 2)
                g.tensor_copy(VA[:], v_all[:, bass.ds(b_idx * QT, QT), bass.ds(g_idx, 1), :]
                              .rearrange("p t g e -> p t (g e)")).then_inc(s_VA, 1)
                if nxt:
                    pool.wait_ge(s_HB, it + 1)
                    copy_wB((it + 1) % GROUPS)
                pool.wait_ge(s_sw, it + 1)
                g.tensor_tensor(cr[:], cr[:], cw[:], ALU.mult).then_inc(s_c1, 1)
                if nxt:
                    pool.wait_ge(s_KAh, it + 2)
                    copy_wA((it + 2) % GROUPS)
                    keys_b(it + 2)

            pool.wait_ge(s_wtc, 9)
            pool.wait_ge(s_pset, N_PSET)
            copy_wA(0)
            copy_wB(0)
            pool.wait_ge(s_KAh, 1)
            copy_wA(1)
            keys_b(1)
            pool.wait_ge(s_vc, 12)
            with g.Fori(0, ITERS - 1) as it:
                body(it, True)
            body(ITERS - 1, False)
            pool.wait_ge(s_wpj, 16 * HG)

        @block.scalar
        def _(act):
            s = nc.scalar
            act.dma_start(cst[:], consts).then_inc(s_cst, 16)
            act.dma_start(qkv_raw, w_qkv).then_inc(s_qkv, 16)
            act.dma_start(cols[:, 0:3], w_conv.rearrange("d a k -> d (a k)")).then_inc(s_col, 16)
            for n, a in enumerate((b_conv, ln1_w, ln1_b, ln2_w, ln2_b)):
                act.dma_start(cols[:, 3 + n:4 + n], a.rearrange("(d a) -> d a", a=1)).then_inc(s_col, 16)
            act.dma_start(kgb[:], b_kgen.partition_broadcast(P)).then_inc(s_col, 16)
            act.dma_start(gb[:], gate_b.partition_broadcast(P)).then_inc(s_col, 16)
            act.dma_start(gw[:], gate_w).then_inc(s_col, 16)
            for n, a in enumerate((c_wq, c_wk, c_wv)):
                act.dma_start(c_w[:, n, :], a).then_inc(s_col, 16)

            def deviation(n):
                src, dst = ((xc, sq), (xc, sq), (zn, zsq), (yn, ynsq))[n]
                act.wait_ge(s_cen, n + 1)
                s.activation(dst, src, ACT.Square).then_inc(s_sqd, 1)
                act.wait_ge(s_var, n + 1)
                s.activation(small[:, STD:STD + NT], small[:, VAR:VAR + NT], ACT.Sqrt).then_inc(s_std, 1)

            deviation(0)
            act.wait_ge(s_wt, 1)
            s.copy(wqT[:, 0:2], ps[:, 0, :].rearrange("p (g h e) -> p g h e", g=2, h=HG)).then_inc(s_wtc, 1)
            act.wait_ge(s_wt, 2)
            s.copy(wqT[:, 2:4], ps[:, 1, :].rearrange("p (g h e) -> p g h e", g=2, h=HG)).then_inc(s_wtc, 1)
            act.wait_ge(s_wt, 3)
            s.copy(wkT[:], ps[:, 2, 0:256].rearrange("p (g e) -> p g e", g=GROUPS)).then_inc(s_wtc, 1)
            s.copy(wvT, ps[:, 2, 256:512]).then_inc(s_wtc, 1)
            for n in range(2):
                act.wait_ge(s_wt, 4 + n)
                s.copy(woT[:, 4 * n:4 * n + 4, :], ps[:, 3 + n, :].rearrange("p (n d) -> p n d", n=4)).then_inc(s_wtc, 1)
            act.wait_ge(s_wt, 6)
            s.copy(wfcT[:], ps[:, 5, :]).then_inc(s_wtc, 1)
            act.wait_ge(s_wt, 7)
            s.copy(wpjT[:], ps[:, 6, :].rearrange("p (n d) -> p n d", n=4)).then_inc(s_wtc, 1)
            act.wait_ge(s_wt, 8)
            s.copy(kgT, ps[:, 7, 0:3]).then_inc(s_wtc, 1)
            for b in range(BATCH):
                act.wait_ge(s_xt, b + 1)
                s.copy(xnT[:, b, :], ps[:, b, :]).then_inc(s_xtc, 1)
            deviation(1)
            act.wait_ge(s_col, 16 * N_COLS)
            for b in range(BATCH):
                act.wait_ge(s_ut, b + 1)
                s.activation(uT[:, b * SEQ:(b + 1) * SEQ], ps[:, 4 + b, :], ACT.Identity, scale=cols[:, 4:5],
                             bias=cols[:, 5:6]).then_inc(s_utc, 1)
            act.wait_ge(s_z, 1)
            s.activation(small[:, DYN:DYN + 12], small[:, DYN:DYN + 12], ACT.Exp, scale=-1.0).then_inc(s_ez, 1)
            for n in range(8):
                act.wait_ge(s_v, n + 1)
                s.copy(v_all[:, 2 * n:2 * n + 2], ps[:, n, :].rearrange("p (t g e) -> p t g e", t=2, g=GROUPS)).then_inc(s_vc, 1)
            for n in range(4):
                act.wait_ge(s_v, 9 + n)
                s.copy(vb_all[:, 4 * n:4 * n + 4].rearrange("p t h e -> p (t h e)"), ps[:, n, :]).then_inc(s_vc, 1)

            def tile(ring, use):
                r = ring.slot(use)
                return ps[:, 2 * r:2 * r + 2, :]

            def reciprocal(dst, src, count, bias, out_sem):
                s.activation(dst, src, ACT.Ln, bias=bias).then_inc(s_ln, 1)
                act.wait_ge(s_ln, count)
                s.activation(dst, dst, ACT.Exp, scale=-1.0).then_inc(out_sem, 1)

            def steps(which, it, ring):
                for use in which:
                    kind = use[0]
                    if kind in FILLS and kind not in ("PB", "PA", "BC", "yA", "yB"):
                        t = tile(ring, use)
                        act.wait_ge(ring_full, ring.filled(use))
                    if kind == "SA":
                        _, j, h = use
                        s.activation(eA[:, j, 2 * h:2 * h + 2, :], t, ACT.Exp, scale=SCALE_A).then_inc(s_eA, 1)
                    elif kind == "SB":
                        _, j, h = use
                        s.activation(eB[:, j, :, :], t, ACT.Exp, scale=SCALE_B).then_inc(s_eB, 1)
                    elif kind == "r":
                        act.wait_ge(s_L, it + 1)
                        reciprocal(cr[:], ps[:, 6, :], it * 3 + 1, 0.0, s_r)
                    elif kind == "ct":
                        act.wait_ge(s_tot, it + 1)
                        reciprocal(ct[:], ps[:, 6, :], it * 3 + 2, col(20), s_rt)
                    elif kind == "LB":
                        act.wait_ge(s_lb, it + 1)
                        reciprocal(rB[:], ps[:, 7, :], it * 3 + 3, 0.0, s_rB)
                    elif kind == "cfh":
                        act.wait_ge(s_cf, it + 1)
                        s.copy(cfh[:], cf[:]).then_inc(s_cfh, 1)
                    elif kind == "VB" and use[1] == 1:
                        act.wait_ge(s_otb, it + 1)
                        s.copy(oB[:], ps[:, 7, :]).then_inc(s_oB, 1)
                    elif kind == "VA":
                        act.wait_ge(s_ota, it * 2 + (use[1] + 1))
                        s.copy(oA[:, use[1], :], ps[:, 6, :]).then_inc(s_oA, 1)
                    elif kind == "qA":
                        s.copy(QS[:, 2 * use[1]:2 * use[1] + 2, :], t).then_inc(s_QS, 1)
                    elif kind == "kA":
                        s.copy(KAh[:], t[:, 0, :]).then_inc(s_KAh, 1)
                    elif kind == "mA":
                        s.copy(QS[64:96, 2 * use[1]:2 * use[1] + 2, :], t[64:96]).then_inc(s_shA, 1)
                    elif kind == "qkB":
                        s.copy(HB[:], t).then_inc(s_HB, 1)

            s.sem_inc(s_oB, 1)
            s.sem_inc(s_oA, 1)
            s.sem_inc(s_oA, 1)
            s.sem_inc(s_rB, 1)
            s.preload_act_table_set("natural_log_exp_and_others")
            steps(PRO_STEPS, -1, Ring("prologue", 0))
            with act.Fori(0, ITERS - 1) as it:
                steps(STEPS, it, Ring("body", it))
            steps(EPI_STEPS, ITERS - 1, Ring("epilogue", ITERS - 1))

            deviation(2)
            for b in range(BATCH):
                act.wait_ge(s_zt, b + 1)
                s.activation(zT[:, b * SEQ:(b + 1) * SEQ], ps[:, b, :], ACT.Identity, scale=cols[:, 6:7],
                             bias=cols[:, 7:8]).then_inc(s_ztc, 1)
            act.wait_ge(s_ztc, BATCH)
            s.copy(zH, zT).then_inc(s_zh, 1)
            s.sem_inc(s_hr, 1)
            s.sem_inc(s_hr, 1)
            with act.Fori(0, EXPERTS // 2) as i:
                for u in range(2):
                    act.wait_ge(s_m1[u], i * 16 + 16)
                    act.wait_ge(s_yf, i * 8 + (4 * u + 4))
                    s.copy(w1h[:, u, :], w1f[:, u, :]).then_inc(s_mh, 1)
                    for tb in range(BATCH):
                        t = 4 * u + tb
                        act.wait_ge(s_yf, i * 8 + (t + 7))
                        for h in range(2):
                            act.wait_ge(s_hf, i * 16 + (2 * t + h + 1))
                            s.activation(hid[:, t % 2, 2 * h:2 * h + 2, :], ps[:, 2 * h:2 * h + 2, :],
                                         ACT.Gelu_apprx_tanh).then_inc(s_hr, 1)

            deviation(3)
            for b in range(BATCH):
                act.wait_ge(s_yt, b + 1)
                s.copy(ynT[:, b * SEQ:(b + 1) * SEQ], ps[:, b, :]).then_inc(s_ytc, 1)
            for n in range(4):
                act.wait_ge(s_vv, n + 1)
                s.copy(vC[:, 4 * n:4 * n + 4, :], ps[:, 4 + n, :].rearrange("p (n d) -> p n d", n=4)).then_inc(s_vvc, 1)
            with act.Fori(0, BATCH) as b:
                act.wait_ge(s_lq, b + 1)
                s.copy(qkC, ps[:, 0:2, :]).then_inc(s_lqc, 1)
                for f in range(2):
                    act.wait_ge(s_fh, b * 2 + (f + 1))
                    s.activation(fr[:, 2 * f:2 * f + 2, :], ps[:, 2 + 2 * f:4 + 2 * f, :], ACT.Relu).then_inc(s_fr, 1)
                for q in range(QT):
                    act.wait_ge(s_lx, b * 4 + (q + 1))
                    s.activation(pC[:, q, 0:P * (q + 1)], score_c(q), ACT.Exp, scale=SCALE_C, bias=small[:, q:q + 1],
                                 accum_out=small[:, 4 + q:5 + q]).then_inc(s_le, 1)
                act.wait_ge(s_lt, b + 1)
                s.copy(pT[:, 0:8, :], ps[:, 2:4, :].rearrange("p b (n t) -> p (b n) t", n=4)).then_inc(s_ltc, 1)
                s.copy(pT[:, 8:10, :], ps[:, 4, 0:256].rearrange("p (n t) -> p n t", n=2)).then_inc(s_ltc, 1)

        @block.tensor
        def _(pe):
            t = nc.tensor
            pe.wait_ge(s_cst, 16)
            pe.wait_ge(s_w, 16 * 7)
            for bank in range(7):
                for n in range(4):
                    m = t.transpose(ps[:, bank, n * P:(n + 1) * P], raw[:, 4 * bank + n, :], ident)
                m.then_inc(s_wt, 1)
            t.transpose(ps[:, 7, 0:3], kg_raw, ident[0:3, 0:3]).then_inc(s_wt, 1)

            def transposed(src, bank, n):
                for q in range(4):
                    m = t.transpose(ps[:, bank, q * P:(q + 1) * P], src[:, 4 * n + q, :], ident)
                return m

            pe.wait_ge(s_nrm, 1)
            pe.wait_ge(s_wtc, 9)
            for n in range(4):
                transposed(acc2, n, n).then_inc(s_xt, 1)
            pe.wait_ge(s_nrm, 2)
            for n in range(4):
                transposed(un, 4 + n, n).then_inc(s_ut, 1)
            pe.wait_ge(s_xtc, BATCH)
            pe.wait_ge(s_ctx, 1)
            for b in range(BATCH):
                m = t.matmul(ps[:, 0, 3 * b:3 * b + 3], ctxb[:, b, :], kgT, start=True, stop=True)
            m.then_inc(s_dyn, 1)
            pe.wait_ge(s_h, BATCH)
            pe.wait_ge(s_utc, BATCH)
            for n in range(8):
                for q in range(2):
                    k = 2 * n + q
                    m = t.matmul(ps[:, n, 256 * q:256 * q + 256], hT[:, k * P:(k + 1) * P], wvT, start=True, stop=True)
                m.then_inc(s_v, 1)
            for n in range(4):
                pe.wait_ge(s_vc, n + 1)
                for q in range(4):
                    k = 4 * n + q
                    m = t.matmul(ps[:, n, P * q:P * q + P], uT[:, k * P:(k + 1) * P], qkv_raw[:, 256:384],
                                 start=True, stop=True)
                m.then_inc(s_v, 1)

            def consumed(use, it):
                kind = use[0]
                if kind in ("SA", "PA", "PB", "BC"):
                    sema = {"SA": s_eA, "PA": s_maxA, "PB": s_maxB, "BC": s_wts}[kind]
                    return sema, it * 8 + (2 * use[1] + use[2] + 1 + 8 * (kind == "PA"))
                if kind == "SB":
                    return s_eB, it * 8 + (HG * use[2] + use[1] + 1)
                if kind in ("qA", "mA"):
                    return (s_QA if kind == "qA" else s_shA), it * 2 + (use[1] + 3)
                return {"kA": (s_KS, it + 2), "qkB": (s_QB, it + 2), "yB": (s_acc, it * 2 + 3),
                        "yA": (s_acc, it * 2 + 4)}[kind]

            def open_tile(ring, use, it):
                last = ring.before(use)
                if last is not None:
                    pe.wait_ge(*consumed(last, it))
                elif ring.section == "prologue":
                    pe.wait_ge(s_vc, 12)
                else:
                    n = ring.order.index(use)
                    if n == 0:
                        pe.wait_ge(s_shA, it * 2 + 2)
                    if n == 1:
                        pe.wait_ge(s_QB, it + 1)
                    else:
                        pe.wait_ge(s_acc, it * 2 + (1 + n // 2))
                r = ring.slot(use)
                return ps[:, 2 * r:2 * r + 2, :]

            def negated_rows(dst, src, q):
                return t.matmul(dst[:, q * P:(q + 1) * P], src, neg_bf[:], start=True, stop=True)

            def steps(which, it, ring):
                g_idx = it % GROUPS
                for use in which:
                    kind = use[0]
                    if kind in FILLS:
                        tile = open_tile(ring, use, it)
                    if kind == "SA":
                        _, j, h = use
                        if h == 0:
                            pe.wait_ge(s_shA, it * 2 + (j // 2 + 1))
                            pe.wait_ge(s_KS, it + 1)
                        for q in range(2):
                            kt = 2 * h + q
                            t.matmul(tile[:, q, :], KAh[:, kt * P:(kt + 1) * P], QA[:, j, :], start=True, stop=False)
                            mm = t.matmul(tile[:, q, :], KS[0:96, kt * P:(kt + 1) * P], QS[0:96, j, :], start=False, stop=True)
                    elif kind == "PB":
                        _, j, h = use
                        if (j, h) == (0, 0):
                            pe.wait_ge(s_QB, it + 1)
                        if h == 0:
                            pe.wait_ge(s_KBj, it * 4 + (j + 1))
                        for q in range(2):
                            k = 2 * h + q
                            mm = t.matmul(tile[:, q, :], QB[:, k * P:(k + 1) * P], KBj[:, j, :], start=True, stop=True)
                    elif kind == "L":
                        pe.wait_ge(s_oA, it * 2 + 2)
                        pe.wait_ge(s_eA, it * 8 + 8)
                        for kt in range(KT):
                            for j in range(HG):
                                mm = t.matmul(ps[32 * j:32 * j + 32, 6, :], cst[:, C_SELL + 32 * kt:C_SELL + 32 * kt + 32],
                                              eA[:, j, kt, :], start=(kt == 0), stop=(kt == KT - 1))
                        mm.then_inc(s_L, 1)
                    elif kind == "TOT":
                        pe.wait_ge(s_sw, it + 1)
                        t.matmul(ps[:, 6, :], cst[:, C_BD:C_BD + P], cw[:], start=True, stop=True).then_inc(s_tot, 1)
                    elif kind == "mB":
                        pe.wait_ge(s_rB, it + 1)
                        pe.wait_ge(s_maxB, it * 8 + 8)
                        for q in range(QT):
                            mm = negated_rows(ps[:, 7, :], maxB[:, q, :], q)
                        mm.then_inc(s_mtB, 1)
                    elif kind == "VB":
                        h = use[1]
                        if h == 0:
                            pe.wait_ge(s_QBs, it + 1)
                            pe.wait_ge(s_VB, it + 1)
                        pe.wait_ge(s_eB, it * 8 + (HG * h + HG))
                        for q in range(2):
                            kt = 2 * h + q
                            for j in range(HG):
                                mm = t.matmul(ps[32 * j:32 * j + 32, 7, :], VB[:, kt, j, :], eB[:, j, q, :],
                                              start=(kt == 0), stop=(kt == KT - 1))
                        if h == 1:
                            mm.then_inc(s_otb, 1)
                    elif kind == "LB":
                        pe.wait_ge(s_oB, it + 2)
                        t.matmul(ps[:, 7, :], cst[:, C_SELB:C_SELB + P], oB[:], start=True, stop=True).then_inc(s_lb, 1)
                    elif kind == "VA":
                        p = use[1]
                        if p == 0:
                            pe.wait_ge(s_rt, it + 1)
                            pe.wait_ge(s_VA, it + 1)
                        else:
                            pe.wait_ge(s_oA, it * 2 + 3)
                        pe.wait_ge(s_wts, it * 8 + (4 * p + 4))
                        for kt in range(KT):
                            for q in range(2):
                                mm = t.matmul(ps[64 * q:64 * q + 64, 6, :], VA[:, kt, :], eA[:, 2 * p + q, kt, :],
                                              start=(kt == 0), stop=(kt == KT - 1))
                        mm.then_inc(s_ota, 1)
                    elif kind == "BC":
                        _, j, h = use
                        if (j, h) == (0, 0):
                            pe.wait_ge(s_cfl, it + 1)
                        for q in range(2):
                            mm = t.matmul(tile[:, q, :], spread[:, KT * j + 2 * h + q, :], cfl[:], start=True, stop=True)
                    elif kind == "SB":
                        _, j, h = use
                        if (j, h) == (0, 0):
                            pe.wait_ge(s_QBs, it + 1)
                        for q in range(2):
                            kt = 2 * h + q
                            mm = t.matmul(tile[:, q, :], KBj[:, j, kt * P:(kt + 1) * P], QB[:], start=True, stop=True)
                    elif kind == "qA":
                        p = use[1]
                        if p == 0:
                            pe.wait_ge(s_wA, it * 4 + 8)
                        for q in range(2):
                            mm = t.matmul(tile[:, q, :], wA[:, 2 * p + q].rearrange("p c e -> p (c e)"),
                                          hT[:, bass.ds((it + 1) // GROUPS * SEQ, SEQ)], start=True, stop=True)
                    elif kind == "kA":
                        mm = t.matmul(tile[:, 0, :], wA[:, HG].rearrange("p c e -> p (c e)"),
                                      hT[:, bass.ds((it + 1) // GROUPS * SEQ, SEQ)], start=True, stop=True)
                    elif kind == "qkB":
                        pe.wait_ge(s_wB, it + 2)
                        for k in range(2):
                            mm = t.matmul(tile[:, k, :], wB[:, k, :], uT[:, bass.ds((it + 1) // GROUPS * SEQ, SEQ)],
                                          start=True, stop=True)
                    elif kind == "PA":
                        _, j, h = use
                        if h == 0:
                            pe.wait_ge(s_QA, it * 2 + (j // 2 + 3))
                            pe.wait_ge(s_KAh, it + 2)
                        for q in range(2):
                            k = 2 * h + q
                            mm = t.matmul(tile[:, q, :], QA[:, j, k * P:(k + 1) * P], KAh[:], start=True, stop=True)
                    elif kind == "mA":
                        p = use[1]
                        pe.wait_ge(s_maxA, it * 8 + (4 * p + 12))
                        for j in range(2):
                            for q in range(QT):
                                mm = negated_rows(tile[:, j, :], maxA[:, q, 2 * p + j, :], q)
                    elif kind == "yB":
                        pe.wait_ge(s_yB, it + 1)
                        for q in range(QT):
                            mm = t.matmul(tile[:, 0, q * P:(q + 1) * P], oB[:, q * P:(q + 1) * P],
                                          wpP[:, bass.ds(g_idx, 1), :].rearrange("p n d -> p (n d)"), start=True, stop=True)
                    elif kind == "yA":
                        pe.wait_ge(s_oA, it * 2 + 4)
                        for q in range(QT):
                            for p in range(2):
                                mm = t.matmul(tile[:, 0, q * P:(q + 1) * P], oA[:, p, q * P:(q + 1) * P],
                                              woT[:, bass.ds(g_idx * 2 + p, 1), :].rearrange("p n d -> p (n d)"),
                                              start=(p == 0), stop=(p == 1))
                    if kind in FILLS:
                        mm.then_inc(ring_full, 1)

            pe.wait_ge(s_pset, N_PSET)
            steps(PRO_STEPS, -1, Ring("prologue", 0))
            pe.wait_ge(s_wpj, 16 * HG)
            with pe.Fori(0, ITERS - 1) as it:
                steps(STEPS, it, Ring("body", it))
            steps(EPI_STEPS, ITERS - 1, Ring("epilogue", ITERS - 1))

            pe.wait_ge(s_nrm, 3)
            for n in range(4):
                transposed(zn, n, n).then_inc(s_zt, 1)
            pe.wait_ge(s_ztc, BATCH)
            for n in range(NT):
                m = t.matmul(ps[:, 4, 8 * n:8 * n + 8], zT[:, n * P:(n + 1) * P], gw[:], start=True, stop=True)
            m.then_inc(s_gl, 1)
            pe.wait_ge(s_hot, 1)
            for _ in range(8):
                t.sem_inc(s_yf, 1)
            with pe.Fori(0, EXPERTS // 2) as i:
                def outputs(n):
                    u, tb = n // BATCH, n % BATCH
                    pe.wait_ge(s_ya, i * 32 + (4 * n + 4))
                    pe.wait_ge(s_hr, i * 16 + (2 * n + 4))
                    pe.wait_ge(s_m2[u], i * 16 + 16)
                    for q in range(QT):
                        for f in range(FB):
                            mm = t.matmul(ps[:, 4 + tb, q * P:(q + 1) * P], hid[:, n % 2, f, q * P:(q + 1) * P],
                                          w2f[:, u, f, :], start=(f == 0), stop=(f == FB - 1))
                    mm.then_inc(s_yf, 1)

                for n in range(8):
                    u, tb = n // BATCH, n % BATCH
                    if tb == 0:
                        pe.wait_ge(s_mh, i * 2 + (u + 1))
                        pe.wait_ge(s_ml, i * 2 + (u + 1))
                    for h in range(2):
                        pe.wait_ge(s_hr, i * 16 + (2 * n + h + 1))
                        for q in range(2):
                            f = 2 * h + q
                            for k, (w, z) in enumerate(((w1h, zH), (w1l, zH), (w1h, zL))):
                                mm = t.matmul(ps[:, f, :], w[:, u, f * P:(f + 1) * P], z[:, tb * SEQ:(tb + 1) * SEQ],
                                              start=(k == 0), stop=(k == 2))
                        mm.then_inc(s_hf, 1)
                    if n:
                        outputs(n - 1)
                outputs(7)

            pe.wait_ge(s_nrm, 4)
            for n in range(4):
                transposed(yn, n, n).then_inc(s_yt, 1)
            pe.wait_ge(s_ytc, BATCH)
            for n in range(4):
                for q in range(4):
                    k = 4 * n + q
                    m = t.matmul(ps[:, 4 + n, P * q:P * q + P], ynT[:, k * P:(k + 1) * P], c_w[:, 2, :], start=True, stop=True)
                m.then_inc(s_vv, 1)
            pe.wait_ge(s_vvc, 4)
            with pe.Fori(0, BATCH) as b:
                rhs = ynT[:, bass.ds(b * SEQ, SEQ)]
                pe.wait_ge(s_fin, b + 1)
                for k in range(2):
                    mm = t.matmul(ps[:, k, :], c_w[:, k, :], rhs, start=True, stop=True)
                mm.then_inc(s_lq, 1)
                for f in range(FB):
                    mm = t.matmul(ps[:, 2 + f, :], wfcT[:, f * P:(f + 1) * P], rhs, start=True, stop=True)
                    if f % 2:
                        mm.then_inc(s_fh, 1)
                pe.wait_ge(s_lqc, b + 1)
                pe.wait_ge(s_fr, b * 2 + 2)
                for q in range(QT):
                    t.matmul(score_c(q), qkC[:, 0, q * P:(q + 1) * P], qkC[:, 1, 0:P * (q + 1)], start=True,
                             stop=True).then_inc(s_ls, 1)
                pe.wait_ge(s_fs, b * 2 + 2)
                for q in range(QT):
                    for f in range(FB):
                        mm = t.matmul(ps[:, 6, q * P:(q + 1) * P], fr[:, f, q * P:(q + 1) * P], wpjT[:, f, :],
                                      start=(f == 0), stop=(f == FB - 1))
                mm.then_inc(s_fy, 1)
                n = 0
                for q in range(QT):
                    pe.wait_ge(s_le, b * 4 + (q + 1))
                    for k in range(q + 1):
                        mm = t.transpose(ps[:, 2 + n // 4, (n % 4) * P:(n % 4 + 1) * P], pC[:, q, k * P:(k + 1) * P], ident)
                        n += 1
                mm.then_inc(s_lt, 1)
                pe.wait_ge(s_ltc, b * 2 + 2)
                n = 0
                for q in range(QT):
                    for k in range(q + 1):
                        mm = t.matmul(ps[:, 5, q * P:(q + 1) * P], pT[:, n, :],
                                      vC[:, bass.ds(b * QT + k, 1), :].rearrange("p n d -> p (n d)"), start=(k == 0), stop=(k == q))
                        n += 1
                mm.then_inc(s_lo, 1)

        @block.vector
        def _(dve):
            v = nc.vector
            chain = [0]

            def link(ins):
                chain[0] += 1
                ins.then_inc(s_chain, 1)
                dve.wait_ge(s_chain, chain[0])

            def layer_norm(n, src, xc, sq, dst):
                link(v.tensor_reduce(small[:, 0:NT], src, AX_X, ALU.add))
                link(v.tensor_scalar(small[:, MEAN:MEAN + NT], small[:, 0:NT], 1.0 / D, None, ALU.mult))
                v.tensor_tensor(xc, src, per_tile(MEAN), ALU.subtract).then_inc(s_cen, 1)
                dve.wait_ge(s_sqd, n + 1)
                link(v.tensor_reduce(small[:, 0:NT], sq, AX_X, ALU.add))
                v.tensor_scalar(small[:, VAR:VAR + NT], small[:, 0:NT], 1.0 / D, EPS, ALU.mult, ALU.add).then_inc(s_var, 1)
                dve.wait_ge(s_std, n + 1)
                link(v.reciprocal(small[:, RSTD:RSTD + NT], small[:, STD:STD + NT]))
                dve.wait_ge(s_cen, n + 1)
                v.tensor_tensor(dst, xc, per_tile(RSTD), ALU.mult).then_inc(s_nrm, 1)
                dve.wait_ge(s_nrm, n + 1)

            dve.wait_ge(s_x, 16 * BATCH)
            layer_norm(0, acc1[:], xc, sq, acc2[:])
            layer_norm(1, acc2[:], xc, sq, un)
            dve.wait_ge(s_xtc, BATCH)
            link(v.tensor_reduce(small[:, CTX:CTX + BATCH], xnT, AX_X, ALU.add))
            v.tensor_scalar(ctxb, small[:, CTX:CTX + BATCH].unsqueeze(2).broadcast_to([P, BATCH, P]), 1.0 / SEQ, None,
                            ALU.mult).then_inc(s_ctx, 1)
            dve.wait_ge(s_col, 16 * N_COLS)
            link(v.tensor_scalar(cacc, xnT, cols[:, 1:2], None, ALU.mult))
            link(v.scalar_tensor_tensor(cacc[:, :, 1:SEQ], xnT[:, :, 0:SEQ - 1], cols[:, 0:1], cacc[:, :, 1:SEQ],
                                        ALU.mult, ALU.add))
            link(v.scalar_tensor_tensor(cacc[:, :, 0:SEQ - 1], xnT[:, :, 1:SEQ], cols[:, 2:3], cacc[:, :, 0:SEQ - 1],
                                        ALU.mult, ALU.add))
            dve.wait_ge(s_dyn, 1)
            dyn = small[:, DYN:DYN + 12].rearrange("p (b k) -> p b k", k=3)
            v.tensor_tensor(dyn, ps[:, 0, 0:12].rearrange("p (b k) -> p b k", k=3),
                            kgb[:].unsqueeze(1).broadcast_to([P, BATCH, 3]), ALU.add).then_inc(s_z, 1)
            dve.wait_ge(s_ez, 1)
            link(v.tensor_scalar(dyn, dyn, 1.0, None, ALU.add))
            link(v.reciprocal(dyn, dyn))
            link(v.tensor_reduce(small[:, GATE:GATE + BATCH], dyn, AX_X, ALU.add))
            link(v.tensor_scalar(small[:, GATE:GATE + BATCH], small[:, GATE:GATE + BATCH], 1.0 / 3.0, None, ALU.mult))
            for b in range(BATCH):
                v.tensor_scalar(hT[:, b * SEQ:(b + 1) * SEQ], cacc[:, b, :], cols[:, 3:4],
                                small[:, GATE + b:GATE + b + 1], ALU.add, ALU.mult).then_inc(s_h, 1)
            v.sem_inc(s_acc, 1)
            v.sem_inc(s_acc, 1)

            def tile(ring, use):
                r = ring.slot(use)
                return ps[:, 2 * r:2 * r + 2, :]

            def steps(which, it, ring):
                for use in which:
                    kind = use[0]
                    if kind in FILLS:
                        t = tile(ring, use)
                    if kind in ("PB", "PA", "BC", "yA", "yB"):
                        dve.wait_ge(ring_full, ring.filled(use))
                    if kind == "PB":
                        _, j, h = use
                        v.tensor_reduce(maxB[:, 2 * h:2 * h + 2, 32 * j:32 * j + 1], t, AX_X, ALU.max).then_inc(s_maxB, 1)
                    elif kind == "PA":
                        _, j, h = use
                        v.tensor_reduce(maxA[:, 2 * h:2 * h + 2, j, 64:64 + NCH],
                                        t.rearrange("p q (c k) -> p q c k", c=NCH), AX_X, ALU.max).then_inc(s_maxA, 1)
                    elif kind == "BC":
                        _, j, h = use
                        e = eA[:, j, 2 * h:2 * h + 2, :]
                        v.tensor_tensor(e, e, t, ALU.mult).then_inc(s_wts, 1)
                    elif kind == "cw":
                        dve.wait_ge(s_r, it + 1)
                        v.tensor_tensor(cw[:], ps[:, 6, :], cr[:], ALU.mult).then_inc(s_sw, 1)
                    elif kind == "mB":
                        dve.wait_ge(s_mtB, it + 1)
                        v.tensor_tensor(QB[:], QB[:].bitcast(F32), ps[:, 7, :], ALU.add).then_inc(s_QBs, 1)
                    elif kind == "qA":
                        p = use[1]
                        dve.wait_ge(s_QS, it * 2 + (p + 3))
                        v.scalar_tensor_tensor(QA[:, 2 * p:2 * p + 2, :], QS[:, 2 * p:2 * p + 2, :].bitcast(F32), col(0), t,
                                               ALU.mult, ALU.add).then_inc(s_QA, 1)
                    elif kind == "kA":
                        dve.wait_ge(s_pset, N_PSET)
                        dve.wait_ge(s_KAh, it + 2)
                        v.tensor_tensor(KS[0:64, :], t[0:64, 0, :], KAh[0:64, :].bitcast(F32), ALU.subtract).then_inc(s_KS, 1)
                    elif kind == "cf":
                        dve.wait_ge(s_rt, it + 1)
                        dve.wait_ge(s_c1, it + 1)
                        v.tensor_tensor(cf[:], cr[:], ct[:], ALU.mult).then_inc(s_cf, 1)
                    elif kind == "cfl":
                        dve.wait_ge(s_cfh, it + 1)
                        v.scalar_tensor_tensor(cfl[:], cfh[:].bitcast(F32), col(3), cf[:], ALU.mult, ALU.add).then_inc(s_cfl, 1)
                    elif kind == "qkB":
                        dve.wait_ge(s_HB, it + 2)
                        v.scalar_tensor_tensor(KB[:], HB[:, 1, :].bitcast(F32), col(2), t[:, 1, :], ALU.mult,
                                               ALU.add).then_inc(s_KB, 1)
                        v.scalar_tensor_tensor(QB[:], HB[:, 0, :].bitcast(F32), col(1), t[:, 0, :], ALU.mult,
                                               ALU.add).then_inc(s_QB, 1)
                    elif kind == "LB":
                        dve.wait_ge(s_rB, it + 2)
                        v.tensor_tensor(oB[:], oB[:], rB[:], ALU.mult).then_inc(s_yB, 1)
                    elif kind in ("yA", "yB"):
                        acc = acc1 if kind == "yA" else acc2
                        a = acc[:, bass.ds((it // GROUPS) * QT, QT), :]
                        dve.wait_ge(s_acc, it * 2 + (2 if kind == "yA" else 1))
                        v.tensor_tensor(a, a, t[:, 0, :].rearrange("p (q d) -> p q d", q=QT), ALU.add).then_inc(s_acc, 1)

            steps(PRO_STEPS, -1, Ring("prologue", 0))
            with dve.Fori(0, ITERS - 1) as it:
                steps(STEPS, it, Ring("body", it))
            steps(EPI_STEPS, ITERS - 1, Ring("epilogue", ITERS - 1))

            dve.wait_ge(s_acc, 2 * ITERS + 2)
            layer_norm(2, acc2[:], zn, zsq, zn)
            v.tensor_tensor(acc1[:], acc1[:], acc2[:], ALU.add).then_inc(s_ya, 1)
            dve.wait_ge(s_zh, 1)
            v.tensor_tensor(zL, zT, zH.bitcast(F32), ALU.subtract).then_inc(s_zl, 1)
            dve.wait_ge(s_gl, 1)
            link(v.tensor_tensor(lg[:], ps[:, 4, 0:NT * EXPERTS].rearrange("p (n e) -> p n e", n=NT),
                                 gb[:].unsqueeze(1).broadcast_to([P, NT, EXPERTS]), ALU.add))
            link(v.tensor_reduce(small[:, 0:NT], lg[:], AX_X, ALU.max))
            per_expert = small[:, 0:NT].unsqueeze(2).broadcast_to([P, NT, EXPERTS])
            link(v.tensor_tensor(lge[:], lg[:], per_expert, ALU.is_equal))
            link(v.tensor_tensor(lge[:], lge[:], cst[:, C_COL + 12:C_COL + 12 + EXPERTS].unsqueeze(1)
                                 .broadcast_to([P, NT, EXPERTS]), ALU.mult))
            link(v.tensor_reduce(small[:, 0:NT], lge[:], AX_X, ALU.max))
            v.tensor_tensor(hot[:].rearrange("p e n -> p n e"), lge[:], per_expert, ALU.is_equal).then_inc(s_hot, 1)
            dve.wait_ge(s_hot, 1)
            for _ in range(15):
                v.sem_inc(s_ya, 1)
            with dve.Fori(0, EXPERTS // 2) as i:
                def low_parts(u):
                    dve.wait_ge(s_mh, i * 2 + (u + 1))
                    v.tensor_tensor(w1l[:, u, :], w1f[:, u, :], w1h[:, u, :].bitcast(F32), ALU.subtract).then_inc(s_ml, 1)

                low_parts(0)
                for n in range(2 * BATCH):
                    u, tb = n // BATCH, n % BATCH
                    if n == 2:
                        low_parts(1)
                    dve.wait_ge(s_yf, i * 8 + (n + 9))
                    dve.wait_ge(s_ya, i * 32 + (4 * n + 16))
                    for q in range(QT):
                        k = tb * QT + q
                        v.scalar_tensor_tensor(acc1[:, k, :], ps[:, 4 + tb, q * P:(q + 1) * P],
                                               hot[:, bass.ds(i * 2 + u, 1), k:k + 1].rearrange("p e n -> p (e n)"),
                                               acc1[:, k, :], ALU.mult, ALU.add).then_inc(s_ya, 1)

            dve.wait_ge(s_ya, 16 + 4 * BATCH * EXPERTS)
            layer_norm(3, acc1[:], yn, ynsq, yn)
            v.sem_inc(s_fin, 1)
            LX, LL = 0, 4
            mem, tmp, spk, cnt = (lif[:, 512 * n:512 * n + 512] for n in range(4))
            with dve.Fori(0, BATCH) as b:
                for f in range(2):
                    dve.wait_ge(s_fr, b * 2 + (f + 1))
                    h = fr[:, 2 * f:2 * f + 2, :]
                    v.tensor_tensor(h, h, h, ALU.mult).then_inc(s_fs, 1)
                for q in range(QT):
                    dve.wait_ge(s_ls, b * 4 + (q + 1))
                    sc = score_c(q)
                    dg = sc[:, q * P:(q + 1) * P]
                    v.tensor_tensor(dg, dg, cst[:, C_CAUSAL:C_CAUSAL + P], ALU.add).then_inc(s_lm, 1)
                    dve.wait_ge(s_lm, b * 8 + (2 * q + 1))
                    v.tensor_reduce(small[:, 8 + q:9 + q], sc, AX_X, ALU.max).then_inc(s_lm, 1)
                    dve.wait_ge(s_lm, b * 8 + (2 * q + 2))
                    v.tensor_scalar(small[:, LX + q:LX + q + 1], small[:, 8 + q:9 + q], -SCALE_C, None, ALU.mult).then_inc(s_lx, 1)
                dve.wait_ge(s_fy, b + 1)
                y = ps[:, 6, :]
                seq = [0]
                LIF_OPS = 3 + 4 * 4

                def spike(ins):
                    seq[0] += 1
                    ins.then_inc(s_sp, 1)
                    dve.wait_ge(s_sp, b * LIF_OPS + seq[0])

                spike(v.tensor_copy(mem, y))
                spike(v.tensor_scalar(spk, mem, 1.0, None, ALU.is_gt))
                spike(v.tensor_copy(cnt, spk))
                for _ in range(4):
                    spike(v.scalar_tensor_tensor(tmp, mem, 0.9, y, ALU.mult, ALU.add))
                    spike(v.tensor_tensor(mem, tmp, spk, ALU.subtract))
                    spike(v.tensor_scalar(spk, mem, 1.0, None, ALU.is_gt))
                    spike(v.tensor_tensor(cnt, cnt, spk, ALU.add))
                dve.wait_ge(s_le, b * 4 + 4)
                v.reciprocal(small[:, 12:16], small[:, LL:LL + 4]).then_inc(s_loa, 1)
                dve.wait_ge(s_loa, b * 6 + 1)
                a = acc1[:, bass.ds(b * QT, QT), :]
                v.scalar_tensor_tensor(a, cnt.rearrange("p (q d) -> p q d", q=QT), 0.2, a, ALU.mult, ALU.add).then_inc(s_loa, 1)
                dve.wait_ge(s_loa, b * 6 + 2)
                dve.wait_ge(s_lo, b + 1)
                for q in range(QT):
                    a = acc1[:, bass.ds(b * QT + q, 1), :].rearrange("p n d -> p (n d)")
                    ins = v.scalar_tensor_tensor(a, ps[:, 5, q * P:(q + 1) * P], small[:, 12 + q:13 + q], a, ALU.mult, ALU.add)
                    ins.then_inc(s_fin if q == QT - 1 else s_loa, 1)
                dve.wait_ge(s_loa, b * 6 + 5)
                v.tensor_copy(small[:, 140:141], small[:, 12:13]).then_inc(s_loa, 1)


_INS = ['L0_attn_hidden_states', 'L0_attn_w_q', 'L0_attn_w_k', 'L0_attn_w_v', 'L0_attn_w_o', 'L0_attn_w_kgen',
        'L0_attn_b_kgen', 'L0_attn_w_conv', 'L0_attn_b_conv', 'L0_ffn_ln1_w', 'L0_ffn_ln1_b', 'L0_ffn_w_qkv',
        'L0_ffn_w_proj', 'L0_ffn_ln2_w', 'L0_ffn_ln2_b', 'L0_ffn_gate_w', 'L0_ffn_gate_b', 'L0_ffn_w1', 'L0_ffn_w2',
        'L1_attn_WQ', 'L1_attn_WK', 'L1_attn_WV', 'L1_ffn_W_fc', 'L1_ffn_W_proj']
_OUTS = [((4, 512, 128), 'float32')]


def kernel(**inputs):
    import numpy as _np
    import concourse.bacc as _bacc
    from concourse import mybir as _mybir
    from concourse.bass_utils import run_bass_kernel_spmd as _run

    nc = _bacc.Bacc("TRN2", target_bir_lowering=False, num_devices=1)
    arrays, args = {}, []
    named = [(name, _np.ascontiguousarray(inputs[name])) for name in _INS] + [("constants", constant_columns())]
    for name, a in named:
        arrays[f"in_{name}_dram"] = a
        args.append(nc.dram_tensor(f"in_{name}_dram", a.shape, _mybir.dt.from_np(a.dtype), kind="ExternalInput").ap())
    for i, (shape, dtype) in enumerate(_OUTS):
        dt = _mybir.dt.from_np(_np.dtype(dtype))
        args.append(nc.dram_tensor(f"out_{i}_dram", shape, dt, kind="ExternalOutput").ap())
    build(nc, *args)
    r = _run(nc, [arrays], core_ids=[0])
    return r.results[0]["out_0_dram"]
```

```python
from contextlib import ExitStack

import numpy as np

import concourse.bass as bass
from concourse import mybir

F32 = mybir.dt.float32
F32R = mybir.dt.float32r
BF16 = mybir.dt.bfloat16
ALU = mybir.AluOpType
ACT = mybir.ActivationFunctionType
AX_X = mybir.AxisListType.X

P = 128
BATCH, SEQ, D = 4, 512, 128
NT = BATCH * SEQ // P
QT = SEQ // P
KT = SEQ // P
GROUPS = 4
HG = 4
HDA = 64
CH = 64
NCH = SEQ // CH
HDB = 8
ITERS = BATCH * GROUPS
EXPERTS, FF = 8, 512
FB = FF // P
SLOT_TILES = NT + EXPERTS
EPS = 1e-5
SCALE_A = HDA ** -0.5
SCALE_B = float(1.0 / np.sqrt(HDB))
SCALE_C = float(1.0 / np.sqrt(D))

C_ID, C_NEG, C_SELB, C_BD, C_SELL, C_CAUSAL, C_COL = 0, 128, 256, 384, 512, 640, 768
C_BEFORE, C_THR, C_TRI, C_SLOT = 792, 920, 936, 1000
C_N = C_SLOT + 24


def constant_columns():
    c = np.zeros((P, C_N), np.float32)
    r = np.arange(P)
    c[:, C_ID:C_ID + P] = np.eye(P)
    c[:, C_NEG:C_NEG + P] = -np.eye(P)
    c[:, C_SELB:C_SELB + P] = r[:, None] == 32 * (r[None, :] // 32) + 8
    c[:, C_BD:C_BD + P] = (r[:, None] // 32 == r[None, :] // 32) & (r[:, None] % 32 < NCH)
    for kt in range(KT):
        m = np.arange(32)
        c[:, C_SELL + 32 * kt:C_SELL + 32 * kt + 32] = (m[None, :] % NCH) == (2 * kt + r[:, None] // CH)
    c[:, C_CAUSAL:C_CAUSAL + P] = np.where(r[None, :] > r[:, None], -1e30, 0.0)
    c[:, C_BEFORE:C_BEFORE + P] = r[:, None] < r[None, :]
    c[:, C_THR:C_THR + NT] = P * np.arange(NT)
    e = np.arange(EXPERTS)
    c[:, C_TRI:C_TRI + EXPERTS ** 2] = (e[None, :] <= e[:, None]).reshape(-1)
    c[:, C_SLOT:C_SLOT + SLOT_TILES] = np.arange(SLOT_TILES)
    k = C_COL
    c[:, k] = -1.0 * (r >= 64)
    c[:, k + 1] = -1.0 * ((r % 32 >= 9) & (r % 32 < 17))
    c[:, k + 2] = -1.0 * ((r % 32 >= 17) & (r % 32 < 25))
    c[:, k + 3] = -1.0 * ((r % 32 >= 8) & (r % 32 < 16))
    for j in range(HG):
        c[:, k + 4 + j] = r // 32 == j
        c[:, k + 8 + j] = r == 32 * j
    c[:, k + 20] = 1e-9
    c[:, k + 21] = EPS
    c[:, k + 23] = 0.2
    c[:, k + 12:k + 12 + EXPERTS] = EXPERTS - np.arange(EXPERTS)
    return c


STEPS = [
    ("SA", 0, 0), ("SA", 0, 1), ("PB", 0, 0), ("SA", 1, 0), ("PB", 0, 1), ("SA", 1, 1), ("PB", 1, 0), ("SA", 2, 0),
    ("PB", 1, 1), ("SA", 2, 1), ("PB", 2, 0), ("SA", 3, 0), ("PB", 2, 1), ("SA", 3, 1), ("PB", 3, 0), ("qA", 0),
    ("PB", 3, 1), ("qA", 1), ("L",), ("mB",), ("QBs",), ("r",), ("kA",), ("cw",), ("SB", 0, 0), ("SB", 1, 0),
    ("SB", 2, 0), ("PA", 0, 0), ("SB", 3, 0), ("TOT",), ("PA", 0, 1), ("ct",), ("cf",), ("PA", 1, 0), ("VB", 0),
    ("cfh",), ("cfl",), ("SB", 0, 1), ("SB", 1, 1), ("PA", 1, 1), ("SB", 2, 1), ("BC", 0, 0), ("SB", 3, 1),
    ("BC", 0, 1), ("BC", 1, 0), ("BC", 1, 1), ("VB", 1), ("BC", 2, 0), ("oB",), ("BC", 2, 1), ("PA", 2, 0), ("VA", 0),
    ("BC", 3, 0), ("mA", 0), ("BC", 3, 1), ("LB",), ("oA", 0), ("PA", 2, 1), ("PA", 3, 0), ("PA", 3, 1), ("rB",),
    ("VA", 1), ("mA", 1), ("sB",), ("yB",), ("oA", 1), ("qkB",), ("yA",)]
FILLS = ("SA", "PB", "BC", "SB", "yA", "yB", "qA", "kA", "qkB", "PA", "mA")
NEXT = ("qA", "kA", "qkB", "PA", "mA")
PRO_STEPS = [u for u in STEPS if u[0] in NEXT]
EPI_STEPS = [u for u in STEPS if u[0] not in NEXT]
PROLOGUE, BODY, EPILOGUE = ([u for u in steps if u[0] in FILLS] for steps in (PRO_STEPS, STEPS, EPI_STEPS))
N_PRO, N_BODY = len(PROLOGUE), len(BODY)
SLOTS = 3
assert N_BODY % SLOTS == 0
assert BODY[-3:] == [("yB",), ("qkB",), ("yA",)]
assert PROLOGUE[-3:] in ([("mA", 0), ("mA", 1), ("qkB",)], [("PA", 3, 1), ("mA", 1), ("qkB",)])


class Ring:

    def __init__(self, section, it):
        self.order, first = {"prologue": (PROLOGUE, 0), "body": (BODY, N_PRO),
                             "epilogue": (EPILOGUE, N_PRO + N_BODY * (ITERS - 1))}[section]
        self.place = {u: first + n for n, u in enumerate(self.order)}
        self.it = it
        self.section = section

    def slot(self, use):
        return self.place[use] % SLOTS

    def before(self, use):
        n = self.order.index(use)
        return self.order[n - SLOTS] if n >= SLOTS else None

    def filled(self, use):
        n = self.place[use] + 1
        return self.it * N_BODY + n if self.section == "body" else n


def build(nc, x, w_q, w_k, w_v, w_o, w_kgen, b_kgen, w_conv, b_conv, ln1_w, ln1_b, w_qkv, w_proj,
          ln2_w, ln2_b, gate_w, gate_b, w1, w2, c_wq, c_wk, c_wv, w_fc, w_pj, consts, by_expert, expert_out, out):
    with ExitStack() as ctx:
        def sb(name, shape, dt=F32):
            return ctx.enter_context(nc.sbuf_tensor(name, shape, dt))

        def sem(name):
            return ctx.enter_context(nc.semaphore(name))

        cst = sb("cst", [P, C_N])
        spread = sb("spread", [P, HG * KT, P], F32R)
        neg_bf = sb("neg_bf", [P, P], BF16)
        acc1 = sb("acc1", [P, NT, D])
        acc2 = sb("acc2", [P, NT, D])
        hT = sb("hT", [P, BATCH * SEQ])
        uT = sb("uT", [P, BATCH * SEQ])
        wqT = sb("wqT", [P, GROUPS, HG, HDA])
        wkT = sb("wkT", [P, GROUPS, HDA])
        w2all = sb("w2all", [P, GROUPS, 2, P])
        wA = sb("wA", [P, HG + 2, HDA])
        wB = sb("wB", [P, 2, P])
        woT = sb("woT", [P, 2 * GROUPS, D])
        wpP = sb("wpP", [P, GROUPS, D])
        v_all = sb("v_all", [P, NT, GROUPS, HDA])
        vb_all = sb("vb_all", [P, NT, GROUPS * HG, HDB])
        QA = sb("QA", [P, HG, SEQ], F32R)
        QS = sb("QS", [P, HG, SEQ], F32R)
        KAh = sb("KAh", [P, SEQ], F32R)
        KS = sb("KS", [P, SEQ], F32R)
        QB = sb("QB", [P, SEQ], F32R)
        KB = sb("KB", [P, SEQ], F32R)
        HB = sb("HB", [P, 2, SEQ], F32R)
        KBj = sb("KBj", [P, HG, SEQ], F32R)
        VA = sb("VA", [P, KT, HDA])
        VB = sb("VB", [P, KT, HG, 32])
        eA = sb("eA", [P, HG, KT, SEQ])
        eB = sb("eB", [P, HG, 2, SEQ])
        maxA = sb("maxA", [P, QT, HG, P], BF16)
        maxB = sb("maxB", [P, QT, P], BF16)
        cr = sb("cr", [P, SEQ])
        cw = sb("cw", [P, SEQ])
        ct = sb("ct", [P, SEQ])
        cf = sb("cf", [P, SEQ])
        cfh = sb("cfh", [P, SEQ], F32R)
        cfl = sb("cfl", [P, SEQ], F32R)
        oB = sb("oB", [P, SEQ])
        rB = sb("rB", [P, SEQ])
        oA = sb("oA", [P, 2, SEQ])
        small = sb("small", [P, 160])
        stat = sb("stat", [P, NT, 6])
        wfcT = sb("wfcT", [P, FF])
        wpjT = sb("wpjT", [P, FB, D])
        cols = sb("cols", [P, 16])
        kgb = sb("kgb", [P, 3])
        gb = sb("gb", [P, EXPERTS])
        gw = sb("gw", [P, EXPERTS])
        c_w = sb("c_w", [P, 3, D])
        ps = ctx.enter_context(nc.psum_tensor("ps", [P, 8, 512], F32))

        ident = cst[:, C_ID:C_ID + P]

        def col(n):
            return cst[:, C_COL + n:C_COL + n + 1]

        eAf = eA[:].rearrange("p a b c -> p (a b c)")
        eBf = eB[:].rearrange("p a b c -> p (a b c)")
        raw = eBf[:, 0:28 * P].rearrange("p (n d) -> p n d", d=D)
        qkv_raw = eBf[:, 28 * P:31 * P]
        kg_raw = eBf[0:3, 31 * P:32 * P]
        xnT = eAf[:, 4096:6144].rearrange("p (b s) -> p b s", b=BATCH)
        wvT = eAf[:, 6144:6400]
        kgT = eAf[:, 6400:6403]
        un = eAf[:, 2048:4096].rearrange("p (n d) -> p n d", d=D)
        ctxb = eAf[:, 6528:7040].rearrange("p (b m) -> p b m", b=BATCH)
        cacc = eAf[:, 0:2048].rearrange("p (b s) -> p b s", b=BATCH)

        s_cst = sem("constants_loaded")
        s_x = sem("x_loaded")
        s_w = sem("weights_loaded")
        s_qkv = sem("qkv_loaded")
        s_col = sem("columns_loaded")
        s_wpj = sem("wproj_loaded")
        s_chain = sem("vector_chain")
        s_pset = sem("gpsimd_constants")
        s_wt = sem("weights_transposed")
        s_wtc = sem("weights_copied")
        s_stat = sem("statistics")
        s_var = sem("variance")
        s_std = sem("deviation")
        s_nrm = sem("normalised")
        s_xt = sem("xn_transposed")
        s_xtc = sem("xn_copied")
        s_ut = sem("ln1_transposed")
        s_utc = sem("ln1_copied")
        s_ctx = sem("context_ready")
        s_dyn = sem("gate_filled")
        s_z = sem("gate_argument")
        s_ez = sem("gate_exponential")
        s_h = sem("conv_ready")
        s_v = sem("values_filled")
        s_vc = sem("values_copied")
        s_va = sem("valuesA_filled")
        s_vac = sem("valuesA_copied")
        s_zt = sem("ln2_transposed")
        s_ztc = sem("ln2_copied")
        s_gl = sem("gate_logits_filled")
        s_hot = sem("one_hot_ready")
        s_yt = sem("norm2_transposed")
        s_ytc = sem("norm2_copied")
        s_vv = sem("L1_values_filled")
        s_vvc = sem("L1_values_copied")

        ring_full = sem("score_tile_filled")
        s_wA = sem("wA_ready")
        s_wB = sem("wB_ready")
        s_VA = sem("VA_ready")
        s_VB = sem("VB_ready")
        s_QS = sem("QS_high_ready")
        s_KAh = sem("KAh_ready")
        s_QAh = sem("QA_high_ready")
        s_QA = sem("QA_low_ready")
        s_KS = sem("KS_ready")
        s_HB = sem("HB_rounded")
        s_KB = sem("KB_ready")
        s_QB = sem("QB_ready")
        s_KBj = sem("KBj_ready")
        s_maxA = sem("maxA_taken")
        s_maxB = sem("maxB_taken")
        s_shA = sem("shiftA_ready")
        s_mtB = sem("shiftB_filled")
        s_QBs = sem("QB_shifted")
        s_eA = sem("eA_ready")
        s_eB = sem("eB_ready")
        s_L = sem("chunk_sums_filled")
        s_ln = sem("logarithm_ready")
        s_r = sem("chunk_reciprocal")
        s_sw = sem("chunk_weight_sum")
        s_tot = sem("total_filled")
        s_c1 = sem("factor_times_sum")
        s_rt = sem("total_reciprocal")
        s_cf = sem("factor_ready")
        s_cfh = sem("factor_high")
        s_cfl = sem("factor_low")
        s_wts = sem("eA_weighted")
        s_ota = sem("outA_filled")
        s_otb = sem("outB_filled")
        s_oA = sem("outA_copied")
        s_oB = sem("outB_copied")
        s_lb = sem("outB_sums_filled")
        s_rB = sem("outB_reciprocal")
        s_yB = sem("outB_scaled")
        s_acc = sem("outputs_added")

        s_zero = sem("scratch_zeroed")
        s_zt0 = sem("zero_tile_ready")
        s_we = sem("expert_weights_loaded")
        s_rk = sem("ranks_filled")
        s_slot = sem("slots_ready")
        s_es = sem("tile_experts_ready")
        s_sc = sem("tokens_scattered")
        s_zg = sem("sorted_tokens_loaded")
        s_sum = sem("layer0_summed")
        s_t1 = sem("sorted_transposed")
        s_zc = sem("sorted_copied")
        s_zs = sem("expert_input_ready")
        s_hf = sem("expert_hidden_filled")
        s_hr = sem("expert_hidden_ready")
        s_ht = sem("expert_hidden_transposed")
        s_hc = sem("expert_hidden_copied")
        s_yf = sem("expert_out_filled")
        s_yo = sem("expert_out_copied")
        s_st = sem("expert_out_stored")
        s_ga = [sem(f"expert_out_gathered{b}") for b in range(BATCH)]
        s_ya = sem("expert_out_added")

        s_lq = sem("L1_qk_filled")
        s_lqc = sem("L1_qk_copied")
        s_ls = sem("L1_scores_filled")
        s_lm = sem("L1_scores_masked")
        s_lx = sem("L1_max_negated")
        s_le = sem("L1_exp_ready")
        s_lt = sem("L1_transposed")
        s_ltc = sem("L1_transposed_copied")
        s_lo = sem("L1_out_filled")
        s_loa = sem("L1_out_added")
        s_fh = sem("ffn_hidden_filled")
        s_fr = sem("ffn_relu_ready")
        s_yc = sem("ffn_out_copied")
        s_cnt = sem("spikes_counted")
        s_lr = sem("L1_reciprocal")
        s_fs = sem("ffn_square_ready")
        s_fy = sem("ffn_out_filled")
        s_sp = sem("spike_step")
        s_fin = sem("batch_finished")
        s_out = sem("stored")

        block = ctx.enter_context(nc.Block())

        zn = eBf[:, 0:2048].rearrange("p (n d) -> p n d", d=D)
        zT = eBf[:, 2048:4096]
        w1e = eAf[:, 0:4096].rearrange("p (e f) -> p e f", e=EXPERTS)
        w2e = eAf[:, 4096:8192].rearrange("p (e n d) -> p e n d", e=EXPERTS, n=FB)
        zg = v_all[:].rearrange("p a b c -> p (a b c)")[:, 0:SLOT_TILES * D].rearrange("p (s d) -> p s d", d=D)
        zs = cr[:, 0:2 * P].rearrange("p (u t) -> p u t", u=2)
        zsT = eBf[:, 0:SLOT_TILES * D].rearrange("p (s t) -> p s t", t=P)
        he = oA
        heT = [cw, ct]
        yo = zsT
        yg = hT[:].rearrange("p (n d) -> p n d", d=D)
        slot = sb("slot", [P, NT], mybir.dt.int32)
        expert_of = sb("expert_of", [P, SLOT_TILES], mybir.dt.int32)
        tot, tiles, upto, first, slot_f = (oB[:, 16 * n:16 * n + 16] for n in range(5))
        cmp = rB
        hot = sb("hot", [P, EXPERTS, NT])
        hot_bf = sb("hot_bf", [P, EXPERTS, NT], BF16)
        before_bf = sb("before_bf", [P, P], BF16)
        ones_bf = sb("ones_bf", [P, P], BF16)
        lg = sb("lg", [P, NT, EXPERTS])
        lge = sb("lge", [P, NT, EXPERTS])
        yn = eAf[:, 0:2048].rearrange("p (n d) -> p n d", d=D)
        ynT = eAf[:, 4096:6144]
        vC = eAf[:, 6144:8192].rearrange("p (n d) -> p n d", d=D)
        qkC = eBf[:, 0:1024].rearrange("p (u t) -> p u t", u=2)
        pC = eBf[:, 1024:3072].rearrange("p (q t) -> p q t", q=QT)
        pT = hT[:, 0:1280].rearrange("p (n t) -> p n t", n=10)
        fr = uT[:].rearrange("p (n t) -> p n t", n=FB)
        lif = v_all[:].rearrange("p a b c -> p (a b c)")


        MEAN, VAR, STD, RSTD, CTX, DYN, GATE, DIF = 16, 32, 48, 64, 80, 96, 128, 144

        def score_c(q):
            return ps[:, (5, 7, 0, 1)[q], 0:P * (q + 1)]

        spk = [lif[:, 512 * n:512 * n + 512] for n in range(5)]
        neg, tmp, ysp = (lif[:, 512 * n:512 * n + 512] for n in range(5, 8))
        cnt = vb_all[:].rearrange("p a b c -> p (a b c)")[:, 0:512]

        x_v = x.rearrange("b (n p) d -> p (b n) d", p=P)
        out_v = out.rearrange("b (n p) d -> b p n d", p=P)
        N_COLS = 12
        N_PSET = 5 + 5 + 2 * 3 * GROUPS

        @block.sync
        def _(sp):
            for b in range(BATCH):
                sp.dma_start(acc1[:, b * QT:(b + 1) * QT, :], x_v[:, b * QT:(b + 1) * QT, :]).then_inc(s_x, 16)
            sp.dma_start(raw[:, 0:8, :], w_q.rearrange("(n p) d -> p n d", p=P)).then_inc(s_w, 16)
            sp.dma_start(raw[:, 8:10, :], w_k.rearrange("(n p) d -> p n d", p=P)).then_inc(s_w, 16)
            sp.dma_start(raw[:, 10:12, :], w_v.rearrange("(n p) d -> p n d", p=P)).then_inc(s_w, 16)
            sp.dma_start(raw[:, 12:20, :], w_o.rearrange("o (n d) -> o n d", d=P)).then_inc(s_w, 16)
            sp.dma_start(raw[:, 20:24, :], w_fc.rearrange("(n p) d -> p n d", p=P)).then_inc(s_w, 16)
            sp.dma_start(raw[:, 24:28, :], w_pj.rearrange("o (n d) -> o n d", d=P)).then_inc(s_w, 16)
            sp.dma_start(kg_raw, w_kgen).then_inc(s_w, 16)

            sp.wait_ge(s_oA, 2 * ITERS + 2)
            for e in range(0, EXPERTS, 4):
                sp.dma_start(w1e[:, e:e + 4], w1[e:e + 4].rearrange("e d f -> d e f")).then_inc(s_we, 16)
                sp.dma_start(w2e[:, e:e + 4], w2[e:e + 4].rearrange("e (n p) d -> p e n d", p=P)).then_inc(s_we, 16)
            sp.wait_ge(s_sc, 16 * NT)
            for n in range(0, SLOT_TILES, 8):
                sp.dma_start(zg[:, n:n + 8, :], by_expert.rearrange("(s p) d -> p s d", p=P)[:, n:n + 8, :]).then_inc(s_zg, 16)
            with sp.Fori(0, SLOT_TILES // 4) as i:
                sp.wait_ge(s_yo, i * 4 + 6)
                sp.dma_start(expert_out.rearrange("(i u p) d -> i p u d", p=P, u=4)[i], yo[:, bass.ds(i * 4, 4), :]).then_inc(s_st, 16)
            with sp.Fori(0, BATCH) as b:
                sp.wait_ge(s_fin, b + 2)
                sp.dma_start(out_v[b], acc1[:, bass.ds(b * QT, QT), :]).then_inc(s_out, 16)
            sp.wait_ge(s_out, 16 * BATCH)

        @block.gpsimd
        def _(pool):
            g = nc.gpsimd
            g.memset(cw[:, 0:P], 0.0).then_inc(s_zt0, 1)
            pool.wait_ge(s_zt0, 1)
            g.dma_start(by_expert.rearrange("(s p) d -> p s d", p=P),
                        cw[:, 0:P].unsqueeze(1).broadcast_to([P, SLOT_TILES, P])).then_inc(s_zero, 16)
            g.memset(wpP[:], 0.0).then_inc(s_pset, 1)
            g.memset(w2all[:], 0.0).then_inc(s_pset, 1)
            g.memset(VB[:], 1.0).then_inc(s_pset, 1)
            g.memset(maxA[:], 0.0).then_inc(s_pset, 1)
            g.memset(maxB[:], 0.0).then_inc(s_pset, 1)
            pool.wait_ge(s_pset, 5)
            wp_v = w_proj.rearrange("(g j i) d -> j i g d", j=HG, i=HDB)
            for j in range(HG):
                g.dma_start(wpP[32 * j:32 * j + HDB, :, :], wp_v[j]).then_inc(s_wpj, 16)
            pool.wait_ge(s_cst, 16)
            pick = ident.rearrange("p (j r) -> p j r", r=32)
            def keys(rows):
                return pick[:, :, rows:rows + NCH].unsqueeze(3).broadcast_to([P, HG, NCH, CH])
            g.tensor_copy(KS[64:96, :].rearrange("p (c m) -> p c m", m=CH),
                          ident[64:96, 64:64 + NCH].unsqueeze(2).broadcast_to([32, NCH, CH])).then_inc(s_pset, 1)
            pool.wait_ge(s_pset, 6)
            g.tensor_tensor(spread[:].rearrange("p (j a) (b m) -> p j (a b) m", j=HG, b=2), keys(0), keys(NCH),
                            ALU.add).then_inc(s_pset, 1)
            g.tensor_copy(neg_bf[:], cst[:, C_NEG:C_NEG + P]).then_inc(s_pset, 1)
            g.tensor_copy(before_bf[:], cst[:, C_BEFORE:C_BEFORE + P]).then_inc(s_pset, 1)
            g.memset(ones_bf[:], 1.0).then_inc(s_pset, 1)
            pool.wait_ge(s_qkv, 16)
            for k in range(2):
                src = qkv_raw[:, k * P:(k + 1) * P].rearrange("p (a e) -> p a e", e=HDB)
                for r in range(3):
                    dst = w2all[:, :, k, :].rearrange("p g (j m) -> p g j m", m=32)[:, :, :, 1 + HDB * r:1 + HDB * (r + 1)]
                    for q in range(GROUPS):
                        g.tensor_copy(dst[:, q], src[:, HG * q:HG * q + HG, :]).then_inc(s_pset, 1)

            def copy_wA(g_idx):
                q = wqT[:, bass.ds(g_idx, 1), :, :].rearrange("p g h e -> p (g h) e")
                k = wkT[:, bass.ds(g_idx, 1), :]
                g.tensor_copy(wA[:, 0:HG, :], q).then_inc(s_wA, 1)
                for c in range(2):
                    g.tensor_copy(wA[:, HG + c:HG + c + 1, :], k).then_inc(s_wA, 1)

            def copy_wB(g_idx):
                g.tensor_copy(wB[:], w2all[:, bass.ds(g_idx, 1), :, :].rearrange("p g k c -> p (g k) c")).then_inc(s_wB, 1)

            def keys_b(count):
                pool.wait_ge(s_pset, N_PSET)
                pool.wait_ge(s_KB, count)
                for j in range(HG):
                    g.tensor_scalar(KBj[:, j, :], KB[:].bitcast(F32), col(4 + j), col(8 + j), ALU.mult,
                                    ALU.add).then_inc(s_KBj, 1)

            def body(it, nxt):
                g_idx = it % GROUPS
                b_idx = it // GROUPS
                pool.wait_ge(s_oB, it + 1)
                g.tensor_copy(VB[:, :, :, 0:HDB],
                              vb_all[:, bass.ds(b_idx * QT, QT), bass.ds(g_idx * HG, HG), :]).then_inc(s_VB, 1)
                pool.wait_ge(s_oA, it * 2 + 2)
                g.tensor_copy(VA[:], v_all[:, bass.ds(b_idx * QT, QT), bass.ds(g_idx, 1), :]
                              .rearrange("p t g e -> p t (g e)")).then_inc(s_VA, 1)
                if nxt:
                    pool.wait_ge(s_HB, it + 1)
                    copy_wB((it + 1) % GROUPS)
                pool.wait_ge(s_sw, it + 1)
                g.tensor_tensor(cr[:], cr[:], cw[:], ALU.mult).then_inc(s_c1, 1)
                if nxt:
                    pool.wait_ge(s_KAh, it + 2)
                    copy_wA((it + 2) % GROUPS)
                    keys_b(it + 2)

            pool.wait_ge(s_wtc, 9)
            pool.wait_ge(s_pset, N_PSET)
            copy_wA(0)
            copy_wB(0)
            pool.wait_ge(s_KAh, 1)
            copy_wA(1)
            keys_b(1)
            pool.wait_ge(s_vc, 4)
            pool.wait_ge(s_vac, 8)
            pool.wait_ge(s_zero, 16)
            with g.Fori(0, ITERS - 1) as it:
                body(it, True)
            body(ITERS - 1, False)
            pool.wait_ge(s_wpj, 16 * HG)
            pool.wait_ge(s_slot, 1)
            pool.wait_ge(s_nrm, 3 * NT)
            for n in range(NT):
                g.indirect_dma_start(by_expert, bass.IndirectOffsetOnAxis(slot[:, n:n + 1], 0), zn[:, n, :],
                                     None).then_inc(s_sc, 16)
            pool.wait_ge(s_acc, 2 * ITERS + 2)
            g.tensor_tensor(acc1[:], acc1[:], acc2[:], ALU.add).then_inc(s_sum, 1)
            pool.wait_ge(s_sc, 16 * NT)
            pool.wait_ge(s_zc, SLOT_TILES // 4)
            with g.Fori(0, SLOT_TILES // 2) as i:
                for u in range(2):
                    pool.wait_ge(s_hf, i * 2 + (u + 1))
                    g.tensor_copy(zs[:, u, :], zsT[:, bass.ds(i * 2 + u, 1), :].rearrange("p s t -> p (s t)")).then_inc(s_zs, 1)
            pool.wait_ge(s_st, 16 * (SLOT_TILES // 4))
            for n in range(NT):
                g.indirect_dma_start(yg[:, n, :], None, expert_out,
                                     bass.IndirectOffsetOnAxis(slot[:, n:n + 1], 0)).then_inc(s_ga[n // QT], 16)
            for b in range(BATCH):
                pool.wait_ge(s_ga[b], 16 * QT)

            g.sem_inc(s_fin, 1)
            with g.Fori(0, BATCH) as b:
                pool.wait_ge(s_fin, b + 1)
                for n in range(1, 5):
                    pool.wait_ge(s_sp, b * 14 + (3 * n + 16))
                    if n > 1:
                        pool.wait_ge(s_cnt, b * 5 + (n + 4))
                    g.tensor_tensor(cnt, spk[0] if n == 1 else cnt, spk[n], ALU.add).then_inc(s_cnt, 1)
                pool.wait_ge(s_cnt, b * 5 + 9)
                g.tensor_tensor(cnt, cnt, col(23).broadcast_to([P, SEQ]), ALU.mult).then_inc(s_cnt, 1)
                pool.wait_ge(s_cnt, b * 5 + 10)
                pool.wait_ge(s_loa, b * 4 + 8)
                a = acc1[:, bass.ds(b * QT, QT), :]
                g.tensor_tensor(a, a, cnt.rearrange("p (q d) -> p q d", q=QT), ALU.add).then_inc(s_fin, 1)

        @block.scalar
        def _(act):
            s = nc.scalar
            act.dma_start(cst[:], consts).then_inc(s_cst, 16)
            act.dma_start(qkv_raw, w_qkv).then_inc(s_qkv, 16)
            act.dma_start(cols[:, 0:3], w_conv.rearrange("d a k -> d (a k)")).then_inc(s_col, 16)
            for n, a in enumerate((b_conv, ln1_w, ln1_b, ln2_w, ln2_b)):
                act.dma_start(cols[:, 3 + n:4 + n], a.rearrange("(d a) -> d a", a=1)).then_inc(s_col, 16)
            act.dma_start(kgb[:], b_kgen.partition_broadcast(P)).then_inc(s_col, 16)
            act.dma_start(gb[:], gate_b.partition_broadcast(P)).then_inc(s_col, 16)
            act.dma_start(gw[:], gate_w).then_inc(s_col, 16)
            for n, a in enumerate((c_wq, c_wk, c_wv)):
                act.dma_start(c_w[:, n, :], a).then_inc(s_col, 16)

            def deviation(n):
                act.wait_ge(s_var, n + 1)
                s.activation(small[:, STD:STD + NT], small[:, VAR:VAR + NT], ACT.Sqrt, bias=col(21)).then_inc(s_std, 1)

            act.wait_ge(s_cst, 16)
            deviation(0)
            act.wait_ge(s_wt, 1)
            s.copy(wqT[:, 0:2], ps[:, 0, :].rearrange("p (g h e) -> p g h e", g=2, h=HG)).then_inc(s_wtc, 1)
            act.wait_ge(s_wt, 2)
            s.copy(wqT[:, 2:4], ps[:, 1, :].rearrange("p (g h e) -> p g h e", g=2, h=HG)).then_inc(s_wtc, 1)
            act.wait_ge(s_wt, 3)
            s.copy(wkT[:], ps[:, 2, 0:256].rearrange("p (g e) -> p g e", g=GROUPS)).then_inc(s_wtc, 1)
            s.copy(wvT, ps[:, 2, 256:512]).then_inc(s_wtc, 1)
            for n in range(2):
                act.wait_ge(s_wt, 4 + n)
                s.copy(woT[:, 4 * n:4 * n + 4, :], ps[:, 3 + n, :].rearrange("p (n d) -> p n d", n=4)).then_inc(s_wtc, 1)
            act.wait_ge(s_wt, 6)
            s.copy(wfcT[:], ps[:, 5, :]).then_inc(s_wtc, 1)
            act.wait_ge(s_wt, 7)
            s.copy(wpjT[:], ps[:, 6, :].rearrange("p (n d) -> p n d", n=4)).then_inc(s_wtc, 1)
            act.wait_ge(s_wt, 8)
            s.copy(kgT, ps[:, 7, 0:3]).then_inc(s_wtc, 1)
            for b in range(BATCH):
                act.wait_ge(s_xt, b + 1)
                s.activation(xnT[:, b, :], ps[:, b, :], ACT.Copy, accum_out=small[:, CTX + b:CTX + b + 1]).then_inc(s_xtc, 1)
            deviation(1)
            s.preload_act_table_set("natural_log_exp_and_others")
            act.wait_ge(s_col, 16 * N_COLS)
            for b in range(BATCH):
                act.wait_ge(s_ut, b + 1)
                s.activation(uT[:, b * SEQ:(b + 1) * SEQ], ps[:, 4 + b, :], ACT.Identity, scale=cols[:, 4:5],
                             bias=cols[:, 5:6]).then_inc(s_utc, 1)
            act.wait_ge(s_z, 1)
            s.activation(small[:, DYN:DYN + 12], small[:, DYN:DYN + 12], ACT.Exp, scale=-1.0).then_inc(s_ez, 1)
            for n in range(4):
                act.wait_ge(s_v, n + 1)
                s.copy(vb_all[:, 4 * n:4 * n + 4].rearrange("p t h e -> p (t h e)"), ps[:, n, :]).then_inc(s_vc, 1)

            def tile(ring, use):
                r = ring.slot(use)
                return ps[:, 2 * r:2 * r + 2, :]

            def reciprocal(dst, src, count, bias, out_sem):
                s.activation(dst, src, ACT.Ln, bias=bias).then_inc(s_ln, 1)
                act.wait_ge(s_ln, count)
                s.activation(dst, dst, ACT.Exp, scale=-1.0).then_inc(out_sem, 1)

            def steps(which, it, ring):
                for use in which:
                    kind = use[0]
                    if kind in FILLS and kind not in ("PB", "PA", "BC", "yA", "yB"):
                        t = tile(ring, use)
                        act.wait_ge(ring_full, ring.filled(use))
                    if kind == "SA":
                        _, j, h = use
                        s.activation(eA[:, j, 2 * h:2 * h + 2, :], t, ACT.Exp, scale=SCALE_A).then_inc(s_eA, 1)
                    elif kind == "SB":
                        _, j, h = use
                        s.activation(eB[:, j, :, :], t, ACT.Exp, scale=SCALE_B).then_inc(s_eB, 1)
                    elif kind == "r":
                        act.wait_ge(s_L, it + 1)
                        reciprocal(cr[:], ps[:, 6, :], it * 3 + 1, 0.0, s_r)
                    elif kind == "ct":
                        act.wait_ge(s_tot, it + 1)
                        reciprocal(ct[:], ps[:, 6, :], it * 3 + 2, col(20), s_rt)
                    elif kind == "rB":
                        act.wait_ge(s_lb, it + 1)
                        reciprocal(rB[:], ps[:, 7, :], it * 3 + 3, 0.0, s_rB)
                    elif kind == "cfh":
                        act.wait_ge(s_cf, it + 1)
                        s.copy(cfh[:], cf[:]).then_inc(s_cfh, 1)
                    elif kind == "oB":
                        act.wait_ge(s_otb, it + 1)
                        s.copy(oB[:], ps[:, 7, :]).then_inc(s_oB, 1)
                    elif kind == "oA":
                        act.wait_ge(s_ota, it * 2 + (use[1] + 1))
                        s.copy(oA[:, use[1], :], ps[:, 6, :]).then_inc(s_oA, 1)
                    elif kind == "qA":
                        p = use[1]
                        for q in range(2):
                            s.copy(QS[0:64, 2 * p + q, :], t[64 * q:64 * q + 64, 0, :]).then_inc(s_QS, 1)
                        act.wait_ge(s_QS, it * 4 + (2 * p + 6))
                        s.copy(QA[0:64, 2 * p:2 * p + 2, :], QS[0:64, 2 * p:2 * p + 2, :].bitcast(F32)).then_inc(s_QAh, 1)
                    elif kind == "kA":
                        s.copy(KAh[:], t[:, 0, :]).then_inc(s_KAh, 1)
                    elif kind == "mA":
                        s.copy(QS[64:96, 2 * use[1]:2 * use[1] + 2, :], t[64:96]).then_inc(s_shA, 1)
                    elif kind == "qkB":
                        s.copy(HB[:], t).then_inc(s_HB, 1)

            s.sem_inc(s_oB, 1)
            s.sem_inc(s_oA, 1)
            s.sem_inc(s_oA, 1)
            s.sem_inc(s_rB, 1)
            n = 0
            for use in PRO_STEPS:
                steps([use], -1, Ring("prologue", 0))
                if use[0] == "PA":
                    act.wait_ge(s_va, n + 1)
                    s.copy(v_all[:, 2 * n:2 * n + 2], ps[:, 6 + n % 2, :].rearrange("p (t g e) -> p t g e", t=2, g=GROUPS)).then_inc(s_vac, 1)
                    n += 1
            with act.Fori(0, ITERS - 1) as it:
                steps(STEPS, it, Ring("body", it))
            steps(EPI_STEPS, ITERS - 1, Ring("epilogue", ITERS - 1))

            deviation(2)
            s.preload_act_table(ACT.Gelu_apprx_tanh)
            for b in range(BATCH):
                act.wait_ge(s_zt, b + 1)
                s.activation(zT[:, b * SEQ:(b + 1) * SEQ], ps[:, b, :], ACT.Identity, scale=cols[:, 6:7],
                             bias=cols[:, 7:8]).then_inc(s_ztc, 1)

            for n in range(SLOT_TILES // 4):
                act.wait_ge(s_t1, n + 1)
                s.activation(zsT[:, 4 * n:4 * n + 4, :], ps[:, n, :].rearrange("p (n t) -> p n t", n=4), ACT.Identity,
                             scale=cols[:, 6:7], bias=cols[:, 7:8]).then_inc(s_zc, 1)
            s.sem_inc(s_hr, 1)
            s.sem_inc(s_hr, 1)
            with act.Fori(0, SLOT_TILES // 2) as i:
                for u in range(2):
                    act.wait_ge(s_hf, i * 2 + (u + 3))
                    s.activation(he[:, u, :], ps[:, 2 + u, :], ACT.Gelu_apprx_tanh).then_inc(s_hr, 1)

            deviation(3)
            for b in range(BATCH):
                act.wait_ge(s_yt, b + 1)
                s.copy(ynT[:, b * SEQ:(b + 1) * SEQ], ps[:, b, :]).then_inc(s_ytc, 1)
            for n in range(4):
                act.wait_ge(s_vv, n + 1)
                s.copy(vC[:, 4 * n:4 * n + 4, :], ps[:, 4 + n, :].rearrange("p (n d) -> p n d", n=4)).then_inc(s_vvc, 1)
            s.preload_act_table(ACT.Exp)
            with act.Fori(0, BATCH) as b:
                act.wait_ge(s_lq, b + 1)
                s.copy(qkC, ps[:, 0:2, :]).then_inc(s_lqc, 1)
                for f in range(2):
                    act.wait_ge(s_fh, b * 2 + (f + 1))
                    s.activation(fr[:, 2 * f:2 * f + 2, :], ps[:, 2 + 2 * f:4 + 2 * f, :], ACT.Relu).then_inc(s_fr, 1)
                for f in range(2):
                    act.wait_ge(s_fr, b * 2 + (f + 1))
                    s.activation(fr[:, 2 * f:2 * f + 2, :], fr[:, 2 * f:2 * f + 2, :], ACT.Square).then_inc(s_fs, 1)
                for q in range(QT):
                    act.wait_ge(s_lx, b * 4 + (q + 1))
                    s.activation(pC[:, q, 0:P * (q + 1)], score_c(q), ACT.Exp, scale=SCALE_C, bias=small[:, q:q + 1],
                                 accum_out=small[:, 4 + q:5 + q]).then_inc(s_le, 1)
                act.wait_ge(s_fy, b + 1)
                act.wait_ge(s_sp, b * 14 + 14)
                s.copy(ysp, ps[:, 6, :]).then_inc(s_yc, 1)
                act.wait_ge(s_lt, b + 1)
                s.copy(pT[:, 0:8, :], ps[:, 2:4, :].rearrange("p b (n t) -> p (b n) t", n=4)).then_inc(s_ltc, 1)
                s.copy(pT[:, 8:10, :], ps[:, 4, 0:256].rearrange("p (n t) -> p n t", n=2)).then_inc(s_ltc, 1)

        @block.tensor
        def _(pe):
            t = nc.tensor
            pe.wait_ge(s_cst, 16)
            pe.wait_ge(s_w, 16 * 7)
            for bank in range(7):
                for n in range(4):
                    m = t.transpose(ps[:, bank, n * P:(n + 1) * P], raw[:, 4 * bank + n, :], ident)
                m.then_inc(s_wt, 1)
            t.transpose(ps[:, 7, 0:3], kg_raw, ident[0:3, 0:3]).then_inc(s_wt, 1)

            def transposed(src, bank, n):
                for q in range(4):
                    m = t.transpose(ps[:, bank, q * P:(q + 1) * P], src[:, 4 * n + q, :], ident)
                return m

            pe.wait_ge(s_wtc, 9)
            for n in range(4):
                pe.wait_ge(s_nrm, 4 * n + 4)
                transposed(acc2, n, n).then_inc(s_xt, 1)
            for n in range(4):
                pe.wait_ge(s_nrm, NT + 4 * n + 4)
                transposed(un, 4 + n, n).then_inc(s_ut, 1)
            for n in range(4):
                pe.wait_ge(s_xtc, n + 1)
                pe.wait_ge(s_utc, n + 1)
                for q in range(4):
                    k = 4 * n + q
                    m = t.matmul(ps[:, n, P * q:P * q + P], uT[:, k * P:(k + 1) * P], qkv_raw[:, 256:384],
                                 start=True, stop=True)
                m.then_inc(s_v, 1)
            pe.wait_ge(s_ctx, 1)
            for b in range(BATCH):
                m = t.matmul(ps[:, 4, 3 * b:3 * b + 3], ctxb[:, b, :], kgT, start=True, stop=True)
            m.then_inc(s_dyn, 1)

            def values_a_all(n):
                if n >= 2:
                    pe.wait_ge(s_vac, n - 1)
                for q in range(2):
                    k = 2 * n + q
                    m = t.matmul(ps[:, 6 + n % 2, 256 * q:256 * q + 256], hT[:, k * P:(k + 1) * P], wvT, start=True, stop=True)
                m.then_inc(s_va, 1)

            def consumed(use, it):
                kind = use[0]
                if kind in ("SA", "PA", "PB", "BC"):
                    sema = {"SA": s_eA, "PA": s_maxA, "PB": s_maxB, "BC": s_wts}[kind]
                    return sema, it * 8 + (2 * use[1] + use[2] + 1 + 8 * (kind == "PA"))
                if kind == "SB":
                    return s_eB, it * 8 + (HG * use[2] + use[1] + 1)
                if kind == "mA":
                    return s_shA, it * 2 + (use[1] + 3)
                if kind == "qA":
                    return s_QA, it * 4 + (2 * use[1] + 6)
                return {"kA": (s_KS, it + 2), "qkB": (s_QB, it + 2), "yB": (s_acc, it * 2 + 3),
                        "yA": (s_acc, it * 2 + 4)}[kind]

            def open_tile(ring, use, it):
                last = ring.before(use)
                if last is not None:
                    pe.wait_ge(*consumed(last, it))
                elif ring.section == "prologue":
                    pe.wait_ge(s_vc, 4)
                else:
                    n = ring.order.index(use)
                    if n == 0:
                        pe.wait_ge(s_shA, it * 2 + 2)
                    if n == 1:
                        pe.wait_ge(s_QB, it + 1)
                    else:
                        pe.wait_ge(s_acc, it * 2 + (1 + n // 2))
                r = ring.slot(use)
                return ps[:, 2 * r:2 * r + 2, :]

            def negated_rows(dst, src, q):
                return t.matmul(dst[:, q * P:(q + 1) * P], src, neg_bf[:], start=True, stop=True)

            def steps(which, it, ring):
                g_idx = it % GROUPS
                for use in which:
                    kind = use[0]
                    if kind in FILLS:
                        tile = open_tile(ring, use, it)
                    if kind == "SA":
                        _, j, h = use
                        if h == 0:
                            pe.wait_ge(s_shA, it * 2 + (j // 2 + 1))
                            pe.wait_ge(s_KS, it + 1)
                        for q in range(2):
                            kt = 2 * h + q
                            t.matmul(tile[:, q, :], KAh[:, kt * P:(kt + 1) * P], QA[:, j, :], start=True, stop=False)
                            mm = t.matmul(tile[:, q, :], KS[0:96, kt * P:(kt + 1) * P], QS[0:96, j, :], start=False, stop=True)
                    elif kind == "PB":
                        _, j, h = use
                        if (j, h) == (0, 0):
                            pe.wait_ge(s_QB, it + 1)
                        if h == 0:
                            pe.wait_ge(s_KBj, it * 4 + (j + 1))
                        for q in range(2):
                            k = 2 * h + q
                            mm = t.matmul(tile[:, q, :], QB[:, k * P:(k + 1) * P], KBj[:, j, :], start=True, stop=True)
                    elif kind == "L":
                        pe.wait_ge(s_oA, it * 2 + 2)
                        pe.wait_ge(s_eA, it * 8 + 8)
                        for kt in range(KT):
                            for j in range(HG):
                                mm = t.matmul(ps[32 * j:32 * j + 32, 6, :], cst[:, C_SELL + 32 * kt:C_SELL + 32 * kt + 32],
                                              eA[:, j, kt, :], start=(kt == 0), stop=(kt == KT - 1))
                        mm.then_inc(s_L, 1)
                    elif kind == "TOT":
                        pe.wait_ge(s_sw, it + 1)
                        t.matmul(ps[:, 6, :], cst[:, C_BD:C_BD + P], cw[:], start=True, stop=True).then_inc(s_tot, 1)
                    elif kind == "mB":
                        pe.wait_ge(s_rB, it + 1)
                        pe.wait_ge(s_maxB, it * 8 + 8)
                        for q in range(QT):
                            mm = negated_rows(ps[:, 7, :], maxB[:, q, :], q)
                        mm.then_inc(s_mtB, 1)
                    elif kind == "VB":
                        h = use[1]
                        if h == 0:
                            pe.wait_ge(s_QBs, it + 1)
                            pe.wait_ge(s_VB, it + 1)
                        pe.wait_ge(s_eB, it * 8 + (HG * h + HG))
                        for q in range(2):
                            kt = 2 * h + q
                            for j in range(HG):
                                mm = t.matmul(ps[32 * j:32 * j + 32, 7, :], VB[:, kt, j, :], eB[:, j, q, :],
                                              start=(kt == 0), stop=(kt == KT - 1))
                        if h == 1:
                            mm.then_inc(s_otb, 1)
                    elif kind == "LB":
                        pe.wait_ge(s_oB, it + 2)
                        t.matmul(ps[:, 7, :], cst[:, C_SELB:C_SELB + P], oB[:], start=True, stop=True).then_inc(s_lb, 1)
                    elif kind == "VA":
                        p = use[1]
                        if p == 0:
                            pe.wait_ge(s_rt, it + 1)
                            pe.wait_ge(s_VA, it + 1)
                        else:
                            pe.wait_ge(s_oA, it * 2 + 3)
                        pe.wait_ge(s_wts, it * 8 + (4 * p + 4))
                        for kt in range(KT):
                            for q in range(2):
                                mm = t.matmul(ps[64 * q:64 * q + 64, 6, :], VA[:, kt, :], eA[:, 2 * p + q, kt, :],
                                              start=(kt == 0), stop=(kt == KT - 1))
                        mm.then_inc(s_ota, 1)
                    elif kind == "BC":
                        _, j, h = use
                        if (j, h) == (0, 0):
                            pe.wait_ge(s_cfl, it + 1)
                        for q in range(2):
                            mm = t.matmul(tile[:, q, :], spread[:, KT * j + 2 * h + q, :], cfl[:], start=True, stop=True)
                    elif kind == "SB":
                        _, j, h = use
                        if (j, h) == (0, 0):
                            pe.wait_ge(s_QBs, it + 1)
                        for q in range(2):
                            kt = 2 * h + q
                            mm = t.matmul(tile[:, q, :], KBj[:, j, kt * P:(kt + 1) * P], QB[:], start=True, stop=True)
                    elif kind == "qA":
                        p = use[1]
                        if p == 0:
                            pe.wait_ge(s_wA, it * 3 + 6)
                        mm = t.matmul(tile[:, 0, :], wA[:, 2 * p:2 * p + 2].rearrange("p c e -> p (c e)"),
                                      hT[:, bass.ds((it + 1) // GROUPS * SEQ, SEQ)], start=True, stop=True)
                    elif kind == "kA":
                        mm = t.matmul(tile[:, 0, :], wA[:, HG:HG + 2].rearrange("p c e -> p (c e)"),
                                      hT[:, bass.ds((it + 1) // GROUPS * SEQ, SEQ)], start=True, stop=True)
                    elif kind == "qkB":
                        pe.wait_ge(s_wB, it + 2)
                        for k in range(2):
                            mm = t.matmul(tile[:, k, :], wB[:, k, :], uT[:, bass.ds((it + 1) // GROUPS * SEQ, SEQ)],
                                          start=True, stop=True)
                    elif kind == "PA":
                        _, j, h = use
                        if h == 0:
                            pe.wait_ge(s_QA, it * 4 + (2 * (j // 2) + 6))
                            pe.wait_ge(s_QAh, it * 2 + (j // 2 + 3))
                            pe.wait_ge(s_KAh, it + 2)
                        for q in range(2):
                            k = 2 * h + q
                            mm = t.matmul(tile[:, q, :], QA[:, j, k * P:(k + 1) * P], KAh[:], start=True, stop=True)
                    elif kind == "mA":
                        p = use[1]
                        pe.wait_ge(s_maxA, it * 8 + (4 * p + 12))
                        for j in range(2):
                            for q in range(QT):
                                mm = negated_rows(tile[:, j, :], maxA[:, q, 2 * p + j, :], q)
                    elif kind == "yB":
                        pe.wait_ge(s_yB, it + 1)
                        for q in range(QT):
                            mm = t.matmul(tile[:, 0, q * P:(q + 1) * P], oB[:, q * P:(q + 1) * P],
                                          wpP[:, bass.ds(g_idx, 1), :].rearrange("p n d -> p (n d)"), start=True, stop=True)
                    elif kind == "yA":
                        pe.wait_ge(s_oA, it * 2 + 4)
                        for q in range(QT):
                            for p in range(2):
                                mm = t.matmul(tile[:, 0, q * P:(q + 1) * P], oA[:, p, q * P:(q + 1) * P],
                                              woT[:, bass.ds(g_idx * 2 + p, 1), :].rearrange("p n d -> p (n d)"),
                                              start=(p == 0), stop=(p == 1))
                    if kind in FILLS:
                        mm.then_inc(ring_full, 1)

            pe.wait_ge(s_pset, N_PSET)
            pe.wait_ge(s_z, 1)
            pe.wait_ge(s_h, BATCH)
            n = 0
            for use in PRO_STEPS:
                steps([use], -1, Ring("prologue", 0))
                if use[0] == "PA":
                    values_a_all(n)
                    n += 1
            pe.wait_ge(s_vac, 8)
            pe.wait_ge(s_wpj, 16 * HG)
            with pe.Fori(0, ITERS - 1) as it:
                steps(STEPS, it, Ring("body", it))
            steps(EPI_STEPS, ITERS - 1, Ring("epilogue", ITERS - 1))

            for n in range(4):
                pe.wait_ge(s_nrm, 2 * NT + 4 * n + 4)
                if n == 0:
                    pe.wait_ge(s_acc, 2 * ITERS + 2)
                transposed(zn, n, n).then_inc(s_zt, 1)
            for n in range(NT):
                if n % QT == 0:
                    pe.wait_ge(s_ztc, n // QT + 1)
                m = t.matmul(ps[:, 4, 8 * n:8 * n + 8], zT[:, n * P:(n + 1) * P], gw[:], start=True, stop=True)
            m.then_inc(s_gl, 1)
            pe.wait_ge(s_hot, 2)
            ranks = ps[:, 5, 0:P].rearrange("p (e n) -> p e n", e=EXPERTS)
            t.matmul(ranks, before_bf[:], hot_bf[:], start=True, stop=False)
            for n in range(NT - 1):
                t.matmul(ranks[:, :, n + 1:NT], ones_bf[:], hot_bf[:, :, n:n + 1].broadcast_to([P, EXPERTS, NT - 1 - n]),
                         start=False, stop=(n == NT - 2))
            t.matmul(ps[:, 6, 0:P], ones_bf[:], hot_bf[:].rearrange("p e n -> p (e n)"), start=True, stop=True).then_inc(s_rk, 1)

            def hidden(i, u, which):
                pe.wait_ge(s_zs, i * 4 + (u + 1))
                pe.wait_ge(s_hr, i * 4 + (u + 1))
                t.matmul(ps[:, 2 + u % 2, :], zs[:, u % 2, :], w1e[:, bass.ds(which, 1), :].rearrange("p e f -> p (e f)"),
                         start=True, stop=True).then_inc(s_hf, 1)

            def hidden_transposed(i, u):
                pe.wait_ge(s_hc, i * 4 + (u + 1))
                pe.wait_ge(s_hr, i * 4 + (u + 3))
                for f in range(FB):
                    mm = t.transpose(ps[:, 4 + u % 2, f * P:(f + 1) * P], he[:, u % 2, f * P:(f + 1) * P], ident)
                mm.then_inc(s_ht, 1)

            def expert_output(i, u, which):
                pe.wait_ge(s_yo, i * 4 + (u + 1))
                pe.wait_ge(s_hc, i * 4 + (u + 3))
                for f in range(FB):
                    mm = t.matmul(ps[:, 6 + u % 2, 0:P], heT[u % 2][:, f * P:(f + 1) * P],
                                  w2e[:, bass.ds(which, 1), f, :].rearrange("p e d -> p (e d)"), start=(f == 0), stop=(f == FB - 1))
                mm.then_inc(s_yf, 1)

            pe.wait_ge(s_zg, 16 * 3)
            pe.wait_ge(s_we, 16 * 4)
            pe.wait_ge(s_es, 1)
            for n in range(SLOT_TILES // 4):
                for q in range(4):
                    m = t.transpose(ps[:, n, q * P:(q + 1) * P], zg[:, 4 * n + q, :], ident)
                m.then_inc(s_t1, 1)
            pe.wait_ge(s_zc, SLOT_TILES // 4)
            t.sem_inc(s_hf, 1)
            t.sem_inc(s_hf, 1)
            with pe.Fori(0, SLOT_TILES // 4) as i:
                _, which = nc.values_load_multi_w_load_instructions(expert_of[0:1, bass.ds(i * 4, 4)], engines=(mybir.EngineType.PE,),
                                                                    min_val=0, max_val=EXPERTS - 1)
                hidden(i, 0, which[0])
                hidden(i, 1, which[1])
                hidden_transposed(i, 0)
                for u in range(2, 4):
                    hidden(i, u, which[u])
                    hidden_transposed(i, u - 1)
                    expert_output(i, u - 2, which[u - 2])
                hidden_transposed(i, 3)
                expert_output(i, 2, which[2])
                expert_output(i, 3, which[3])

            for n in range(4):
                pe.wait_ge(s_nrm, 3 * NT + 4 * n + 4)
                transposed(yn, n, n).then_inc(s_yt, 1)
            pe.wait_ge(s_ytc, BATCH)
            for n in range(4):
                for q in range(4):
                    k = 4 * n + q
                    m = t.matmul(ps[:, 4 + n, P * q:P * q + P], ynT[:, k * P:(k + 1) * P], c_w[:, 2, :], start=True, stop=True)
                m.then_inc(s_vv, 1)
            pe.wait_ge(s_vvc, 4)
            with pe.Fori(0, BATCH) as b:
                rhs = ynT[:, bass.ds(b * SEQ, SEQ)]
                for k in range(2):
                    mm = t.matmul(ps[:, k, :], c_w[:, k, :], rhs, start=True, stop=True)
                mm.then_inc(s_lq, 1)
                for f in range(FB):
                    mm = t.matmul(ps[:, 2 + f, :], wfcT[:, f * P:(f + 1) * P], rhs, start=True, stop=True)
                    if f % 2:
                        mm.then_inc(s_fh, 1)
                pe.wait_ge(s_lqc, b + 1)
                pe.wait_ge(s_fr, b * 2 + 2)
                pe.wait_ge(s_loa, b * 4 + 4)
                for q in range(QT):
                    t.matmul(score_c(q), qkC[:, 0, q * P:(q + 1) * P], qkC[:, 1, 0:P * (q + 1)], start=True,
                             stop=True).then_inc(s_ls, 1)
                pe.wait_ge(s_fs, b * 2 + 2)
                pe.wait_ge(s_yc, b + 1)
                for q in range(QT):
                    for f in range(FB):
                        mm = t.matmul(ps[:, 6, q * P:(q + 1) * P], fr[:, f, q * P:(q + 1) * P], wpjT[:, f, :],
                                      start=(f == 0), stop=(f == FB - 1))
                mm.then_inc(s_fy, 1)
                n = 0
                for q in range(QT):
                    pe.wait_ge(s_le, b * 4 + (q + 1))
                    for k in range(q + 1):
                        mm = t.transpose(ps[:, 2 + n // 4, (n % 4) * P:(n % 4 + 1) * P], pC[:, q, k * P:(k + 1) * P], ident)
                        n += 1
                mm.then_inc(s_lt, 1)
                pe.wait_ge(s_ltc, b * 2 + 2)
                n = 0
                for q in range(QT):
                    for k in range(q + 1):
                        mm = t.matmul(ps[:, 7, q * P:(q + 1) * P], pT[:, n, :],
                                      vC[:, bass.ds(b * QT + k, 1), :].rearrange("p n d -> p (n d)"), start=(k == 0), stop=(k == q))
                        n += 1
                mm.then_inc(s_lo, 1)

        @block.vector
        def _(dve):
            v = nc.vector
            chain = [0]

            def link(ins):
                chain[0] += 1
                ins.then_inc(s_chain, 1)
                dve.wait_ge(s_chain, chain[0])

            def statistics(src, tiles):
                for k in tiles:
                    v.bn_stats(stat[:, k, :], src[:, k, :]).then_inc(s_stat, 1)

            def layer_norm(n, src, dst, tiles=range(NT)):
                statistics(src, tiles)
                dve.wait_ge(s_stat, NT * (n + 1))
                mean, dif, var = small[:, MEAN:MEAN + NT], small[:, DIF:DIF + NT], small[:, VAR:VAR + NT]
                v.tensor_tensor(mean, stat[:, :, 1], stat[:, :, 4], ALU.add).then_inc(s_chain, 1)
                v.tensor_tensor(dif, stat[:, :, 1], stat[:, :, 4], ALU.subtract).then_inc(s_chain, 1)
                chain[0] += 2
                link(v.tensor_tensor(var, stat[:, :, 2], stat[:, :, 5], ALU.add))
                link(v.scalar_tensor_tensor(dif, dif, 0.25, dif, ALU.mult, ALU.mult))
                v.scalar_tensor_tensor(var, var, 1.0 / D, dif, ALU.mult, ALU.add).then_inc(s_var, 1)
                link(v.tensor_scalar(mean, mean, 0.5, None, ALU.mult))
                dve.wait_ge(s_std, n + 1)
                link(v.reciprocal(small[:, RSTD:RSTD + NT], small[:, STD:STD + NT]))
                for k in range(NT):
                    v.tensor_scalar(dst[:, k, :], src[:, k, :], small[:, MEAN + k:MEAN + k + 1],
                                    small[:, RSTD + k:RSTD + k + 1], ALU.subtract, ALU.mult).then_inc(s_nrm, 1)

            dve.wait_ge(s_x, 16 * BATCH)
            layer_norm(0, acc1, acc2)
            dve.wait_ge(s_nrm, NT)
            layer_norm(1, acc2, un)
            dve.wait_ge(s_xtc, BATCH)
            v.tensor_scalar(ctxb, small[:, CTX:CTX + BATCH].unsqueeze(2).broadcast_to([P, BATCH, P]), 1.0 / SEQ, None,
                            ALU.mult).then_inc(s_ctx, 1)
            dve.wait_ge(s_col, 16 * N_COLS)
            link(v.tensor_scalar(cacc, xnT, cols[:, 1:2], None, ALU.mult))
            link(v.scalar_tensor_tensor(cacc[:, :, 1:SEQ], xnT[:, :, 0:SEQ - 1], cols[:, 0:1], cacc[:, :, 1:SEQ],
                                        ALU.mult, ALU.add))
            link(v.scalar_tensor_tensor(cacc[:, :, 0:SEQ - 1], xnT[:, :, 1:SEQ], cols[:, 2:3], cacc[:, :, 0:SEQ - 1],
                                        ALU.mult, ALU.add))
            dve.wait_ge(s_dyn, 1)
            dyn = small[:, DYN:DYN + 12].rearrange("p (b k) -> p b k", k=3)
            v.tensor_tensor(dyn, ps[:, 4, 0:12].rearrange("p (b k) -> p b k", k=3),
                            kgb[:].unsqueeze(1).broadcast_to([P, BATCH, 3]), ALU.add).then_inc(s_z, 1)
            dve.wait_ge(s_ez, 1)
            link(v.tensor_scalar(dyn, dyn, 1.0, None, ALU.add))
            link(v.reciprocal(dyn, dyn))
            link(v.tensor_reduce(small[:, GATE:GATE + BATCH], dyn, AX_X, ALU.add))
            link(v.tensor_scalar(small[:, GATE:GATE + BATCH], small[:, GATE:GATE + BATCH], 1.0 / 3.0, None, ALU.mult))
            for b in range(BATCH):
                v.tensor_scalar(hT[:, b * SEQ:(b + 1) * SEQ], cacc[:, b, :], cols[:, 3:4],
                                small[:, GATE + b:GATE + b + 1], ALU.add, ALU.mult).then_inc(s_h, 1)
            v.sem_inc(s_acc, 1)
            v.sem_inc(s_acc, 1)

            def tile(ring, use):
                r = ring.slot(use)
                return ps[:, 2 * r:2 * r + 2, :]

            def steps(which, it, ring):
                for use in which:
                    kind = use[0]
                    if kind in FILLS:
                        t = tile(ring, use)
                    if kind in ("PB", "PA", "BC", "yA", "yB"):
                        dve.wait_ge(ring_full, ring.filled(use))
                    if kind == "PB":
                        _, j, h = use
                        v.tensor_reduce(maxB[:, 2 * h:2 * h + 2, 32 * j:32 * j + 1], t, AX_X, ALU.max).then_inc(s_maxB, 1)
                    elif kind == "PA":
                        _, j, h = use
                        v.tensor_reduce(maxA[:, 2 * h:2 * h + 2, j, 64:64 + NCH],
                                        t.rearrange("p q (c k) -> p q c k", c=NCH), AX_X, ALU.max).then_inc(s_maxA, 1)
                    elif kind == "BC":
                        _, j, h = use
                        e = eA[:, j, 2 * h:2 * h + 2, :]
                        v.tensor_tensor(e, e, t, ALU.mult).then_inc(s_wts, 1)
                    elif kind == "cw":
                        dve.wait_ge(s_r, it + 1)
                        v.tensor_tensor(cw[:], ps[:, 6, :], cr[:], ALU.mult).then_inc(s_sw, 1)
                    elif kind == "QBs":
                        dve.wait_ge(s_mtB, it + 1)
                        v.tensor_tensor(QB[:], QB[:].bitcast(F32), ps[:, 7, :], ALU.add).then_inc(s_QBs, 1)
                    elif kind == "qA":
                        p = use[1]
                        for q in range(2):
                            dve.wait_ge(s_QS, it * 4 + (2 * p + q + 5))
                            v.tensor_tensor(QA[64:128, 2 * p + q, :], t[64 * q:64 * q + 64, 0, :],
                                            QS[0:64, 2 * p + q, :].bitcast(F32), ALU.subtract).then_inc(s_QA, 1)
                    elif kind == "kA":
                        dve.wait_ge(s_pset, N_PSET)
                        dve.wait_ge(s_KAh, it + 2)
                        v.tensor_tensor(KS[0:64, :], t[0:64, 0, :], KAh[0:64, :].bitcast(F32), ALU.subtract).then_inc(s_KS, 1)
                    elif kind == "cf":
                        dve.wait_ge(s_rt, it + 1)
                        dve.wait_ge(s_c1, it + 1)
                        v.tensor_tensor(cf[:], cr[:], ct[:], ALU.mult).then_inc(s_cf, 1)
                    elif kind == "cfl":
                        dve.wait_ge(s_cfh, it + 1)
                        v.scalar_tensor_tensor(cfl[:], cfh[:].bitcast(F32), col(3), cf[:], ALU.mult, ALU.add).then_inc(s_cfl, 1)
                    elif kind == "qkB":
                        dve.wait_ge(s_HB, it + 2)
                        v.scalar_tensor_tensor(KB[:], HB[:, 1, :].bitcast(F32), col(2), t[:, 1, :], ALU.mult,
                                               ALU.add).then_inc(s_KB, 1)
                        v.scalar_tensor_tensor(QB[:], HB[:, 0, :].bitcast(F32), col(1), t[:, 0, :], ALU.mult,
                                               ALU.add).then_inc(s_QB, 1)
                    elif kind == "sB":
                        dve.wait_ge(s_rB, it + 2)
                        v.tensor_tensor(oB[:], oB[:], rB[:], ALU.mult).then_inc(s_yB, 1)
                    elif kind in ("yA", "yB"):
                        acc = acc1 if kind == "yA" else acc2
                        a = acc[:, bass.ds((it // GROUPS) * QT, QT), :]
                        dve.wait_ge(s_acc, it * 2 + (2 if kind == "yA" else 1))
                        v.tensor_tensor(a, a, t[:, 0, :].rearrange("p (q d) -> p q d", q=QT), ALU.add).then_inc(s_acc, 1)

            steps(PRO_STEPS, -1, Ring("prologue", 0))
            with dve.Fori(0, ITERS - 1) as it:
                steps(STEPS, it, Ring("body", it))
            steps(EPI_STEPS[:-1], ITERS - 1, Ring("epilogue", ITERS - 1))

            dve.wait_ge(s_acc, 2 * ITERS + 1)
            layer_norm(2, acc2, zn)
            steps(EPI_STEPS[-1:], ITERS - 1, Ring("epilogue", ITERS - 1))
            dve.wait_ge(s_gl, 1)
            link(v.tensor_tensor(lg[:], ps[:, 4, 0:NT * EXPERTS].rearrange("p (n e) -> p n e", n=NT),
                                 gb[:].unsqueeze(1).broadcast_to([P, NT, EXPERTS]), ALU.add))
            link(v.tensor_reduce(small[:, 0:NT], lg[:], AX_X, ALU.max))
            per_expert = small[:, 0:NT].unsqueeze(2).broadcast_to([P, NT, EXPERTS])
            link(v.tensor_tensor(lge[:], lg[:], per_expert, ALU.is_equal))
            link(v.tensor_tensor(lge[:], lge[:], cst[:, C_COL + 12:C_COL + 12 + EXPERTS].unsqueeze(1)
                                 .broadcast_to([P, NT, EXPERTS]), ALU.mult))
            link(v.tensor_reduce(small[:, 0:NT], lge[:], AX_X, ALU.max))
            v.tensor_tensor(hot[:].rearrange("p e n -> p n e"), lge[:], per_expert, ALU.is_equal).then_inc(s_hot, 1)
            v.tensor_tensor(hot_bf[:].rearrange("p e n -> p n e"), lge[:], per_expert, ALU.is_equal).then_inc(s_hot, 1)
            dve.wait_ge(s_hot, 2)
            dve.wait_ge(s_rk, 1)
            e8 = lambda a: a[:, 0:EXPERTS]
            cmp_et = cmp[:, 0:P].rearrange("p (e t) -> p e t", e=EXPERTS)
            cmp_ee = cmp[:, P:P + 64].rearrange("p (e f) -> p e f", e=EXPERTS)
            cmp_se = cmp[:, 192:192 + 8 * SLOT_TILES].rearrange("p (s e) -> p s e", e=EXPERTS)
            link(v.tensor_reduce(e8(tot), ps[:, 6, 0:P].rearrange("p (e n) -> p e n", e=EXPERTS), AX_X, ALU.add))
            link(v.tensor_tensor(cmp_et, e8(tot).unsqueeze(2).broadcast_to([P, EXPERTS, NT]),
                                 cst[:, C_THR:C_THR + NT].unsqueeze(1).broadcast_to([P, EXPERTS, NT]), ALU.is_gt))
            link(v.tensor_reduce(e8(tiles), cmp_et, AX_X, ALU.add))
            link(v.tensor_tensor(cmp_ee, e8(tiles).unsqueeze(1).broadcast_to([P, EXPERTS, EXPERTS]),
                                 cst[:, C_TRI:C_TRI + 64].rearrange("p (e f) -> p e f", e=EXPERTS), ALU.mult))
            link(v.tensor_reduce(e8(upto), cmp_ee, AX_X, ALU.add))
            link(v.tensor_tensor(e8(first), e8(upto), e8(tiles), ALU.subtract))
            link(v.scalar_tensor_tensor(cmp_et, e8(first).unsqueeze(2).broadcast_to([P, EXPERTS, NT]), float(P),
                                        ps[:, 5, 0:P].rearrange("p (e n) -> p e n", e=EXPERTS), ALU.mult, ALU.add))
            link(v.tensor_tensor(cmp_et, cmp_et, hot[:], ALU.mult))
            link(v.tensor_reduce(slot_f, cmp[:, 0:P].rearrange("p (e n) -> p n e", e=EXPERTS), AX_X, ALU.add))
            v.tensor_copy(slot[:], slot_f).then_inc(s_slot, 1)
            link(v.tensor_tensor(cmp_se, e8(upto).unsqueeze(1).broadcast_to([P, SLOT_TILES, EXPERTS]),
                                 cst[:, C_SLOT:C_SLOT + SLOT_TILES].unsqueeze(2).broadcast_to([P, SLOT_TILES, EXPERTS]), ALU.is_le))
            link(v.tensor_reduce(cmp[:, 448:448 + SLOT_TILES], cmp_se, AX_X, ALU.add))
            v.tensor_scalar(expert_of[:], cmp[:, 448:448 + SLOT_TILES], float(EXPERTS - 1), None, ALU.min).then_inc(s_es, 1)
            for _ in range(2):
                v.sem_inc(s_hc, 1)
                v.sem_inc(s_yo, 1)
            dve.wait_ge(s_sc, 16 * NT)
            with dve.Fori(0, SLOT_TILES // 4) as i:
                def hidden_copy(u):
                    dve.wait_ge(s_ht, i * 4 + (u + 1))
                    v.tensor_copy(heT[u % 2][:], ps[:, 4 + u % 2, :]).then_inc(s_hc, 1)

                def output_copy(u):
                    dve.wait_ge(s_yf, i * 4 + (u + 1))
                    v.tensor_scalar(yo[:, bass.ds(i * 4 + u, 1), :].rearrange("p s d -> p (s d)"), ps[:, 6 + u % 2, 0:P], 1.0,
                                    None, ALU.mult).then_inc(s_yo, 1)

                hidden_copy(0)
                for u in range(1, 4):
                    hidden_copy(u)
                    output_copy(u - 1)
                output_copy(3)
            dve.wait_ge(s_sum, 1)
            for b in range(BATCH):
                dve.wait_ge(s_ga[b], 16 * QT)
                a = acc1[:, b * QT:(b + 1) * QT, :]
                v.tensor_tensor(a, a, yg[:, b * QT:(b + 1) * QT, :], ALU.add).then_inc(s_ya, 1)
                dve.wait_ge(s_ya, b + 1)
                statistics(acc1, range(b * QT, (b + 1) * QT))

            layer_norm(3, acc1, yn, ())
            for _ in range(4):
                v.sem_inc(s_loa, 1)
            for _ in range(14):
                v.sem_inc(s_sp, 1)
            for _ in range(5):
                v.sem_inc(s_cnt, 1)
            v.sem_inc(s_yc, 1)
            LX, LL = 0, 4
            with dve.Fori(0, BATCH) as b:
                for q in range(QT):
                    dve.wait_ge(s_ls, b * 4 + (q + 1))
                    sc = score_c(q)
                    dg = sc[:, q * P:(q + 1) * P]
                    v.tensor_tensor(dg, dg, cst[:, C_CAUSAL:C_CAUSAL + P], ALU.add).then_inc(s_lm, 1)
                    dve.wait_ge(s_lm, b * 8 + (2 * q + 1))
                    v.tensor_reduce(small[:, 8 + q:9 + q], sc, AX_X, ALU.max).then_inc(s_lm, 1)
                    dve.wait_ge(s_lm, b * 8 + (2 * q + 2))
                    v.tensor_scalar(small[:, LX + q:LX + q + 1], small[:, 8 + q:9 + q], -SCALE_C, None, ALU.mult).then_inc(s_lx, 1)
                dve.wait_ge(s_yc, b + 2)
                dve.wait_ge(s_cnt, b * 5 + 5)
                v.tensor_scalar(neg, ysp, -1.0, None, ALU.mult).then_inc(s_sp, 1)
                dve.wait_ge(s_sp, b * 14 + 15)
                v.tensor_scalar(spk[0], neg, -1.0, None, ALU.is_lt).then_inc(s_sp, 1)
                for n in range(1, 5):
                    v.scalar_tensor_tensor(tmp, neg, 0.9, ysp, ALU.mult, ALU.subtract).then_inc(s_sp, 1)
                    dve.wait_ge(s_sp, b * 14 + (3 * n + 14))
                    v.tensor_tensor(neg, tmp, spk[n - 1], ALU.add).then_inc(s_sp, 1)
                    dve.wait_ge(s_sp, b * 14 + (3 * n + 15))
                    v.tensor_scalar(spk[n], neg, -1.0, None, ALU.is_lt).then_inc(s_sp, 1)
                dve.wait_ge(s_le, b * 4 + 4)
                v.reciprocal(small[:, 12:16], small[:, LL:LL + 4]).then_inc(s_lr, 1)
                dve.wait_ge(s_lr, b + 1)
                dve.wait_ge(s_lo, b + 1)
                for q in range(QT):
                    a = acc1[:, bass.ds(b * QT + q, 1), :].rearrange("p n d -> p (n d)")
                    v.scalar_tensor_tensor(a, ps[:, 7, q * P:(q + 1) * P], small[:, 12 + q:13 + q], a, ALU.mult,
                                           ALU.add).then_inc(s_loa, 1)


_INS = ['L0_attn_hidden_states', 'L0_attn_w_q', 'L0_attn_w_k', 'L0_attn_w_v', 'L0_attn_w_o', 'L0_attn_w_kgen',
        'L0_attn_b_kgen', 'L0_attn_w_conv', 'L0_attn_b_conv', 'L0_ffn_ln1_w', 'L0_ffn_ln1_b', 'L0_ffn_w_qkv',
        'L0_ffn_w_proj', 'L0_ffn_ln2_w', 'L0_ffn_ln2_b', 'L0_ffn_gate_w', 'L0_ffn_gate_b', 'L0_ffn_w1', 'L0_ffn_w2',
        'L1_attn_WQ', 'L1_attn_WK', 'L1_attn_WV', 'L1_ffn_W_fc', 'L1_ffn_W_proj']
_OUTS = [((4, 512, 128), 'float32')]


def kernel(**inputs):
    import numpy as _np
    import concourse.bacc as _bacc
    from concourse import mybir as _mybir
    from concourse.bass_utils import run_bass_kernel_spmd as _run

    nc = _bacc.Bacc("TRN2", target_bir_lowering=False, num_devices=1)
    arrays, args = {}, []
    named = [(name, _np.ascontiguousarray(inputs[name])) for name in _INS] + [("constants", constant_columns())]
    for name, a in named:
        arrays[f"in_{name}_dram"] = a
        args.append(nc.dram_tensor(f"in_{name}_dram", a.shape, _mybir.dt.from_np(a.dtype), kind="ExternalInput").ap())
    for name in ("by_expert", "expert_out"):
        args.append(nc.dram_tensor(name, (SLOT_TILES * P, D), _mybir.dt.float32, kind="Internal").ap())
    for i, (shape, dtype) in enumerate(_OUTS):
        dt = _mybir.dt.from_np(_np.dtype(dtype))
        args.append(nc.dram_tensor(f"out_{i}_dram", shape, dt, kind="ExternalOutput").ap())
    build(nc, *args)
    r = _run(nc, [arrays], core_ids=[0])
    return r.results[0]["out_0_dram"]
```
